# Optimizing a Trainium2 kernel written in Bass

```python
import numpy as np
import jax
import jax.numpy as jnp

def _softmax(x, axis=-1):
    return jax.nn.softmax(x, axis=axis)

def _gelu(x):
    return jax.nn.gelu(x, approximate=True)

def _silu(x):
    return jax.nn.silu(x)

def _sigmoid(x):
    return jax.nn.sigmoid(x)

def _layernorm(x, axis=-1, eps=1e-05):
    m = jnp.mean(x, axis=axis, keepdims=True)
    v = jnp.var(x, axis=axis, keepdims=True)
    return (x - m) / jnp.sqrt(v + eps)

def _scatter_add(tgt, idx, src, axis=0):
    return tgt.at[idx].add(src)

def _segment_sum(src, seg, n):
    return jax.ops.segment_sum(src, seg, n)
kernel_name = 'mk_gnn_ffn_d2_gnn_r32_f03c8c'

def setup_inputs(seed: int=0):
    np.random.seed(seed)
    _w = jnp.asarray

    def _rec_inputs():
        import jax
        import jax.numpy as jnp
        _gk = jax.random.key(seed)
        x = -5.39e-05 + 0.9998 * jax.random.normal(jax.random.fold_in(_gk, 1), (3125, 256), jnp.float32)
        src = jax.random.randint(jax.random.fold_in(_gk, 2), (50000,), 0, 3125, jnp.int32)
        dst = jnp.minimum((3125 * jax.random.uniform(jax.random.fold_in(_gk, 3), (50000,)) ** 2.0).astype(jnp.int32), 99999)
        _o = jnp.argsort(dst, stable=True)
        src = src[_o]
        dst = dst[_o]
        return (x, src, dst)
    x, src, dst = _rec_inputs()

    def _L0_gnn_setup():
        import jax, jax.numpy as jnp
        import numpy as np
        NUM_NODES = 3125
        IN_CH = 256
        HIDDEN = 128
        OUT_CH = 256
        NUM_EDGES = 100000

        def gcn_conv(x, W, b, src, dst, num_nodes):
            h = x @ W
            loop = jnp.arange(num_nodes, dtype=src.dtype)
            s = jnp.concatenate([src, loop])
            d = jnp.concatenate([dst, loop])
            deg = jax.ops.segment_sum(jnp.ones_like(d, dtype=h.dtype), d, num_segments=num_nodes)
            dinv = jnp.where(deg > 0, jax.lax.rsqrt(deg), 0.0)
            norm = dinv[s] * dinv[d]
            msg = h[s] * norm[:, None]
            out = jax.ops.segment_sum(msg, d, num_segments=num_nodes)
            return out + b
        key = jax.random.key(seed)
        k1, k2, k3, k4 = jax.random.split(key, 4)
        edge_index = jax.random.randint(k1, (2, NUM_EDGES), 0, NUM_NODES, dtype=jnp.int64)
        node_features = jax.random.normal(k2, (NUM_NODES, IN_CH), dtype=jnp.float32)
        W1 = jax.random.normal(k3, (IN_CH, HIDDEN), dtype=jnp.float32) * (1.0 / np.sqrt(IN_CH))
        b1 = jnp.zeros((HIDDEN,), dtype=jnp.float32)
        W2 = jax.random.normal(k4, (HIDDEN, OUT_CH), dtype=jnp.float32) * (1.0 / np.sqrt(HIDDEN))
        b2 = jnp.zeros((OUT_CH,), dtype=jnp.float32)
        return {'node_features': node_features, 'W1': W1, 'b1': b1, 'W2': W2, 'b2': b2, 'edge_index': edge_index}
    _L0_gnn_all = _L0_gnn_setup()
    _L0_gnn_in = {k: v for k, v in _L0_gnn_all.items() if k in ('W1', 'b1', 'W2', 'b2')}
    del _L0_gnn_all

    def _L0_ffn_setup():
        import jax, jax.numpy as jnp
        import numpy as np
        D_MODEL = 256
        EXPERT_DIM = 512
        NUM_EXPERTS = 8
        TOP_K = 2
        SEQ_LEN = 64
        BATCH = 2
        key = jax.random.key(seed)
        ks = jax.random.split(key, 8)
        s = 0.02
        x = jax.random.normal(ks[0], (SEQ_LEN, BATCH, D_MODEL), dtype=jnp.float32)
        Wg = jax.random.normal(ks[1], (D_MODEL, NUM_EXPERTS), dtype=jnp.float32) * s
        bg = jax.random.normal(ks[2], (NUM_EXPERTS,), dtype=jnp.float32) * s
        bias = jnp.zeros((NUM_EXPERTS,), dtype=jnp.float32)
        W1 = jax.random.normal(ks[3], (NUM_EXPERTS, D_MODEL, EXPERT_DIM), dtype=jnp.float32) * s
        b1 = jax.random.normal(ks[4], (NUM_EXPERTS, EXPERT_DIM), dtype=jnp.float32) * s
        W2 = jax.random.normal(ks[5], (NUM_EXPERTS, EXPERT_DIM, D_MODEL), dtype=jnp.float32) * s
        b2 = jax.random.normal(ks[6], (NUM_EXPERTS, D_MODEL), dtype=jnp.float32) * s
        return {'x': x, 'Wg': Wg, 'bg': bg, 'bias': bias, 'W1': W1, 'b1': b1, 'W2': W2, 'b2': b2}
    _L0_ffn_all = _L0_ffn_setup()
    _L0_ffn_in = {k: v for k, v in _L0_ffn_all.items() if k in ('Wg', 'bg', 'bias', 'W1', 'b1', 'W2', 'b2')}
    del _L0_ffn_all

    def _L1_gnn_setup():
        import jax, jax.numpy as jnp
        import numpy as np
        N, HID, HEADS = (50000, 256, 8)
        D = HID // HEADS
        E = 25000

        def _gnn_layer(x, edge_index, Wq, bq, Wk, bk, Wv, bv, Wskip, bskip, gamma, beta):
            n = x.shape[0]
            src, dst = (edge_index[0], edge_index[1])
            q = (x @ Wq + bq).reshape(n, HEADS, D)
            k = (x @ Wk + bk).reshape(n, HEADS, D)
            v = (x @ Wv + bv).reshape(n, HEADS, D)
            logits = jnp.einsum('ehd,ehd->eh', q[dst], k[src]) / jnp.sqrt(jnp.float32(D))
            seg_max = jax.ops.segment_max(logits, dst, num_segments=n)
            expv = jnp.exp(logits - seg_max[dst])
            denom = jax.ops.segment_sum(expv, dst, num_segments=n)
            attn = expv / denom[dst]
            agg = jax.ops.segment_sum(attn[:, :, None] * v[src], dst, num_segments=n)
            out = agg.reshape(n, HID) + (x @ Wskip + bskip)
            h = jax.nn.gelu(out, approximate=False)
            y = x + h
            mu = jnp.mean(y, axis=-1, keepdims=True)
            var = jnp.var(y, axis=-1, keepdims=True)
            return (y - mu) / jnp.sqrt(var + 1e-05) * gamma + beta
        key = jax.random.key(seed)
        ks = jax.random.split(key, 12)
        s = 0.02
        x = jax.random.normal(ks[0], (N, HID), dtype=jnp.float32)
        edge_index = jax.random.randint(ks[1], (2, E), 0, N, dtype=jnp.int64)
        Wq = jax.random.normal(ks[2], (HID, HID), dtype=jnp.float32) * s
        bq = jnp.zeros((HID,), dtype=jnp.float32)
        Wk = jax.random.normal(ks[3], (HID, HID), dtype=jnp.float32) * s
        bk = jnp.zeros((HID,), dtype=jnp.float32)
        Wv = jax.random.normal(ks[4], (HID, HID), dtype=jnp.float32) * s
        bv = jnp.zeros((HID,), dtype=jnp.float32)
        Wskip = jax.random.normal(ks[5], (HID, HID), dtype=jnp.float32) * s
        bskip = jnp.zeros((HID,), dtype=jnp.float32)
        gamma = jnp.ones((HID,), dtype=jnp.float32)
        beta = jnp.zeros((HID,), dtype=jnp.float32)
        return {'x': x, 'edge_index': edge_index, 'Wq': Wq, 'bq': bq, 'Wk': Wk, 'bk': bk, 'Wv': Wv, 'bv': bv, 'Wskip': Wskip, 'bskip': bskip, 'gamma': gamma, 'beta': beta}
    _L1_gnn_all = _L1_gnn_setup()
    _L1_gnn_in = {k: v for k, v in _L1_gnn_all.items() if k in ('Wq', 'bq', 'Wk', 'bk', 'Wv', 'bv', 'Wskip', 'bskip', 'gamma', 'beta')}
    del _L1_gnn_all

    def _L1_ffn_setup():
        import jax, jax.numpy as jnp
        import numpy as np
        B, S, D = (8, 128, 256)
        H = 4 * D
        CAPACITY = 0.5
        key = jax.random.key(seed)
        ks = jax.random.split(key, 6)
        x = jax.random.normal(ks[0], (B, S, D), dtype=jnp.float32)
        attention_mask = jnp.zeros((B, 1, 1, S), dtype=jnp.float32)
        wr = jax.random.normal(ks[1], (D, 1), dtype=jnp.float32) * 0.02
        br = jnp.zeros((1,), dtype=jnp.float32)
        w1 = jax.random.normal(ks[2], (D, H), dtype=jnp.float32) * 0.02
        b1 = jnp.zeros((H,), dtype=jnp.float32)
        w2 = jax.random.normal(ks[3], (H, D), dtype=jnp.float32) * 0.02
        b2 = jnp.zeros((D,), dtype=jnp.float32)
        return {'x': x, 'attention_mask': attention_mask, 'wr': wr, 'br': br, 'w1': w1, 'b1': b1, 'w2': w2, 'b2': b2}
    _L1_ffn_all = _L1_ffn_setup()
    _L1_ffn_in = {k: v for k, v in _L1_ffn_all.items() if k in ('attention_mask', 'wr', 'br', 'w1', 'b1', 'w2', 'b2')}
    del _L1_ffn_all
    return {'x': x, 'src': src, 'dst': dst, 'L0_gnn_W1': _L0_gnn_in['W1'], 'L0_gnn_b1': _L0_gnn_in['b1'], 'L0_gnn_W2': _L0_gnn_in['W2'], 'L0_gnn_b2': _L0_gnn_in['b2'], 'L0_ffn_Wg': _L0_ffn_in['Wg'], 'L0_ffn_bg': _L0_ffn_in['bg'], 'L0_ffn_bias': _L0_ffn_in['bias'], 'L0_ffn_W1': _L0_ffn_in['W1'], 'L0_ffn_b1': _L0_ffn_in['b1'], 'L0_ffn_W2': _L0_ffn_in['W2'], 'L0_ffn_b2': _L0_ffn_in['b2'], 'L1_gnn_Wq': _L1_gnn_in['Wq'], 'L1_gnn_bq': _L1_gnn_in['bq'], 'L1_gnn_Wk': _L1_gnn_in['Wk'], 'L1_gnn_bk': _L1_gnn_in['bk'], 'L1_gnn_Wv': _L1_gnn_in['Wv'], 'L1_gnn_bv': _L1_gnn_in['bv'], 'L1_gnn_Wskip': _L1_gnn_in['Wskip'], 'L1_gnn_bskip': _L1_gnn_in['bskip'], 'L1_gnn_gamma': _L1_gnn_in['gamma'], 'L1_gnn_beta': _L1_gnn_in['beta'], 'L1_ffn_attention_mask': _L1_ffn_in['attention_mask'], 'L1_ffn_wr': _L1_ffn_in['wr'], 'L1_ffn_br': _L1_ffn_in['br'], 'L1_ffn_w1': _L1_ffn_in['w1'], 'L1_ffn_b1': _L1_ffn_in['b1'], 'L1_ffn_w2': _L1_ffn_in['w2'], 'L1_ffn_b2': _L1_ffn_in['b2']}

def reference(x, src, dst, L0_gnn_W1, L0_gnn_b1, L0_gnn_W2, L0_gnn_b2, L0_ffn_Wg, L0_ffn_bg, L0_ffn_bias, L0_ffn_W1, L0_ffn_b1, L0_ffn_W2, L0_ffn_b2, L1_gnn_Wq, L1_gnn_bq, L1_gnn_Wk, L1_gnn_bk, L1_gnn_Wv, L1_gnn_bv, L1_gnn_Wskip, L1_gnn_bskip, L1_gnn_gamma, L1_gnn_beta, L1_ffn_attention_mask, L1_ffn_wr, L1_ffn_br, L1_ffn_w1, L1_ffn_b1, L1_ffn_w2, L1_ffn_b2):
    import jax
    import jax.numpy as jnp

    def _L0_gnn_ref(node_features, W1, b1, W2, b2, edge_index):
        import jax, jax.numpy as jnp
        import numpy as np
        NUM_NODES = 3125
        IN_CH = 256
        HIDDEN = 128
        OUT_CH = 256
        NUM_EDGES = 100000

        def gcn_conv(x, W, b, src, dst, num_nodes):
            h = x @ W
            loop = jnp.arange(num_nodes, dtype=src.dtype)
            s = jnp.concatenate([src, loop])
            d = jnp.concatenate([dst, loop])
            deg = jax.ops.segment_sum(jnp.ones_like(d, dtype=h.dtype), d, num_segments=num_nodes)
            dinv = jnp.where(deg > 0, jax.lax.rsqrt(deg), 0.0)
            norm = dinv[s] * dinv[d]
            msg = h[s] * norm[:, None]
            out = jax.ops.segment_sum(msg, d, num_segments=num_nodes)
            return out + b
        src, dst = (edge_index[0], edge_index[1])
        x = gcn_conv(node_features, W1, b1, src, dst, NUM_NODES)
        x = jax.nn.relu(x)
        x = gcn_conv(x, W2, b2, src, dst, NUM_NODES)
        return x

    def _L0_ffn_ref(x, Wg, bg, bias, W1, b1, W2, b2):
        import jax, jax.numpy as jnp
        import numpy as np
        D_MODEL = 256
        EXPERT_DIM = 512
        NUM_EXPERTS = 8
        TOP_K = 2
        SEQ_LEN = 64
        BATCH = 2
        x_flat = x.reshape(-1, D_MODEL)
        gate_logits = x_flat @ Wg + bg + bias
        topk_vals, topk_idx = jax.lax.top_k(gate_logits, TOP_K)
        topk_w = jax.nn.softmax(topk_vals, axis=-1)
        combine = (jax.nn.one_hot(topk_idx, NUM_EXPERTS, dtype=x.dtype) * topk_w[..., None]).sum(axis=1)
        h = jax.nn.relu(jnp.einsum('td,edh->teh', x_flat, W1) + b1)
        y = jnp.einsum('teh,ehd->ted', h, W2) + b2
        out = jnp.einsum('ted,te->td', y, combine)
        return out.reshape(x.shape)

    def _L1_gnn_ref(x, edge_index, Wq, bq, Wk, bk, Wv, bv, Wskip, bskip, gamma, beta):
        import jax, jax.numpy as jnp
        import numpy as np
        N, HID, HEADS = (50000, 256, 8)
        D = HID // HEADS
        E = 25000

        def _gnn_layer(x, edge_index, Wq, bq, Wk, bk, Wv, bv, Wskip, bskip, gamma, beta):
            n = x.shape[0]
            src, dst = (edge_index[0], edge_index[1])
            q = (x @ Wq + bq).reshape(n, HEADS, D)
            k = (x @ Wk + bk).reshape(n, HEADS, D)
            v = (x @ Wv + bv).reshape(n, HEADS, D)
            logits = jnp.einsum('ehd,ehd->eh', q[dst], k[src]) / jnp.sqrt(jnp.float32(D))
            seg_max = jax.ops.segment_max(logits, dst, num_segments=n)
            expv = jnp.exp(logits - seg_max[dst])
            denom = jax.ops.segment_sum(expv, dst, num_segments=n)
            attn = expv / denom[dst]
            agg = jax.ops.segment_sum(attn[:, :, None] * v[src], dst, num_segments=n)
            out = agg.reshape(n, HID) + (x @ Wskip + bskip)
            h = jax.nn.gelu(out, approximate=False)
            y = x + h
            mu = jnp.mean(y, axis=-1, keepdims=True)
            var = jnp.var(y, axis=-1, keepdims=True)
            return (y - mu) / jnp.sqrt(var + 1e-05) * gamma + beta
        return _gnn_layer(x, edge_index, Wq, bq, Wk, bk, Wv, bv, Wskip, bskip, gamma, beta)

    def _L1_ffn_ref(x, attention_mask, wr, br, w1, b1, w2, b2):
        import jax, jax.numpy as jnp
        import numpy as np
        B, S, D = (8, 128, 256)
        H = 4 * D
        CAPACITY = 0.5
        b, s, d = x.shape
        weights = (jnp.einsum('bsd,do->bso', x, wr) + br)[..., 0]
        k = max(1, int(CAPACITY * s))
        kk = k - 1 if k > 1 else 1
        _, idx = jax.lax.top_k(weights, k)
        sel_idx = idx[:, :kk]
        sel = jnp.take_along_axis(x, sel_idx[:, :, None], axis=1)
        h = jax.nn.gelu(jnp.einsum('bkd,dh->bkh', sel, w1) + b1)
        y = jnp.einsum('bkh,hd->bkd', h, w2) + b2
        w_sel = jnp.take_along_axis(weights, sel_idx, axis=1)
        y = y * w_sel[..., None]
        batch_idx = jnp.arange(b)[:, None]
        processed = jnp.zeros_like(x).at[batch_idx, sel_idx].set(y)
        return processed + x
    edge_index = jnp.stack([src, dst])
    x = x + _L0_gnn_ref(_layernorm(x, axis=-1), L0_gnn_W1, L0_gnn_b1, L0_gnn_W2, L0_gnn_b2, edge_index)
    x = x + _L0_ffn_ref(_layernorm(x, axis=-1)[None], L0_ffn_Wg, L0_ffn_bg, L0_ffn_bias, L0_ffn_W1, L0_ffn_b1, L0_ffn_W2, L0_ffn_b2)[0]
    x = x + _L1_gnn_ref(_layernorm(x, axis=-1), edge_index, L1_gnn_Wq, L1_gnn_bq, L1_gnn_Wk, L1_gnn_bk, L1_gnn_Wv, L1_gnn_bv, L1_gnn_Wskip, L1_gnn_bskip, L1_gnn_gamma, L1_gnn_beta)
    x = x + _L1_ffn_ref(_layernorm(x, axis=-1)[None], L1_ffn_attention_mask, L1_ffn_wr, L1_ffn_br, L1_ffn_w1, L1_ffn_b1, L1_ffn_w2, L1_ffn_b2)[0]
    return x

_drawn_inputs = setup_inputs


def setup_inputs(seed=0):
    import zlib

    import numpy as np

    out = dict(_drawn_inputs(seed))
    spreads = {'L0_gnn_b1': (0.0, 0.1),
     'L0_gnn_b2': (0.0, 0.1),
     'L0_ffn_bias': (0.0, 0.1),
     'L1_gnn_bq': (0.0, 0.8),
     'L1_gnn_bk': (0.0, 0.8),
     'L1_gnn_bv': (0.0, 0.281),
     'L1_gnn_bskip': (0.0, 0.292),
     'L1_gnn_gamma': (1.0, 0.2),
     'L1_gnn_beta': (0.0, 0.1),
     'L1_ffn_b1': (0.0, 0.8),
     'L1_ffn_b2': (0.0, 0.8)}
    factors = {'L0_ffn_bg': 3.966,
     'L0_ffn_b1': 8.0,
     'L0_ffn_b2': 4.001,
     'L1_gnn_Wq': 8.0,
     'L1_gnn_Wk': 8.0,
     'L1_ffn_wr': 5.975,
     'L1_ffn_w1': 7.108,
     'L1_ffn_w2': 6.673}
    for name, (base, spread) in spreads.items():
        noise = np.random.default_rng([zlib.crc32(name.encode()), seed]).standard_normal(out[name].shape)
        drawn = base * np.exp(spread * noise) if base else spread * noise
        out[name] = jnp.asarray(drawn.astype(out[name].dtype))
    for name, factor in factors.items():
        out[name] = (out[name] * factor).astype(out[name].dtype)
    return out
```

```python
from contextlib import ExitStack

import concourse.bass as bass
from concourse import mybir

P = 128
F32 = mybir.dt.float32
I32 = mybir.dt.int32
ALU = mybir.AluOpType
ACT = mybir.ActivationFunctionType
AX = mybir.AxisListType
PE_ONLY = (mybir.EngineType.PE,)
DVE_ONLY = (mybir.EngineType.DVE,)

U = 8
HALF = U // 2
BIG = 1.0e30
EPS = 1e-5


class Chain:

    def __init__(self, eng, sem):
        self.eng, self.sem, self.n = eng, sem, 0

    def __call__(self, ins):
        self.n += 1
        ins.then_inc(self.sem, 1)
        self.eng.wait_ge(self.sem, self.n)


def wait_count(eng, sem, value):
    if isinstance(value, int) and value <= 0:
        return
    eng.wait_ge(sem, value)


def gnn_program(nc, a, out):
    N, D = a["x"].shape
    E = a["src"].shape[0]
    HID = a["L0_gnn_W1"].shape[1]
    EXP, _, EH = a["L0_ffn_W1"].shape
    FH = a["L1_ffn_w1"].shape[1]
    HEADS = 8
    HD = D // HEADS
    KC = D // P
    KEEP = max(1, int(0.5 * N)) - 1
    FULL = N // P
    TAIL = N - FULL * P
    BLOCKS = FULL + 1 + (FULL + 1) % 2
    PAIRS = BLOCKS // 2
    NODES = BLOCKS * P
    TILES = -(-E // P)
    ETAIL = E - (TILES - 1) * P
    SLOTS = -(-(TILES + FULL) // 16) * 16
    STEPS = SLOTS // U
    RUNS = 4
    RP = SLOTS // RUNS
    CH = P // HEADS
    CS = SLOTS // CH
    SEQ = CS * P
    FAR = 1 << 14
    AW = D + HEADS
    assert SLOTS % (2 * U) == 0 and RP <= P and KC == 2 and HID == P and FULL < BLOCKS

    with ExitStack() as top:
        x_in = top.enter_context(nc.semaphore("x_in"))
        in_use = []

        def sem(name):
            in_use.append(nc.alloc_semaphore(name=name))
            return in_use[-1]

        def recycle():
            nc.all_engine_barrier()
            nc.clear_and_free_semaphores(in_use)
            nc.all_engine_barrier()
            in_use.clear()

        def keep(name, shape, dt=F32):
            return top.enter_context(nc.sbuf_tensor(name, shape, dt))

        src_d = nc.dram_tensor("src_d", [TILES, P], I32, kind="Internal").ap()
        dst_d = nc.dram_tensor("dst_d", [TILES, P], I32, kind="Internal").ap()
        key_d = nc.dram_tensor("key_d", [SLOTS, P], F32, kind="Internal").ap()
        blk_d = nc.dram_tensor("blk_d", [3, SLOTS], I32, kind="Internal").ap()
        g1_d = nc.dram_tensor("g1_d", [NODES, HID], F32, kind="Internal").ap()
        g2_d = nc.dram_tensor("g2_d", [NODES, HID], F32, kind="Internal").ap()
        k_d = nc.dram_tensor("k_d", [NODES, D], F32, kind="Internal").ap()
        v_d = nc.dram_tensor("v_d", [NODES, D], F32, kind="Internal").ap()
        w_d = nc.dram_tensor("w_d", [BLOCKS, P], F32, kind="Internal").ap()

        ident = keep("ident", [P, P])
        ones = keep("ones", [P, P])
        lane = keep("lane", [P, P])
        X = keep("X", [P, BLOCKS, D])
        Z = keep("Z", [P, BLOCKS, D])
        src_i = keep("src_i", [P, SLOTS], I32)
        dl = keep("dl", [P, SLOTS])
        blk1 = keep("blk1", [1, SLOTS], I32)
        blk2 = keep("blk2", [1, SLOTS], I32)
        blk3 = keep("blk3", [1, SLOTS], I32)
        dinv = keep("dinv", [P, BLOCKS])
        stat = keep("stat", [P, BLOCKS])
        stat2 = keep("stat2", [P, BLOCKS])

        def rows(t, blocks=BLOCKS):
            return t.rearrange("(b p) f -> p b f", p=P)[:, 0:blocks, :]

        def per_node(t):
            return t[:, :].unsqueeze(2).broadcast_to([P, BLOCKS, D])

        with ExitStack() as ph:
            def sb(name, shape, dt=F32):
                return ph.enter_context(nc.sbuf_tensor(name, shape, dt))

            pb = [ph.enter_context(nc.psum_tensor(f"t_ps{i}", [P, 512], F32)) for i in range(3)]
            last_i = sb("last_i", [1, TILES - 1], I32)
            last_b = sb("last_b", [1, TILES - 1], I32)
            last_f = sb("last_f", [1, TILES - 1])
            tile_no = sb("tile_no", [1, TILES - 1])
            slot_no = sb("slot_no", [P, RUNS])
            less = sb("less", [P, TILES - 1])
            t_f = sb("t_f", [P, RUNS])
            t_i = sb("t_i", [P, RUNS], I32)
            b_f = sb("b_f", [P, RUNS])
            b_m = sb("b_m", [P, RUNS])
            b_i = sb("b_i", [P, 3, RUNS], I32)
            pad = sb("pad", [1, 2, P], I32)
            ed = sb("ed", [P, RUNS, P], I32)
            es = sb("es", [P, RUNS, P], I32)
            edf = sb("edf", [P, RUNS, P])
            esf = sb("esf", [P, RUNS, P])
            edl = sb("edl", [P, RUNS, P])
            inside = sb("inside", [P, RUNS, P])
            key = sb("key", [P, RUNS, P])
            last_in, pad_set, edges_out = sem("last_in"), sem("pad_set"), sem("edges_out")
            const_set, id_zero, x_zero = sem("const_set"), sem("id_zero"), sem("x_zero")
            t_chain, last_set, spread, t_set, tiles_in = (
                sem("t_chain"), sem("last_set"), sem("spread"), sem("t_set"), sem("tiles_in"))
            b_set, key_set, tables_out, turned, tables_in, copied = (
                sem("b_set"), sem("key_set"), sem("tables_out"), sem("turned"), sem("tables_in"), sem("copied"))
            block = ph.enter_context(nc.Block())

            @block.sync
            def _(sp):
                sp.dma_start(last_i[:, :], a["dst"][0:(TILES - 1) * P].rearrange("(t e) -> e t", e=P)[P - 1:P, :],
                             allow_slow_non_contiguous=True).then_inc(last_in, 16)
                for t, d in (("src", src_d), ("dst", dst_d)):
                    sp.dma_start(d[0:TILES - 1, :], a[t][0:(TILES - 1) * P].rearrange("(t e) -> t e", e=P))\
                        .then_inc(edges_out, 16)
                    sp.dma_start(d[TILES - 1:TILES, 0:ETAIL], a[t][(TILES - 1) * P:E].rearrange("(o e) -> o e", o=1))\
                        .then_inc(edges_out, 16)
                sp.wait_ge(pad_set, 2)
                if ETAIL < P:
                    sp.dma_start(src_d[TILES - 1:TILES, ETAIL:P], pad[:, 0, ETAIL:P]).then_inc(edges_out, 16)
                    sp.dma_start(dst_d[TILES - 1:TILES, ETAIL:P], pad[:, 1, ETAIL:P]).then_inc(edges_out, 16)
                sp.wait_ge(b_set, 3)
                for m in range(3):
                    sp.dma_start(blk_d[m, :].rearrange("(r p) -> p r", p=RP), b_i[0:RP, m, :],
                                 allow_slow_non_contiguous=True).then_inc(tables_out, 16)
                sp.wait_ge(key_set, 1)
                sp.dma_start(key_d.rearrange("(r p) e -> p r e", p=RP), key[0:RP, :, :]).then_inc(tables_out, 16)
                sp.wait_ge(tables_out, 64)
                for m, t in enumerate((blk1, blk2, blk3)):
                    sp.dma_start(t[:, :], blk_d[m:m + 1, :]).then_inc(tables_in, 16)
                sp.wait_ge(tables_in, 48)
                sp.wait_ge(edges_out, 96 if ETAIL < P else 64)

            @block.scalar
            def _(act):
                act.wait_ge(x_zero, 1)
                act.dma_start(X[:, 0:FULL, :], a["x"][0:FULL * P, :].rearrange("(b p) f -> p b f", p=P)).then_inc(x_in, 16)
                act.dma_start(X[0:TAIL, FULL, :], a["x"][FULL * P:N, :]).then_inc(x_in, 16)
                act.wait_ge(turned, 2 * RUNS)
                nc.scalar.activation(dl[:, :], pb[1][:, 0:SLOTS], ACT.Copy).then_inc(copied, 1)
                nc.scalar.activation(src_i[:, :], pb[2][:, 0:SLOTS], ACT.Copy).then_inc(copied, 1)
                act.wait_ge(copied, 2)
                act.wait_ge(x_in, 32)

            @block.gpsimd
            def _(pool):
                pool.memset(pad[:, 0, :], 0).then_inc(pad_set, 1)
                pool.memset(pad[:, 1, :], FAR).then_inc(pad_set, 1)
                pool.memset(X[:, FULL:BLOCKS, :], 0.0).then_inc(x_zero, 1)
                pool.memset(ones[:, :], 1.0).then_inc(const_set, 1)
                pool.iota(tile_no[:, :], pattern=[[1, TILES - 1]], base=0, channel_multiplier=0,
                          allow_small_or_imprecise_dtypes=True).then_inc(const_set, 1)
                pool.iota(slot_no[:, :], pattern=[[RP, RUNS]], base=0, channel_multiplier=1,
                          allow_small_or_imprecise_dtypes=True).then_inc(const_set, 1)
                pool.iota(lane[:, :], pattern=[[1, P]], base=0, channel_multiplier=0,
                          allow_small_or_imprecise_dtypes=True).then_inc(const_set, 1)
                pool.memset(ident[:, :], 0.0).then_inc(id_zero, 1)
                pool.wait_ge(id_zero, 1)
                pool.affine_select(out=ident[:, :], in_=ident[:, :], compare_op=ALU.not_equal, fill=1.0,
                                   base=0, pattern=[[-1, P]], channel_multiplier=1).then_inc(const_set, 1)
                pool.wait_ge(edges_out, 96 if ETAIL < P else 64)
                pool.wait_ge(t_set, 1)
                for r in range(RUNS):
                    at = bass.IndirectOffsetOnAxis(ap=t_i[0:RP, r:r + 1], axis=0)
                    pool.indirect_dma_start(ed[0:RP, r, :], None, dst_d[:, :], at).then_inc(tiles_in, 16)
                    pool.indirect_dma_start(es[0:RP, r, :], None, src_d[:, :], at).then_inc(tiles_in, 16)

            @block.vector
            def _(dve):
                link = Chain(dve, t_chain)
                dve.wait_ge(last_in, 16)
                link(nc.vector.tensor_scalar(last_b[:, :], last_i[:, :], 7, None, ALU.arith_shift_right))
                link(nc.vector.tensor_copy(last_f[:, :], last_b[:, :]))
                dve.wait_ge(const_set, 5)
                nc.vector.tensor_tensor(last_f[:, :], last_f[:, :], tile_no[:, :], ALU.add).then_inc(last_set, 1)
                dve.wait_ge(spread, 1)
                for r in range(RUNS):
                    link(nc.vector.tensor_scalar(less[0:RP, :], pb[0][0:RP, 0:TILES - 1], slot_no[0:RP, r:r + 1], None,
                                                 ALU.is_lt))
                    link(nc.vector.tensor_reduce(t_f[0:RP, r:r + 1], less[0:RP, :], AX.X, ALU.add))
                nc.vector.tensor_copy(t_i[0:RP, :], t_f[0:RP, :]).then_inc(t_set, 1)
                link(nc.vector.tensor_tensor(b_f[0:RP, :], slot_no[0:RP, :], t_f[0:RP, :], ALU.subtract))
                for m, width in enumerate((P, D, AW)):
                    nc.vector.tensor_scalar(b_i[0:RP, m, :], b_f[0:RP, :], float(width), None, ALU.mult).then_inc(b_set, 1)
                link(nc.vector.tensor_scalar(b_m[0:RP, :], b_f[0:RP, :], -float(P), None, ALU.mult))
                dve.wait_ge(tiles_in, 2 * RUNS * 16)
                link(nc.vector.tensor_copy(edf[0:RP, :, :], ed[0:RP, :, :]))
                link(nc.vector.tensor_copy(esf[0:RP, :, :], es[0:RP, :, :]))
                link(nc.vector.tensor_tensor(edl[0:RP, :, :], edf[0:RP, :, :],
                                             b_m[0:RP, :].unsqueeze(2).broadcast_to([RP, RUNS, P]), ALU.add))
                link(nc.vector.tensor_scalar(inside[0:RP, :, :], edl[0:RP, :, :], 0.0, None, ALU.is_ge))
                link(nc.vector.scalar_tensor_tensor(out=inside[0:RP, :, :], in0=edl[0:RP, :, :], scalar=float(P),
                                                    in1=inside[0:RP, :, :], op0=ALU.is_lt, op1=ALU.mult))
                nc.vector.scalar_tensor_tensor(out=key[0:RP, :, :], in0=edf[0:RP, :, :], scalar=1.0,
                                               in1=inside[0:RP, :, :], op0=ALU.add, op1=ALU.mult).then_inc(key_set, 1)

            @block.tensor
            def _(pe):
                pe.wait_ge(last_set, 1)
                nc.tensor.matmul(pb[0][:, 0:TILES - 1], ones[0:1, :], last_f[:, :], start=True, stop=True).then_inc(spread, 1)
                pe.wait_ge(key_set, 1)
                for m, t in ((1, edl), (2, esf)):
                    for r in range(RUNS):
                        nc.tensor.transpose(pb[m][:, r * RP:(r + 1) * RP], t[0:RP, r, :], ident[0:RP, 0:RP])\
                            .then_inc(turned, 1)

        def layer_norm(phase, out_t, in_t, gamma=None, beta=None, add_to=None):
            with ExitStack() as ph:
                sq = ph.enter_context(nc.sbuf_tensor(f"{phase}_sq", [P, BLOCKS, D], F32))
                chain, var_set, root_set, squared = (
                    sem(f"{phase}_chain"), sem(f"{phase}_var"), sem(f"{phase}_root"), sem(f"{phase}_squared"))
                centred = sem(f"{phase}_centred")
                block = ph.enter_context(nc.Block())

                @block.vector
                def _(dve):
                    link = Chain(dve, chain)
                    link(nc.vector.tensor_reduce(stat[:, :], in_t[:, :, :], AX.X, ALU.add))
                    link(nc.vector.tensor_scalar(stat[:, :], stat[:, :], 1.0 / D, None, ALU.mult))
                    nc.vector.tensor_tensor(out_t[:, :, :], in_t[:, :, :], per_node(stat), ALU.subtract)\
                        .then_inc(centred, 1)
                    dve.wait_ge(squared, 1)
                    link(nc.vector.tensor_reduce(stat2[:, :], sq[:, :, :], AX.X, ALU.add))
                    nc.vector.tensor_scalar(stat2[:, :], stat2[:, :], 1.0 / D, EPS, ALU.mult, ALU.add).then_inc(var_set, 1)
                    dve.wait_ge(root_set, 1)
                    link(nc.vector.reciprocal(stat[:, :], stat2[:, :]))
                    link(nc.vector.tensor_tensor(out_t[:, :, :], out_t[:, :, :], per_node(stat), ALU.mult))
                    if gamma is not None:
                        for t, op in ((gamma, ALU.mult), (beta, ALU.add)):
                            wide = t[:, :].unsqueeze(1).broadcast_to([P, BLOCKS, D])
                            link(nc.vector.tensor_tensor(out_t[:, :, :], out_t[:, :, :], wide, op))
                        link(nc.vector.tensor_tensor(add_to[:, :, :], add_to[:, :, :], out_t[:, :, :], ALU.add))

                @block.scalar
                def _(act):
                    act.wait_ge(centred, 1)
                    nc.scalar.activation(sq[:, :, :], out_t[:, :, :], ACT.Square).then_inc(squared, 1)
                    act.wait_ge(var_set, 1)
                    nc.scalar.activation(stat2[:, :], stat2[:, :], ACT.Sqrt).then_inc(root_set, 1)

        with ExitStack() as ph:
            oh = ph.enter_context(nc.sbuf_tensor("deg_oh", [P, U, P], F32))
            ps = ph.enter_context(nc.psum_tensor("deg_ps", [P, BLOCKS], F32))
            oh_ready, counted, deg_root, deg_sqrt = sem("deg_oh_ready"), sem("deg_counted"), sem("deg_root"), sem("deg_sqrt")
            deg_done = sem("deg_done")
            block = ph.enter_context(nc.Block())

            @block.vector
            def _(dve):
                def step(it):
                    for h in range(2):
                        wait_count(dve, counted, U * it + HALF * (h + 1) - U)
                        nc.vector.tensor_tensor(
                            oh[:, HALF * h:HALF * (h + 1), :], lane[:, :].unsqueeze(1).broadcast_to([P, HALF, P]),
                            dl[:, bass.ds(U * it + HALF * h, HALF)].unsqueeze(2).broadcast_to([P, HALF, P]),
                            ALU.is_equal).then_inc(oh_ready, 1)
                step(0)
                with dve.Fori(1, STEPS) as it:
                    step(it)
                dve.wait_ge(deg_root, 1)
                nc.vector.reciprocal(dinv[:, :], stat[:, :]).then_inc(deg_done, 1)
                dve.wait_ge(deg_done, 1)

            @block.tensor
            def _(pe):
                nc.tensor.matmul(ps[:, :], ident[:, :], ones[:, 0:BLOCKS], start=True, stop=False, skip_group_check=True)

                def step(it):
                    _, at = nc.values_load_multi_w_load_instructions(
                        blk1[0:1, bass.ds(U * it, U)], engines=PE_ONLY, min_val=0, max_val=(BLOCKS - 1) * P,
                        skip_runtime_bounds_check_because="a slot's block is below BLOCKS")
                    for k in range(U):
                        if k % HALF == 0:
                            pe.wait_ge(oh_ready, 2 * it + k // HALF + 1)
                        nc.tensor.matmul(ps[:, bass.ds(at[k] // P, 1)], oh[:, k, :], ones[:, 0:1],
                                         start=False, stop=False, skip_group_check=True).then_inc(counted, 1)
                step(0)
                with pe.Fori(1, STEPS) as it:
                    step(it)

            @block.scalar
            def _(act):
                act.wait_ge(counted, SLOTS)
                nc.scalar.activation(stat[:, :], ps[:, :], ACT.Sqrt).then_inc(deg_root, 1)

        recycle()

        layer_norm("ln0", Z, X)

        def load_broadcast(eng, tile, vector, done):
            eng.dma_start(tile, vector.rearrange("(o f) -> o f", o=1).broadcast_to([P, vector.shape[0]])).then_inc(done, 16)

        def project(phase, in_t, kc, weights, evacuate, parts, save_t=None):
            with ExitStack() as ph:
                stage = ph.enter_context(nc.sbuf_tensor(f"{phase}_stage", [P, 2, kc, P], F32))
                zt = ph.enter_context(nc.sbuf_tensor(f"{phase}_zt", [P, 2, kc, P], F32))
                pt = [ph.enter_context(nc.psum_tensor(f"{phase}_pt{k}", [P, kc, P], F32)) for k in range(2)]
                width = sum(w for _, w in weights)
                banks = -(-width // 512)
                po = [ph.enter_context(nc.psum_tensor(f"{phase}_po{k}", [P, banks * 512], F32)) for k in range(2)]
                staged, turned_, zt_set, product, taken = (
                    sem(f"{phase}_staged"), sem(f"{phase}_turned"), sem(f"{phase}_zt"), sem(f"{phase}_product"),
                    sem(f"{phase}_taken"))
                chain = sem(f"{phase}_chain")
                block = ph.enter_context(nc.Block())

                @block.gpsimd
                def _(pool):
                    def step(i):
                        for k in range(2):
                            b = 2 * i + k
                            wait_count(pool, turned_, b - 1)
                            pool.wait_ge(x_in, 32)
                            nc.gpsimd.tensor_copy(stage[:, k, :, :],
                                                  in_t[:, bass.ds(b, 1), :].rearrange("p o (c f) -> p (o c) f", c=kc))\
                                .then_inc(staged, 1)
                    step(0)
                    with pool.Fori(1, PAIRS) as i:
                        step(i)

                @block.tensor
                def _(pe):
                    def step(i):
                        for k in range(2):
                            b = 2 * i + k
                            pe.wait_ge(staged, b + 1)
                            wait_count(pe, zt_set, b - 1)
                            for c in range(kc):
                                last = nc.tensor.transpose(pt[k][:, c, :], stage[:, k, c, :], ident[:, :])
                            last.then_inc(turned_, 1)
                            pe.wait_ge(zt_set, b + 1)
                            wait_count(pe, taken, b - 1)
                            at = 0
                            for w, n in weights:
                                for c in range(kc):
                                    last = nc.tensor.matmul(po[k][:, at:at + n], zt[:, k, c, :], w[:, c, :],
                                                            start=(c == 0), stop=(c == kc - 1))
                                at += n
                            last.then_inc(product, 1)
                    step(0)
                    with pe.Fori(1, PAIRS) as i:
                        step(i)

                @block.scalar
                def _(act):
                    def step(i):
                        for k in range(2):
                            b = 2 * i + k
                            act.wait_ge(turned_, b + 1)
                            wait_count(act, product, b - 1)
                            if save_t is not None:
                                nc.scalar.activation(save_t[:, :, bass.ds(b * P, P)], pt[k][:, :, :], ACT.Copy)
                            nc.scalar.activation(zt[:, k, :, :], pt[k][:, :, :], ACT.Copy).then_inc(zt_set, 1)
                    step(0)
                    with act.Fori(1, PAIRS) as i:
                        step(i)

                @block.vector
                def _(dve):
                    def step(i):
                        for k in range(2):
                            b = 2 * i + k
                            dve.wait_ge(product, b + 1)
                            evacuate(dve, b, po[k], chain, parts * b).then_inc(taken, 1)
                    step(0)
                    with dve.Fori(1, PAIRS) as i:
                        step(i)

        def load_weights(phase, loads):
            with ExitStack() as ph:
                done = sem(f"{phase}_in")
                block = ph.enter_context(nc.Block())

                @block.sync
                def _(sp):
                    for f in loads:
                        f(sp, done)
                    sp.wait_ge(done, 16 * len(loads))

        def matrix(tile, w):
            return lambda sp, done: sp.dma_start(tile, w.rearrange("(c p) f -> p c f", p=P),
                                                   allow_slow_non_contiguous=w.shape[1] == 1).then_inc(done, 16)

        def vector(tile, v):
            return lambda sp, done: load_broadcast(sp, tile[:, :], v, done)

        def store_rows(phase, table, tile):
            with ExitStack() as ph:
                done = sem(f"{phase}_out")
                block = ph.enter_context(nc.Block())

                @block.sync
                def _(sp):
                    sp.dma_start(rows(table), tile[:, :, :]).then_inc(done, 16)
                    sp.wait_ge(done, 16)

        def convolve(phase, table, own, out_t):
            with ExitStack() as ph:
                oh = ph.enter_context(nc.sbuf_tensor(f"{phase}_oh", [P, U, P], F32))
                ring = ph.enter_context(nc.sbuf_tensor(f"{phase}_ring", [P, U, HID], F32))
                ix = ph.enter_context(nc.sbuf_tensor(f"{phase}_ix", [P, U], I32))
                acc = ph.enter_context(nc.psum_tensor(f"{phase}_acc", [P, 8 * 512], F32))
                landed = [sem(f"{phase}_landed{k}") for k in range(U)]
                may_gather = sem(f"{phase}_may_gather")
                oh_ready, ix_ready, summed, scaled = (
                    sem(f"{phase}_oh_ready"), sem(f"{phase}_ix_ready"), sem(f"{phase}_summed"), sem(f"{phase}_scaled"))
                block = ph.enter_context(nc.Block())

                @block.gpsimd
                def _(pool):
                    def step(it):
                        for h in range(2):
                            pool.wait_ge(ix_ready, 2 * it + h + 1)
                            pool.sem_inc(may_gather, 1)
                            for k in range(HALF * h, HALF * (h + 1)):
                                pool.indirect_dma_start(
                                    ring[:, k, :], None, table[:, :],
                                    bass.IndirectOffsetOnAxis(ap=ix[:, k:k + 1], axis=0)).then_inc(landed[k], 16)
                    with pool.Fori(0, STEPS) as it:
                        step(it)

                @block.vector
                def _(dve):
                    def step(it):
                        for h in range(2):
                            mine = slice(HALF * h, HALF * (h + 1))
                            wait_count(dve, summed, U * it + HALF * (h + 1) - U)
                            nc.vector.tensor_copy(ix[:, mine], src_i[:, bass.ds(U * it + HALF * h, HALF)]).then_inc(ix_ready, 1)
                            nc.vector.tensor_tensor(
                                oh[:, mine, :], lane[:, :].unsqueeze(1).broadcast_to([P, HALF, P]),
                                dl[:, bass.ds(U * it + HALF * h, HALF)].unsqueeze(2).broadcast_to([P, HALF, P]),
                                ALU.is_equal).then_inc(oh_ready, 1)
                    step(0)
                    with dve.Fori(1, STEPS) as it:
                        step(it)
                    dve.wait_ge(summed, SLOTS)
                    nc.vector.tensor_tensor(out_t[:, :, :],
                                            acc[:, 0:BLOCKS * HID].rearrange("p (b f) -> p b f", f=HID),
                                            dinv[:, :].unsqueeze(2).broadcast_to([P, BLOCKS, HID]), ALU.mult).then_inc(scaled, 1)
                    dve.wait_ge(scaled, 1)

                @block.tensor
                def _(pe):
                    for b in range(0, BLOCKS, 512 // HID):
                        n = min(512 // HID, BLOCKS - b)
                        nc.tensor.matmul(acc[:, b * HID:(b + n) * HID], ident[:, :], own[:, b:b + n, :],
                                         start=True, stop=False, skip_group_check=True)

                    def step(it):
                        _, at = nc.values_load_multi_w_load_instructions(
                            blk1[0:1, bass.ds(U * it, U)], engines=PE_ONLY, min_val=0, max_val=(BLOCKS - 1) * P,
                            skip_runtime_bounds_check_because="a slot's block is below BLOCKS")
                        for k in range(U):
                            if k % HALF == 0:
                                pe.wait_ge(oh_ready, 2 * it + k // HALF + 1)
                            pe.wait_ge(landed[k], 16 * it + 16)
                            nc.tensor.matmul(acc[:, bass.ds(at[k], HID)], oh[:, k, :], ring[:, k, :],
                                             start=False, stop=False, skip_group_check=True).then_inc(summed, 1)
                    step(0)
                    with pe.Fori(1, STEPS) as it:
                        step(it)

        with ExitStack() as ph:
            G = ph.enter_context(nc.sbuf_tensor("G", [P, BLOCKS, HID], F32))
            A = ph.enter_context(nc.sbuf_tensor("A", [P, BLOCKS, HID], F32))
            w1 = ph.enter_context(nc.sbuf_tensor("gw1", [P, KC, HID], F32))
            b1 = ph.enter_context(nc.sbuf_tensor("gb1", [P, HID], F32))
            w2 = ph.enter_context(nc.sbuf_tensor("gw2", [P, 1, D], F32))
            b2 = ph.enter_context(nc.sbuf_tensor("gb2", [P, D], F32))
            load_weights("gw", [matrix(w1[:, :, :], a["L0_gnn_W1"]), matrix(w2[:, :, :], a["L0_gnn_W2"]),
                                vector(b1, a["L0_gnn_b1"]), vector(b2, a["L0_gnn_b2"])])

            project("h1", Z, KC, [(w1, HID)], lambda dve, b, po, chain, at: nc.vector.tensor_scalar(
                G[:, bass.ds(b, 1), :], po[:, 0:HID].unsqueeze(1), dinv[:, bass.ds(b, 1)], None, ALU.mult), 0)
            store_rows("g1", g1_d, G)
            convolve("cv1", g1_d, G, A)

            with ExitStack() as ph2:
                chain = sem("relu_chain")
                block = ph2.enter_context(nc.Block())

                @block.vector
                def _(dve):
                    link = Chain(dve, chain)
                    link(nc.vector.tensor_tensor(A[:, :, :], A[:, :, :],
                                                 b1[:, :].unsqueeze(1).broadcast_to([P, BLOCKS, HID]), ALU.add))
                    link(nc.vector.scalar_tensor_tensor(
                        out=G[:, :, :], in0=A[:, :, :], scalar=0.0,
                        in1=dinv[:, :].unsqueeze(2).broadcast_to([P, BLOCKS, HID]), op0=ALU.max, op1=ALU.mult))
            store_rows("g2", g2_d, G)
            convolve("cv2", g2_d, G, A)

            def add_conv(dve, b, po, chain, at):
                nc.vector.tensor_tensor(X[:, bass.ds(b, 1), :], X[:, bass.ds(b, 1), :], b2[:, :].unsqueeze(1), ALU.add)\
                    .then_inc(chain, 1)
                dve.wait_ge(chain, at + 1)
                return nc.vector.tensor_tensor(X[:, bass.ds(b, 1), :], X[:, bass.ds(b, 1), :], po[:, 0:D].unsqueeze(1), ALU.add)
            project("h2", A, 1, [(w2, D)], add_conv, 1)

        layer_norm("ln1", Z, X)

        recycle()

        HC = EH // P
        with ExitStack() as ph:
            def sb(name, shape, dt=F32):
                return ph.enter_context(nc.sbuf_tensor(name, shape, dt))

            zt_all = sb("m_zt_all", [P, KC, NODES])
            wg = sb("m_wg", [P, KC, EXP])
            bg = sb("m_bg", [P, EXP])
            bias = sb("m_bias", [P, EXP])
            b1 = sb("m_b1", [P, EXP * HC])
            b2 = sb("m_b2", [1, EXP, D])
            logit = sb("m_logit", [P, BLOCKS, EXP])
            rest = sb("m_rest", [P, BLOCKS, EXP])
            order = sb("m_order", [P, BLOCKS, EXP])
            pick = [sb(f"m_pick{i}", [P, BLOCKS, EXP]) for i in range(2)]
            comb = sb("m_comb", [P, BLOCKS, EXP])
            top_v = [sb(f"m_top{i}", [P, BLOCKS]) for i in range(2)]
            first = sb("m_first", [P, BLOCKS])
            gap = sb("m_gap", [P, BLOCKS])
            load_weights("mw", [
                matrix(wg[:, :, :], a["L0_ffn_Wg"]), vector(bg, a["L0_ffn_bg"]), vector(bias, a["L0_ffn_bias"]),
                lambda sp, done: sp.dma_start(b1[:, :].rearrange("p (e c) -> p e c", c=HC),
                                              a["L0_ffn_b1"].rearrange("e (c p) -> p e c", p=P),
                                              allow_slow_non_contiguous=True).then_inc(done, 16),
                lambda sp, done: sp.dma_start(b2[:, :, :], a["L0_ffn_b2"].rearrange("(o e) d -> o e d", o=1)).then_inc(done, 16)])

            def add_bg(dve, b, po, chain, at):
                nc.vector.tensor_tensor(logit[:, bass.ds(b, 1), :], po[:, 0:EXP].unsqueeze(1), bg[:, :].unsqueeze(1), ALU.add)\
                    .then_inc(chain, 1)
                dve.wait_ge(chain, at + 1)
                return nc.vector.tensor_tensor(logit[:, bass.ds(b, 1), :], logit[:, bass.ds(b, 1), :],
                                               bias[:, :].unsqueeze(1), ALU.add)
            project("gate", Z, KC, [(wg, EXP)], add_bg, 1, save_t=zt_all)

            with ExitStack() as ph2:
                chain, gap_set, gap_exp, order_set = sem("pick_chain"), sem("gap_set"), sem("gap_exp"), sem("order_set")
                block = ph2.enter_context(nc.Block())

                @block.gpsimd
                def _(pool):
                    pool.iota(order[:, :, :], pattern=[[0, BLOCKS], [1, EXP]], base=0, channel_multiplier=0,
                              allow_small_or_imprecise_dtypes=True).then_inc(order_set, 1)

                @block.vector
                def _(dve):
                    link = Chain(dve, chain)

                    def wide(t):
                        return t[:, :].unsqueeze(2).broadcast_to([P, BLOCKS, EXP])

                    dve.wait_ge(order_set, 1)
                    left = logit
                    for i in range(2):
                        link(nc.vector.tensor_reduce(top_v[i][:, :], left[:, :, :], AX.X, ALU.max))
                        link(nc.vector.tensor_tensor(pick[i][:, :, :], left[:, :, :], wide(top_v[i]), ALU.not_equal))
                        link(nc.vector.scalar_tensor_tensor(out=pick[i][:, :, :], in0=pick[i][:, :, :], scalar=float(EXP),
                                                            in1=order[:, :, :], op0=ALU.mult, op1=ALU.add))
                        link(nc.vector.tensor_reduce(first[:, :], pick[i][:, :, :], AX.X, ALU.min))
                        link(nc.vector.tensor_tensor(pick[i][:, :, :], order[:, :, :], wide(first), ALU.is_equal))
                        if i == 0:
                            link(nc.vector.scalar_tensor_tensor(out=rest[:, :, :], in0=pick[0][:, :, :], scalar=-BIG,
                                                                in1=logit[:, :, :], op0=ALU.mult, op1=ALU.add))
                            left = rest
                    nc.vector.tensor_tensor(gap[:, :], top_v[1][:, :], top_v[0][:, :], ALU.subtract).then_inc(gap_set, 1)
                    dve.wait_ge(gap_exp, 1)
                    link(nc.vector.tensor_scalar(first[:, :], gap[:, :], 1.0, None, ALU.add))
                    link(nc.vector.reciprocal(first[:, :], first[:, :]))
                    link(nc.vector.tensor_tensor(gap[:, :], gap[:, :], first[:, :], ALU.mult))
                    link(nc.vector.tensor_tensor(pick[0][:, :, :], pick[0][:, :, :], wide(first), ALU.mult))
                    link(nc.vector.tensor_tensor(pick[1][:, :, :], pick[1][:, :, :], wide(gap), ALU.mult))
                    link(nc.vector.tensor_tensor(comb[:, :, :], pick[0][:, :, :], pick[1][:, :, :], ALU.add))

                @block.scalar
                def _(act):
                    act.wait_ge(gap_set, 1)
                    nc.scalar.activation(gap[:, :], gap[:, :], ACT.Exp).then_inc(gap_exp, 1)

            with ExitStack() as ph2:
                w1 = [ph2.enter_context(nc.sbuf_tensor(f"m_w1_{k}", [P, KC, EH], F32)) for k in range(2)]
                w2 = [ph2.enter_context(nc.sbuf_tensor(f"m_w2_{k}", [P, HC, D], F32)) for k in range(2)]
                ht = ph2.enter_context(nc.sbuf_tensor("m_ht", [P, HC, 2 * P], F32))
                ps_h = [ph2.enter_context(nc.psum_tensor(f"m_ps_h{c}", [P, 512], F32)) for c in range(HC)]
                ps_y = [ph2.enter_context(nc.psum_tensor(f"m_ps_y{k}", [P, 512], F32)) for k in range(2)]
                w_in = [sem(f"m_w_in{k}") for k in range(2)]
                h_set, h_relu, y_set, y_taken = sem("m_h_set"), sem("m_h_relu"), sem("m_y_set"), sem("m_y_taken")
                block = ph2.enter_context(nc.Block())

                @block.sync
                def _(sp):
                    def step(j):
                        for k in range(2):
                            wait_count(sp, y_set, (2 * j + k - 1) * NODES // P)
                            e = 2 * j + k
                            sp.dma_start(w1[k][:, :, :], a["L0_ffn_W1"][bass.ds(e, 1), :, :]
                                         .rearrange("o (c p) f -> p (o c) f", p=P)).then_inc(w_in[k], 16)
                            sp.dma_start(w2[k][:, :, :], a["L0_ffn_W2"][bass.ds(e, 1), :, :]
                                         .rearrange("o (c p) f -> p (o c) f", p=P)).then_inc(w_in[k], 16)
                    step(0)
                    with sp.Fori(1, EXP // 2) as j:
                        step(j)

                @block.tensor
                def _(pe):
                    with pe.Fori(0, EXP // 2) as j:
                        for k in range(2):
                            with pe.Fori(0, PAIRS) as i:
                                pe.wait_ge(w_in[k], 32 * j + 32)
                                n = (2 * j + k) * PAIRS + i
                                for h in range(HC):
                                    for c in range(KC):
                                        last = nc.tensor.matmul(ps_h[h][:, 0:2 * P], w1[k][:, c, h * P:(h + 1) * P],
                                                                zt_all[:, c, bass.ds(i * 2 * P, 2 * P)],
                                                                start=(c == 0), stop=(c == KC - 1))
                                    last.then_inc(h_set, 1)
                                for m in range(2):
                                    pe.wait_ge(y_taken, 2 * n)
                                    for h in range(HC):
                                        pe.wait_ge(h_relu, HC * n + h + 1)
                                        nc.tensor.matmul(ps_y[m][:, 0:D], ht[:, h, m * P:(m + 1) * P], w2[k][:, h, :],
                                                         start=(h == 0), stop=False)
                                    nc.tensor.matmul(ps_y[m][:, 0:D], ones[0:1, :],
                                                     b2[0:1, bass.ds(2 * j + k, 1), :].rearrange("o e d -> o (e d)"),
                                                     start=False, stop=True).then_inc(y_set, 1)

                @block.scalar
                def _(act):
                    with act.Fori(0, EXP // 2) as j:
                        for k in range(2):
                            with act.Fori(0, PAIRS) as i:
                                n = (2 * j + k) * PAIRS + i
                                act.wait_ge(y_set, 2 * n)
                                for h in range(HC):
                                    act.wait_ge(h_set, HC * n + h + 1)
                                    nc.scalar.activation(ht[:, h, :], ps_h[h][:, 0:2 * P], ACT.Relu,
                                                         bias=b1[:, bass.ds((2 * j + k) * HC + h, 1)]).then_inc(h_relu, 1)

                @block.vector
                def _(dve):
                    with dve.Fori(0, EXP) as e:
                        with dve.Fori(0, PAIRS) as i:
                            for m in range(2):
                                dve.wait_ge(y_set, 2 * (e * PAIRS + i) + m + 1)
                                nc.vector.scalar_tensor_tensor(
                                    out=X[:, bass.ds(2 * i + m, 1), :], in0=ps_y[m][:, 0:D].unsqueeze(1),
                                    scalar=comb[:, bass.ds(2 * i + m, 1), bass.ds(e, 1)].rearrange("p a b -> p (a b)"),
                                    in1=X[:, bass.ds(2 * i + m, 1), :], op0=ALU.mult, op1=ALU.add).then_inc(y_taken, 1)

        layer_norm("ln2", Z, X)

        recycle()

        SCALE = float(HD) ** -0.5
        with ExitStack() as at_ph:
            skip = at_ph.enter_context(nc.sbuf_tensor("a_skip", [P, BLOCKS, D], F32))
            L = at_ph.enter_context(nc.sbuf_tensor("a_L", [P, HEADS, SLOTS], F32))
            with ExitStack() as q_ph:
                Q = q_ph.enter_context(nc.sbuf_tensor("a_Q", [P, BLOCKS, D], F32))
                with ExitStack() as ph:
                    K = ph.enter_context(nc.sbuf_tensor("a_K", [P, BLOCKS, D], F32))
                    V = ph.enter_context(nc.sbuf_tensor("a_V", [P, BLOCKS, D], F32))
                    names = ("q", "k", "v", "skip")
                    w = [ph.enter_context(nc.sbuf_tensor(f"a_w{m}", [P, KC, D], F32)) for m in names]
                    bs = [ph.enter_context(nc.sbuf_tensor(f"a_b{m}", [P, D], F32)) for m in names]
                    load_weights("aw", [matrix(w[m][:, :, :], a["L1_gnn_W" + n]) for m, n in enumerate(names)] +
                                 [vector(bs[m], a["L1_gnn_b" + n]) for m, n in enumerate(names)])

                    def add_biases(dve, b, po, chain, at):
                        for m, t in enumerate((Q, K, V, skip)):
                            last = nc.vector.tensor_tensor(t[:, bass.ds(b, 1), :], po[:, m * D:(m + 1) * D].unsqueeze(1),
                                                           bs[m][:, :].unsqueeze(1), ALU.add)
                        return last
                    project("qkvs", Z, KC, [(t, D) for t in w], add_biases, 0)
                    store_rows("k", k_d, K)
                    store_rows("v", v_d, V)

                with ExitStack() as ph:
                    oh = ph.enter_context(nc.sbuf_tensor("l_oh", [P, U, P], F32))
                    oht = ph.enter_context(nc.sbuf_tensor("l_oht", [P, U, P], F32))
                    ring = ph.enter_context(nc.sbuf_tensor("l_ring", [P, U, D], F32))
                    prod = ph.enter_context(nc.sbuf_tensor("l_prod", [P, HALF, D], F32))
                    ix = ph.enter_context(nc.sbuf_tensor("l_ix", [P, U], I32))
                    pt = [ph.enter_context(nc.psum_tensor(f"l_pt{h}", [P, HALF, P], F32)) for h in range(2)]
                    pq = [ph.enter_context(nc.psum_tensor(f"l_pq{h}", [P, HALF, D], F32)) for h in range(2)]
                    landed = [sem(f"l_landed{k}") for k in range(U)]
                    may_gather = sem("l_may_gather")
                    oh_ready, ix_ready, turned_, oht_set, q_set, multiplied, reduced = (
                        sem("l_oh_ready"), sem("l_ix_ready"), sem("l_turned"), sem("l_oht_set"), sem("l_q_set"),
                        sem("l_multiplied"), sem("l_reduced"))
                    block = ph.enter_context(nc.Block())

                    @block.gpsimd
                    def _(pool):
                        with pool.Fori(0, STEPS) as it:
                            for h in range(2):
                                pool.wait_ge(ix_ready, 2 * it + h + 1)
                                pool.sem_inc(may_gather, 1)
                                for k in range(HALF * h, HALF * (h + 1)):
                                    pool.indirect_dma_start(
                                        ring[:, k, :], None, k_d[:, :],
                                        bass.IndirectOffsetOnAxis(ap=ix[:, k:k + 1], axis=0)).then_inc(landed[k], 16)

                    @block.vector
                    def _(dve):
                        def prepare(it, h):
                            mine = slice(HALF * h, HALF * (h + 1))
                            wait_count(dve, multiplied, 2 * it + h - 1)
                            nc.vector.tensor_copy(ix[:, mine], src_i[:, bass.ds(U * it + HALF * h, HALF)]).then_inc(ix_ready, 1)
                            wait_count(dve, turned_, 2 * it + h - 1)
                            nc.vector.tensor_tensor(
                                oh[:, mine, :], lane[:, :].unsqueeze(1).broadcast_to([P, HALF, P]),
                                dl[:, bass.ds(U * it + HALF * h, HALF)].unsqueeze(2).broadcast_to([P, HALF, P]),
                                ALU.is_equal).then_inc(oh_ready, 1)

                        def use(it, h):
                            dve.wait_ge(q_set, 2 * it + h + 1)
                            for k in range(HALF * h, HALF * (h + 1)):
                                dve.wait_ge(landed[k], 16 * it + 16)
                            wait_count(dve, reduced, 2 * it + h)
                            nc.vector.tensor_tensor(prod[:, :, :], pq[h][:, :, :], ring[:, HALF * h:HALF * (h + 1), :],
                                                    ALU.mult).then_inc(multiplied, 1)
                            dve.wait_ge(multiplied, 2 * it + h + 1)
                            nc.vector.tensor_reduce(
                                L[:, :, bass.ds(U * it + HALF * h, HALF)].rearrange("p n k -> p k n"),
                                prod[:, :, :].rearrange("p k (n d) -> p k n d", d=HD), AX.X, ALU.add).then_inc(reduced, 1)
                        prepare(0, 0)
                        prepare(0, 1)
                        with dve.Fori(0, STEPS - 1) as it:
                            for h in range(2):
                                use(it, h)
                                prepare(it + 1, h)
                        use(STEPS - 1, 0)
                        use(STEPS - 1, 1)
                        dve.wait_ge(reduced, 2 * STEPS)

                    @block.tensor
                    def _(pe):
                        def step(it):
                            _, at = nc.values_load_multi_w_load_instructions(
                                blk2[0:1, bass.ds(U * it, U)], engines=PE_ONLY, min_val=0, max_val=(BLOCKS - 1) * D,
                                skip_runtime_bounds_check_because="a slot's block is below BLOCKS")
                            q_rows = Q[:, :, :].rearrange("p b f -> p (b f)")
                            for h in range(2):
                                pe.wait_ge(oh_ready, 2 * it + h + 1)
                                wait_count(pe, oht_set, 2 * it + h - 1)
                                for k in range(HALF):
                                    last = nc.tensor.transpose(pt[h][:, k, :], oh[:, HALF * h + k, :], ident[:, :])
                                last.then_inc(turned_, 1)
                            for h in range(2):
                                pe.wait_ge(oht_set, 2 * it + h + 1)
                                wait_count(pe, multiplied, 2 * it + h - 1)
                                for k in range(HALF):
                                    last = nc.tensor.matmul(pq[h][:, k, :], oht[:, HALF * h + k, :],
                                                            q_rows[:, bass.ds(at[HALF * h + k], D)], start=True, stop=True)
                                last.then_inc(q_set, 1)
                        step(0)
                        with pe.Fori(1, STEPS) as it:
                            step(it)

                    @block.scalar
                    def _(act):
                        def step(it):
                            for h in range(2):
                                act.wait_ge(turned_, 2 * it + h + 1)
                                wait_count(act, q_set, 2 * it + h - 1)
                                nc.scalar.activation(oht[:, HALF * h:HALF * (h + 1), :], pt[h][:, :, :], ACT.Copy)\
                                    .then_inc(oht_set, 1)
                        step(0)
                        with act.Fori(1, STEPS) as it:
                            step(it)

            with ExitStack() as ph:
                def sb(name, shape, dt=F32):
                    return ph.enter_context(nc.sbuf_tensor(name, shape, dt))

                LT = sb("s_LT", [P, CS, P])
                FT = sb("s_FT", [P, CS, P])
                MT = sb("s_MT", [P, CS, P])
                KT = sb("s_KT", [P, CS, P])
                brk = sb("s_brk", [P, SEQ + 1])
                cols = sb("s_cols", [P, 4])
                row = sb("s_row", [1, 2, HEADS, CH])
                pen_f = sb("s_pen_f", [1, HEADS, CH])
                pen_b = sb("s_pen_b", [1, HEADS, CH])
                link_f = sb("s_link_f", [1, HEADS, CH])
                link_b = sb("s_link_b", [1, HEADS, CH])
                ends = sb("s_ends", [1, HEADS, CH])
                run_max = sb("s_run_max", [1, HEADS, CH])
                carry = sb("s_carry", [1, HEADS, CH])
                init = sb("s_init", [P, 2])
                NT = 4
                groups = [(g, min(NT, CS - g)) for g in range(0, CS, NT)]
                pt = [ph.enter_context(nc.psum_tensor(f"s_pt{i}", [P, NT, P], F32)) for i in range(2)]
                pr = ph.enter_context(nc.psum_tensor("s_pr", [1, 512], F32))
                pc = ph.enter_context(nc.psum_tensor("s_pc", [P, 2], F32))
                key_in, s_turned, s_copied, col_set, row_set, row_copied, carry_set, init_set = (
                    sem("key_in"), sem("s_turned"), sem("s_copied"), sem("col_set"), sem("row_set"), sem("row_copied"),
                    sem("carry_set"), sem("init_set"))
                s_chain, less_max, s_exp, e_turned, e_copied = (
                    sem("s_chain"), sem("less_max"), sem("s_exp"), sem("e_turned"), sem("e_copied"))
                block = ph.enter_context(nc.Block())
                lt, ft, mt, kt = (t[:, :, :].rearrange("p j e -> p (j e)") for t in (LT, FT, MT, KT))

                @block.sync
                def _(sp):
                    for h in range(HEADS):
                        sp.dma_start(KT[h * CH:(h + 1) * CH, :, :].rearrange("c j e -> c (j e)"),
                                     key_d.rearrange("(c j) e -> c (j e)", j=CS)).then_inc(key_in, 16)
                    sp.wait_ge(key_in, 16 * HEADS)

                @block.tensor
                def _(pe):
                    by_j = L[:, :, :].rearrange("p h (c j) -> p j (h c)", j=CS)
                    for g, (j0, n) in enumerate(groups):
                        wait_count(pe, s_copied, g - 1)
                        for j in range(n):
                            last = nc.tensor.transpose(pt[g % 2][:, j, :], by_j[:, j0 + j, :], ident[:, :])
                        last.then_inc(s_turned, 1)
                    for n, m in enumerate((0, 1, 2, 3)):
                        pe.wait_ge(col_set, n + 1)
                        nc.tensor.matmul(pr[0:1, m * P:(m + 1) * P], cols[:, m:m + 1], ident[:, :], start=True, stop=True)\
                            .then_inc(row_set, 1)
                        if m >= 2:
                            pe.wait_ge(carry_set, m - 1)
                            nc.tensor.matmul(pc[:, m - 2:m - 1], carry[:, :, :].rearrange("o h c -> o (h c)"), ones[0:1, 0:1],
                                             start=True, stop=True).then_inc(init_set, 1)
                    pe.wait_ge(s_exp, 1)
                    for g, (j0, n) in enumerate(groups):
                        wait_count(pe, e_copied, g - 1)
                        for j in range(n):
                            last = nc.tensor.transpose(pt[g % 2][:, j, :], MT[:, j0 + j, :], ident[:, :])
                        last.then_inc(e_turned, 1)

                @block.scalar
                def _(act):
                    for g, (j0, n) in enumerate(groups):
                        act.wait_ge(s_turned, g + 1)
                        nc.scalar.activation(LT[:, j0:j0 + n, :], pt[g % 2][:, 0:n, :], ACT.Copy).then_inc(s_copied, 1)
                    act.wait_ge(less_max, 1)
                    nc.scalar.activation(MT[:, :, :], MT[:, :, :], ACT.Exp, scale=SCALE).then_inc(s_exp, 1)
                    by_j = L[:, :, :].rearrange("p h (c j) -> p j (h c)", j=CS)
                    for g, (j0, n) in enumerate(groups):
                        act.wait_ge(e_turned, g + 1)
                        for j in range(n):
                            last = nc.scalar.activation(by_j[:, j0 + j, :], pt[g % 2][:, j, :], ACT.Copy)
                        last.then_inc(e_copied, 1)

                @block.vector
                def _(dve):
                    link = Chain(dve, s_chain)
                    dve.wait_ge(key_in, 16 * HEADS)
                    link(nc.vector.memset(brk[:, 0:1], 0.0))
                    link(nc.vector.memset(brk[:, SEQ:SEQ + 1], 0.0))
                    link(nc.vector.tensor_tensor(brk[:, 1:SEQ], kt[:, 1:SEQ], kt[:, 0:SEQ - 1], ALU.not_equal))
                    link(nc.vector.tensor_scalar(brk[:, 1:SEQ], brk[:, 1:SEQ], -BIG, None, ALU.mult))
                    nc.vector.tensor_copy(cols[:, 0:1], kt[:, 0:1]).then_inc(col_set, 1)
                    nc.vector.tensor_copy(cols[:, 1:2], kt[:, SEQ - 1:SEQ]).then_inc(col_set, 1)
                    dve.wait_ge(row_set, 2)
                    first, final = (pr[0:1, m * P:(m + 1) * P].rearrange("o (h c) -> o h c", h=HEADS) for m in (0, 1))
                    row0, row1 = (row[:, m, :, :] for m in (0, 1))
                    link(nc.vector.tensor_copy(row0, first))
                    link(nc.vector.tensor_copy(row1, final))
                    link(nc.vector.memset(link_f[:, :, :], -BIG))
                    link(nc.vector.memset(link_b[:, :, :], -BIG))
                    link(nc.vector.tensor_tensor(link_f[:, :, 1:CH], row0[:, :, 1:CH], row1[:, :, 0:CH - 1], ALU.not_equal))
                    link(nc.vector.tensor_scalar(link_f[:, :, 1:CH], link_f[:, :, 1:CH], -BIG, None, ALU.mult))
                    link(nc.vector.tensor_copy(link_b[:, :, 0:CH - 1], link_f[:, :, 1:CH]))
                    link(nc.vector.tensor_tensor(ends[:, :, :], row0, row1, ALU.not_equal))
                    link(nc.vector.scalar_tensor_tensor(out=pen_f[:, :, :], in0=ends[:, :, :], scalar=-BIG, in1=link_f[:, :, :],
                                                        op0=ALU.mult, op1=ALU.add))
                    link(nc.vector.scalar_tensor_tensor(out=pen_b[:, :, :], in0=ends[:, :, :], scalar=-BIG, in1=link_b[:, :, :],
                                                        op0=ALU.mult, op1=ALU.add))
                    dve.wait_ge(s_copied, len(groups))

                    def flat(t):
                        return t[:, :, :].rearrange("o h c -> o (h c)")

                    link(nc.vector.tensor_tensor_scan(ft, brk[:, 0:SEQ], lt, -BIG, ALU.add, ALU.max))
                    nc.vector.tensor_copy(cols[:, 2:3], ft[:, SEQ - 1:SEQ]).then_inc(col_set, 1)
                    dve.wait_ge(row_set, 3)
                    link(nc.vector.tensor_copy(ends[:, :, :], pr[0:1, 2 * P:3 * P].rearrange("o (h c) -> o h c", h=HEADS)))
                    link(nc.vector.tensor_tensor_scan(flat(run_max), flat(pen_f), flat(ends), -BIG, ALU.add, ALU.max))
                    link(nc.vector.memset(carry[:, :, :], -BIG))
                    nc.vector.tensor_tensor(carry[:, :, 1:CH], run_max[:, :, 0:CH - 1],
                                            link_f[:, :, 1:CH], ALU.add).then_inc(carry_set, 1)
                    dve.wait_ge(init_set, 1)
                    link(nc.vector.tensor_copy(init[:, 0:1], pc[:, 0:1]))
                    link(nc.vector.tensor_tensor_scan(ft, brk[:, 0:SEQ], lt, init[:, 0:1], ALU.add, ALU.max))
                    back = brk[:, SEQ:0:-1]
                    link(nc.vector.tensor_tensor_scan(mt[:, ::-1], back, ft[:, ::-1], -BIG, ALU.add, ALU.max))
                    nc.vector.tensor_copy(cols[:, 3:4], mt[:, 0:1]).then_inc(col_set, 1)
                    dve.wait_ge(row_set, 4)
                    link(nc.vector.tensor_copy(ends[:, :, :], pr[0:1, 3 * P:4 * P].rearrange("o (h c) -> o h c", h=HEADS)))
                    link(nc.vector.tensor_tensor_scan(flat(run_max)[:, ::-1], flat(pen_b)[:, ::-1], flat(ends)[:, ::-1],
                                                      -BIG, ALU.add, ALU.max))
                    link(nc.vector.memset(carry[:, :, :], -BIG))
                    nc.vector.tensor_tensor(carry[:, :, 0:CH - 1], run_max[:, :, 1:CH],
                                            link_b[:, :, 0:CH - 1], ALU.add).then_inc(carry_set, 1)
                    dve.wait_ge(init_set, 2)
                    link(nc.vector.tensor_copy(init[:, 1:2], pc[:, 1:2]))
                    link(nc.vector.tensor_tensor_scan(mt[:, ::-1], back, ft[:, ::-1], init[:, 1:2], ALU.add, ALU.max))
                    nc.vector.tensor_tensor(mt, lt, mt, ALU.subtract).then_inc(less_max, 1)

            with ExitStack() as sum_ph:
                total = sum_ph.enter_context(nc.sbuf_tensor("a_total", [P, BLOCKS * AW], F32))
                with ExitStack() as ph:
                    oh = ph.enter_context(nc.sbuf_tensor("v_oh", [P, U, P], F32))
                    ring = ph.enter_context(nc.sbuf_tensor("v_ring", [P, U, D], F32))
                    msg = ph.enter_context(nc.sbuf_tensor("v_msg", [P, U, AW], F32))
                    ix = ph.enter_context(nc.sbuf_tensor("v_ix", [P, U], I32))
                    pm = [ph.enter_context(nc.psum_tensor(f"v_pm{k}", [P, 512], F32)) for k in range(U)]
                    landed = [sem(f"v_landed{k}") for k in range(U)]
                    may_gather = sem("v_may_gather")
                    oh_ready, ix_ready, msg_set, weight_set, product, added, cleared = (
                        sem("v_oh_ready"), sem("v_ix_ready"), sem("v_msg_set"), sem("v_weight_set"), sem("v_product"),
                        sem("v_added"), sem("v_cleared"))
                    block = ph.enter_context(nc.Block())

                    @block.gpsimd
                    def _(pool):
                        pool.memset(total[:, :], 0.0).then_inc(cleared, 1)
                        with pool.Fori(0, STEPS) as it:
                            for h in range(2):
                                pool.wait_ge(ix_ready, 2 * it + h + 1)
                                pool.sem_inc(may_gather, 1)
                                for k in range(HALF * h, HALF * (h + 1)):
                                    pool.indirect_dma_start(
                                        ring[:, k, :], None, v_d[:, :],
                                        bass.IndirectOffsetOnAxis(ap=ix[:, k:k + 1], axis=0)).then_inc(landed[k], 16)

                    @block.scalar
                    def _(act):
                        def step(it):
                            for h in range(2):
                                wait_count(act, product, U * it + HALF * (h + 1) - U)
                                nc.scalar.activation(msg[:, HALF * h:HALF * (h + 1), D:AW],
                                                     L[:, :, bass.ds(U * it + HALF * h, HALF)].rearrange("p n k -> p k n"), ACT.Copy).then_inc(weight_set, 1)
                        step(0)
                        with act.Fori(1, STEPS) as it:
                            step(it)

                    @block.vector
                    def _(dve):
                        def stage(it, h):
                            nc.vector.tensor_copy(ix[:, HALF * h:HALF * (h + 1)],
                                                  src_i[:, bass.ds(U * it + HALF * h, HALF)]).then_inc(ix_ready, 1)

                        def messages(it, h, more):
                            mine = slice(HALF * h, HALF * (h + 1))
                            slots = bass.ds(U * it + HALF * h, HALF)
                            wait_count(dve, product, U * it + HALF * (h + 1) - U)
                            nc.vector.tensor_tensor(
                                oh[:, mine, :], lane[:, :].unsqueeze(1).broadcast_to([P, HALF, P]),
                                dl[:, slots].unsqueeze(2).broadcast_to([P, HALF, P]), ALU.is_equal).then_inc(oh_ready, 1)
                            for k in range(HALF * h, HALF * (h + 1)):
                                dve.wait_ge(landed[k], 16 * it + 16)
                            nc.vector.tensor_tensor(
                                msg[:, mine, 0:D].rearrange("p k (n d) -> p k n d", d=HD),
                                ring[:, mine, :].rearrange("p k (n d) -> p k n d", d=HD),
                                L[:, :, slots].rearrange("p n k -> p k n").unsqueeze(3).broadcast_to([P, HALF, HEADS, HD]), ALU.mult).then_inc(msg_set, 1)
                            if more:
                                dve.wait_ge(msg_set, 2 * it + h + 1)
                                stage(it + 1, h)

                        def add(it, h, at):
                            for k in range(HALF * h, HALF * (h + 1)):
                                dve.wait_ge(product, U * it + k + 1)
                                where = total[:, bass.ds(at[k], AW)]
                                wait_count(dve, added, U * it + k)
                                nc.vector.tensor_tensor(where, where, pm[k][:, 0:AW], ALU.add).then_inc(added, 1)

                        def blocks_of(it):
                            return nc.values_load_multi_w_load_instructions(
                                blk3[0:1, bass.ds(U * it, U)], engines=DVE_ONLY, min_val=0, max_val=(BLOCKS - 1) * AW,
                                skip_runtime_bounds_check_because="a slot's block is below BLOCKS")[1]
                        dve.wait_ge(cleared, 1)
                        stage(0, 0)
                        stage(0, 1)
                        messages(0, 0, True)
                        messages(0, 1, True)
                        with dve.Fori(1, STEPS - 1) as it:
                            at = blocks_of(it - 1)
                            for h in range(2):
                                add(it - 1, h, at)
                                messages(it, h, True)
                        at = blocks_of(STEPS - 2)
                        for h in range(2):
                            add(STEPS - 2, h, at)
                            messages(STEPS - 1, h, False)
                        at = blocks_of(STEPS - 1)
                        for h in range(2):
                            add(STEPS - 1, h, at)
                        dve.wait_ge(added, SLOTS)

                    @block.tensor
                    def _(pe):
                        def step(it):
                            for k in range(U):
                                if k % HALF == 0:
                                    pe.wait_ge(oh_ready, 2 * it + k // HALF + 1)
                                    pe.wait_ge(msg_set, 2 * it + k // HALF + 1)
                                    pe.wait_ge(weight_set, 2 * it + k // HALF + 1)
                                wait_count(pe, added, U * it + k - U + 1)
                                nc.tensor.matmul(pm[k][:, 0:AW], oh[:, k, :], msg[:, k, :], start=True, stop=True)\
                                    .then_inc(product, 1)
                        step(0)
                        with pe.Fori(1, STEPS) as it:
                            step(it)

                gamma = sum_ph.enter_context(nc.sbuf_tensor("a_gamma", [P, D], F32))
                beta = sum_ph.enter_context(nc.sbuf_tensor("a_beta", [P, D], F32))
                load_weights("agb", [vector(gamma, a["L1_gnn_gamma"]), vector(beta, a["L1_gnn_beta"])])
                with ExitStack() as ph:
                    den = ph.enter_context(nc.sbuf_tensor("f_den", [P, BLOCKS, HEADS], F32))
                    chain, out_set, gelu_set = sem("f_chain"), sem("f_out_set"), sem("f_gelu_set")
                    block = ph.enter_context(nc.Block())
                    by_block = total[:, :].rearrange("p (b f) -> p b f", f=AW)

                    @block.vector
                    def _(dve):
                        link = Chain(dve, chain)
                        link(nc.vector.tensor_scalar(den[:, :, :], by_block[:, :, D:AW], 1e-30, None, ALU.max))
                        link(nc.vector.reciprocal(den[:, :, :], den[:, :, :]))
                        values = by_block[:, :, 0:D].rearrange("p b (n d) -> p b n d", d=HD)
                        link(nc.vector.tensor_tensor(values, values, den[:, :, :].unsqueeze(3).broadcast_to([P, BLOCKS, HEADS, HD]),
                                                     ALU.mult))
                        nc.vector.tensor_tensor(skip[:, :, :], skip[:, :, :], by_block[:, :, 0:D], ALU.add).then_inc(out_set, 1)
                        dve.wait_ge(gelu_set, 1)
                        link(nc.vector.tensor_tensor(skip[:, :, :], skip[:, :, :], Z[:, :, :], ALU.add))

                    @block.scalar
                    def _(act):
                        act.wait_ge(out_set, 1)
                        nc.scalar.activation(skip[:, :, :], skip[:, :, :], ACT.Gelu).then_inc(gelu_set, 1)
                layer_norm("lna", Z, skip, gamma, beta, X)

        layer_norm("ln3", Z, X)

        recycle()

        FC = FH // P
        with ExitStack() as ph:
            def sb(name, shape, dt=F32):
                return ph.enter_context(nc.sbuf_tensor(name, shape, dt))

            zt_all = sb("r_zt_all", [P, KC, NODES])
            wr = sb("r_wr", [P, KC, 1])
            br = sb("r_br", [P, 1])
            w1 = sb("r_w1", [P, KC, FH])
            w2 = sb("r_w2", [P, FC, D])
            b1 = sb("r_b1", [P, FC])
            b2 = sb("r_b2", [1, D])
            weight = sb("r_weight", [P, BLOCKS])
            every = sb("r_every", [P, NODES])
            number = sb("r_number", [P, NODES])
            mine = sb("r_mine", [P, BLOCKS])
            above = sb("r_above", [P, BLOCKS])
            ties = sb("r_ties", [P, BLOCKS])
            coef = sb("r_coef", [P, BLOCKS])
            load_weights("rw", [
                matrix(wr[:, :, :], a["L1_ffn_wr"]), vector(br, a["L1_ffn_br"]), matrix(w1[:, :, :], a["L1_ffn_w1"]),
                matrix(w2[:, :, :], a["L1_ffn_w2"]),
                lambda sp, done: sp.dma_start(b1[:, :], a["L1_ffn_b1"].rearrange("(c p) -> p c", p=P),
                                              allow_slow_non_contiguous=True).then_inc(done, 16),
                lambda sp, done: sp.dma_start(b2[:, :], a["L1_ffn_b2"].rearrange("(o d) -> o d", o=1)).then_inc(done, 16)])
            project("route", Z, KC, [(wr, 1)], lambda dve, b, po, chain, at: nc.vector.tensor_tensor(
                weight[:, bass.ds(b, 1)], po[:, 0:1], br[:, :], ALU.add), 0, save_t=zt_all)

            with ExitStack() as ph2:
                pw = ph2.enter_context(nc.psum_tensor("r_pw", [BLOCKS, P], F32))
                wt = ph2.enter_context(nc.sbuf_tensor("r_wt", [BLOCKS, P], F32))
                w_turned, wt_set, w_out, every_in, every_set, number_set = (
                    sem("w_turned"), sem("wt_set"), sem("w_out"), sem("every_in"), sem("every_set"), sem("number_set"))
                block = ph2.enter_context(nc.Block())

                @block.tensor
                def _(pe):
                    nc.tensor.transpose(pw[:, :], weight[:, :], ident[:, :]).then_inc(w_turned, 1)

                @block.scalar
                def _(act):
                    act.wait_ge(w_turned, 1)
                    nc.scalar.activation(wt[:, :], pw[:, :], ACT.Copy).then_inc(wt_set, 1)

                @block.sync
                def _(sp):
                    sp.wait_ge(wt_set, 1)
                    sp.dma_start(w_d[:, :], wt[:, :]).then_inc(w_out, 16)
                    sp.wait_ge(w_out, 16)
                    sp.dma_start(every[:, :], w_d.rearrange("(o b) p -> o (b p)", o=1).broadcast_to([P, NODES]))\
                        .then_inc(every_in, 16)

                @block.gpsimd
                def _(pool):
                    pool.iota(number[:, :], pattern=[[1, NODES]], base=0, channel_multiplier=0,
                              allow_small_or_imprecise_dtypes=True).then_inc(number_set, 1)
                    pool.iota(mine[:, :], pattern=[[P, BLOCKS]], base=0, channel_multiplier=1,
                              allow_small_or_imprecise_dtypes=True).then_inc(number_set, 1)

                @block.vector
                def _(dve):
                    dve.wait_ge(every_in, 16)
                    nc.vector.memset(every[:, N:NODES], -3.0e38).then_inc(every_set, 1)
                    dve.wait_ge(every_set, 1)
                    dve.wait_ge(number_set, 2)

            with ExitStack() as ph2:
                ht = ph2.enter_context(nc.sbuf_tensor("r_ht", [P, FC, 2 * P], F32))
                cmp = [ph2.enter_context(nc.sbuf_tensor(f"r_cmp{i}", [P, NODES], F32)) for i in range(2)]
                ps_h = [ph2.enter_context(nc.psum_tensor(f"r_ps_h{c}", [P, 512], F32)) for c in range(4)]
                ps_y = [ph2.enter_context(nc.psum_tensor(f"r_ps_y{k}", [P, 512], F32)) for k in range(2)]
                h_set, h_gelu, y_set, y_taken, chain, x_out = (
                    sem("r_h_set"), sem("r_h_gelu"), sem("r_y_set"), sem("r_y_taken"), sem("r_chain"), sem("x_out"))
                block = ph2.enter_context(nc.Block())

                @block.tensor
                def _(pe):
                    def step(n):
                        for h in range(FC):
                            wait_count(pe, h_gelu, FC * n + h - 3)
                            for c in range(KC):
                                last = nc.tensor.matmul(ps_h[h % 4][:, 0:2 * P], w1[:, c, h * P:(h + 1) * P],
                                                        zt_all[:, c, bass.ds(n * 2 * P, 2 * P)],
                                                        start=(c == 0), stop=(c == KC - 1))
                            last.then_inc(h_set, 1)
                        for m in range(2):
                            wait_count(pe, y_taken, 2 * n + m - 1)
                            for h in range(FC):
                                pe.wait_ge(h_gelu, FC * n + h + 1)
                                nc.tensor.matmul(ps_y[m][:, 0:D], ht[:, h, m * P:(m + 1) * P], w2[:, h, :],
                                                 start=(h == 0), stop=False)
                            nc.tensor.matmul(ps_y[m][:, 0:D], ones[0:1, :], b2[:, :], start=False, stop=True).then_inc(y_set, 1)
                    step(0)
                    with pe.Fori(1, PAIRS) as n:
                        step(n)

                @block.scalar
                def _(act):
                    def step(n):
                        wait_count(act, y_set, 2 * n)
                        for h in range(FC):
                            act.wait_ge(h_set, FC * n + h + 1)
                            nc.scalar.activation(ht[:, h, :], ps_h[h % 4][:, 0:2 * P], ACT.Gelu_apprx_tanh,
                                                 bias=b1[:, h:h + 1]).then_inc(h_gelu, 1)
                    step(0)
                    with act.Fori(1, PAIRS) as n:
                        step(n)

                @block.vector
                def _(dve):
                    STEP = 9

                    with dve.Fori(0, PAIRS) as n:
                        for m in range(2):
                            b = 2 * n + m
                            one = bass.ds(b, 1)
                            made = [0]

                            def link(ins):
                                made[0] += 1
                                ins.then_inc(chain, 1)
                                dve.wait_ge(chain, STEP * b + made[0])

                            link(nc.vector.tensor_scalar(cmp[0][:, :], every[:, :], weight[:, one], None, ALU.is_gt))
                            link(nc.vector.tensor_reduce(above[:, one], cmp[0][:, :], AX.X, ALU.add))
                            link(nc.vector.tensor_scalar(cmp[1][:, :], every[:, :], weight[:, one], None, ALU.is_equal))
                            link(nc.vector.scalar_tensor_tensor(out=cmp[1][:, :], in0=number[:, :], scalar=mine[:, one],
                                                                in1=cmp[1][:, :], op0=ALU.is_lt, op1=ALU.mult))
                            link(nc.vector.tensor_reduce(ties[:, one], cmp[1][:, :], AX.X, ALU.add))
                            link(nc.vector.tensor_tensor(above[:, one], above[:, one], ties[:, one], ALU.add))
                            link(nc.vector.scalar_tensor_tensor(out=coef[:, one], in0=above[:, one], scalar=float(KEEP),
                                                                in1=weight[:, one], op0=ALU.is_lt, op1=ALU.mult))
                            link(nc.vector.tensor_tensor(X[:, one, :], X[:, one, :], Z[:, one, :], ALU.add))
                            dve.wait_ge(y_set, b + 1)
                            link(nc.vector.scalar_tensor_tensor(out=X[:, one, :], in0=ps_y[m][:, 0:D].unsqueeze(1),
                                                                scalar=coef[:, one], in1=X[:, one, :],
                                                                op0=ALU.mult, op1=ALU.add))
                            nc.vector.sem_inc(y_taken, 1)

                @block.sync
                def _(sp):
                    sp.wait_ge(y_taken, BLOCKS)
                    sp.dma_start(out[0:FULL * P, :].rearrange("(b p) f -> p b f", p=P), X[:, 0:FULL, :]).then_inc(x_out, 16)
                    sp.dma_start(out[FULL * P:N, :], X[0:TAIL, FULL, :]).then_inc(x_out, 16)
                    sp.wait_ge(x_out, 32)


_INS = ["x", "src", "dst", "L0_gnn_W1", "L0_gnn_b1", "L0_gnn_W2", "L0_gnn_b2", "L0_ffn_Wg", "L0_ffn_bg", "L0_ffn_bias",
        "L0_ffn_W1", "L0_ffn_b1", "L0_ffn_W2", "L0_ffn_b2", "L1_gnn_Wq", "L1_gnn_bq", "L1_gnn_Wk", "L1_gnn_bk",
        "L1_gnn_Wv", "L1_gnn_bv", "L1_gnn_Wskip", "L1_gnn_bskip", "L1_gnn_gamma", "L1_gnn_beta",
        "L1_ffn_wr", "L1_ffn_br", "L1_ffn_w1", "L1_ffn_b1", "L1_ffn_w2", "L1_ffn_b2"]


def kernel(**inputs):
    import numpy as _np
    import concourse.bacc as _bacc
    from concourse.bass_utils import run_bass_kernel_spmd as _run

    nc = _bacc.Bacc("TRN2", target_bir_lowering=False, num_devices=1)
    arrays, args = {}, {}
    for name in _INS:
        a = _np.ascontiguousarray(inputs[name])
        arrays[f"in_{name}"] = a
        args[name] = nc.dram_tensor(f"in_{name}", a.shape, mybir.dt.from_np(a.dtype), kind="ExternalInput").ap()
    out = nc.dram_tensor("out_x", inputs["x"].shape, F32, kind="ExternalOutput").ap()
    gnn_program(nc, args, out)
    r = _run(nc, [arrays], core_ids=[0])
    return r.results[0]["out_x"]
```

```python
from contextlib import ExitStack

import concourse.bass as bass
from concourse import mybir

P = 128
F32 = mybir.dt.float32
I32 = mybir.dt.int32
ALU = mybir.AluOpType
ACT = mybir.ActivationFunctionType
AX = mybir.AxisListType
PE_ONLY = (mybir.EngineType.PE,)
DVE_ONLY = (mybir.EngineType.DVE,)

U = 8
HALF = U // 2
BIG = 1.0e30
EPS = 1e-5


class Chain:

    def __init__(self, eng, sem):
        self.eng, self.sem, self.n = eng, sem, 0

    def __call__(self, ins):
        self.n += 1
        ins.then_inc(self.sem, 1)
        self.eng.wait_ge(self.sem, self.n)


def wait_count(eng, sem, value):
    if isinstance(value, int) and value <= 0:
        return
    eng.wait_ge(sem, value)


def gnn_program(nc, a, out):
    N, D = a["x"].shape
    E = a["src"].shape[0]
    HID = a["L0_gnn_W1"].shape[1]
    EXP, _, EH = a["L0_ffn_W1"].shape
    FH = a["L1_ffn_w1"].shape[1]
    HEADS = 8
    HD = D // HEADS
    KC = D // P
    KEEP = max(1, int(0.5 * N)) - 1
    FULL = N // P
    TAIL = N - FULL * P
    BLOCKS = FULL + 1 + (FULL + 1) % 2
    PAIRS = BLOCKS // 2
    NODES = BLOCKS * P
    TILES = -(-E // P)
    ETAIL = E - (TILES - 1) * P
    SLOTS = -(-(TILES + FULL) // 16) * 16
    STEPS = SLOTS // U
    RUNS = 4
    RP = SLOTS // RUNS
    CH = P // HEADS
    CS = SLOTS // CH
    SEQ = CS * P
    FAR = 1 << 14
    AW = D + HEADS
    assert SLOTS % (2 * U) == 0 and RP <= P and KC == 2 and HID == P and FULL < BLOCKS

    with ExitStack() as top:
        x_in = top.enter_context(nc.semaphore("x_in"))
        gnn_in = top.enter_context(nc.semaphore("gnn_in"))
        attn_in = top.enter_context(nc.semaphore("attn_in"))
        moe_in = top.enter_context(nc.semaphore("moe_in"))
        route_in = top.enter_context(nc.semaphore("route_in"))
        in_use = []

        def sem(name):
            in_use.append(nc.alloc_semaphore(name=name))
            return in_use[-1]

        def recycle():
            nc.all_engine_barrier()
            nc.clear_and_free_semaphores(in_use)
            nc.all_engine_barrier()
            in_use.clear()

        def keep(name, shape, dt=F32):
            return top.enter_context(nc.sbuf_tensor(name, shape, dt))

        src_d = nc.dram_tensor("src_d", [TILES, P], I32, kind="Internal").ap()
        dst_d = nc.dram_tensor("dst_d", [TILES, P], I32, kind="Internal").ap()
        key_d = nc.dram_tensor("key_d", [SLOTS, P], F32, kind="Internal").ap()
        blk_d = nc.dram_tensor("blk_d", [3, SLOTS], I32, kind="Internal").ap()
        g1_d = nc.dram_tensor("g1_d", [NODES, HID], F32, kind="Internal").ap()
        g2_d = nc.dram_tensor("g2_d", [NODES, HID], F32, kind="Internal").ap()
        k_d = nc.dram_tensor("k_d", [NODES, D], F32, kind="Internal").ap()
        v_d = nc.dram_tensor("v_d", [NODES, D], F32, kind="Internal").ap()
        w_d = nc.dram_tensor("w_d", [BLOCKS, P], F32, kind="Internal").ap()

        ident = keep("ident", [P, P])
        ones = keep("ones", [P, P])
        lane = keep("lane", [P, P])
        before = keep("before", [P, P])
        number = keep("number", [P, BLOCKS])
        real = keep("real", [P, BLOCKS])
        X = keep("X", [P, BLOCKS, D])
        Z = keep("Z", [P, BLOCKS, D])
        src_i = keep("src_i", [P, SLOTS], I32)
        dl = keep("dl", [P, SLOTS])
        blk1 = keep("blk1", [1, SLOTS], I32)
        blk2 = keep("blk2", [1, SLOTS], I32)
        blk3 = keep("blk3", [1, SLOTS], I32)
        dinv = keep("dinv", [P, BLOCKS])
        stat = keep("stat", [P, BLOCKS])
        halves = keep("halves", [P, BLOCKS, 6])
        scale = keep("scale", [P, BLOCKS])
        shift = keep("shift", [P, BLOCKS])
        gw1 = keep("gw1", [P, KC, HID])
        gb1 = keep("gb1", [P, HID])
        gw2 = keep("gw2", [P, 1, D])
        gb2 = keep("gb2", [P, D])
        attn = ("q", "k", "v", "skip")
        aw = [keep(f"aw_{m}", [P, KC, D]) for m in attn]
        ab = [keep(f"ab_{m}", [P, D]) for m in attn]

        def rows(t, blocks=BLOCKS):
            return t.rearrange("(b p) f -> p b f", p=P)[:, 0:blocks, :]

        def load_broadcast(eng, tile, vector, done):
            eng.dma_start(tile, vector.rearrange("(o f) -> o f", o=1).broadcast_to([P, vector.shape[0]])).then_inc(done, 16)

        with ExitStack() as ph:
            def sb(name, shape, dt=F32):
                return ph.enter_context(nc.sbuf_tensor(name, shape, dt))

            pb = [ph.enter_context(nc.psum_tensor(f"t_ps{i}", [P, 512], F32)) for i in range(3)]
            last_i = sb("last_i", [1, TILES - 1], I32)
            last_b = sb("last_b", [1, TILES - 1], I32)
            last_f = sb("last_f", [1, TILES - 1])
            tile_no = sb("tile_no", [1, TILES - 1])
            slot_no = sb("slot_no", [P, RUNS])
            less = sb("less", [P, TILES - 1])
            t_f = sb("t_f", [P, RUNS])
            t_i = sb("t_i", [P, RUNS], I32)
            b_f = sb("b_f", [P, RUNS])
            b_m = sb("b_m", [P, RUNS])
            b_i = sb("b_i", [P, 3, RUNS], I32)
            pad = sb("pad", [1, 2, P], I32)
            ed = sb("ed", [P, RUNS, P], I32)
            es = sb("es", [P, RUNS, P], I32)
            edf = sb("edf", [P, RUNS, P])
            esf = sb("esf", [P, RUNS, P])
            edl = sb("edl", [P, RUNS, P])
            inside = sb("inside", [P, RUNS, P])
            key = sb("key", [P, RUNS, P])
            last_in, pad_set, edges_out = sem("last_in"), sem("pad_set"), sem("edges_out")
            const_set, id_zero, x_zero = sem("const_set"), sem("id_zero"), sem("x_zero")
            t_chain, last_set, spread, t_set, tiles_in = (
                sem("t_chain"), sem("last_set"), sem("spread"), sem("t_set"), sem("tiles_in"))
            b_set, key_set, tables_out, turned, tables_in, copied = (
                sem("b_set"), sem("key_set"), sem("tables_out"), sem("turned"), sem("tables_in"), sem("copied"))
            block = ph.enter_context(nc.Block())

            @block.sync
            def _(sp):
                sp.dma_start(last_i[:, :], a["dst"][0:(TILES - 1) * P].rearrange("(t e) -> e t", e=P)[P - 1:P, :],
                             allow_slow_non_contiguous=True).then_inc(last_in, 16)
                for t, d in (("src", src_d), ("dst", dst_d)):
                    sp.dma_start(d[0:TILES - 1, :], a[t][0:(TILES - 1) * P].rearrange("(t e) -> t e", e=P))\
                        .then_inc(edges_out, 16)
                    sp.dma_start(d[TILES - 1:TILES, 0:ETAIL], a[t][(TILES - 1) * P:E].rearrange("(o e) -> o e", o=1))\
                        .then_inc(edges_out, 16)
                sp.wait_ge(pad_set, 2)
                if ETAIL < P:
                    sp.dma_start(src_d[TILES - 1:TILES, ETAIL:P], pad[:, 0, ETAIL:P]).then_inc(edges_out, 16)
                    sp.dma_start(dst_d[TILES - 1:TILES, ETAIL:P], pad[:, 1, ETAIL:P]).then_inc(edges_out, 16)
                sp.wait_ge(b_set, 3)
                for m in range(3):
                    sp.dma_start(blk_d[m, :].rearrange("(r p) -> p r", p=RP), b_i[0:RP, m, :],
                                 allow_slow_non_contiguous=True).then_inc(tables_out, 16)
                sp.wait_ge(key_set, 1)
                sp.dma_start(key_d.rearrange("(r p) e -> p r e", p=RP), key[0:RP, :, :]).then_inc(tables_out, 16)
                sp.wait_ge(tables_out, 64)
                for m, t in enumerate((blk1, blk2, blk3)):
                    sp.dma_start(t[:, :], blk_d[m:m + 1, :]).then_inc(tables_in, 16)
                sp.wait_ge(tables_in, 48)
                sp.wait_ge(edges_out, 96 if ETAIL < P else 64)

            @block.scalar
            def _(act):
                act.wait_ge(x_zero, 1)
                act.dma_start(X[:, 0:FULL, :], a["x"][0:FULL * P, :].rearrange("(b p) f -> p b f", p=P)).then_inc(x_in, 16)
                act.dma_start(X[0:TAIL, FULL, :], a["x"][FULL * P:N, :]).then_inc(x_in, 16)
                act.dma_start(gw1[:, :, :], a["L0_gnn_W1"].rearrange("(c p) f -> p c f", p=P)).then_inc(gnn_in, 16)
                act.dma_start(gw2[:, :, :], a["L0_gnn_W2"].rearrange("(c p) f -> p c f", p=P)).then_inc(gnn_in, 16)
                load_broadcast(act, gb1[:, :], a["L0_gnn_b1"], gnn_in)
                load_broadcast(act, gb2[:, :], a["L0_gnn_b2"], gnn_in)
                for m, name in enumerate(attn):
                    act.dma_start(aw[m][:, :, :], a["L1_gnn_W" + name].rearrange("(c p) f -> p c f", p=P)).then_inc(attn_in, 16)
                    load_broadcast(act, ab[m][:, :], a["L1_gnn_b" + name], attn_in)
                act.wait_ge(turned, 2 * RUNS)
                nc.scalar.activation(dl[:, :], pb[1][:, 0:SLOTS], ACT.Copy).then_inc(copied, 1)
                nc.scalar.activation(src_i[:, :], pb[2][:, 0:SLOTS], ACT.Copy).then_inc(copied, 1)
                act.wait_ge(copied, 2)
                act.wait_ge(x_in, 32)
                act.wait_ge(gnn_in, 64)

            @block.gpsimd
            def _(pool):
                pool.memset(pad[:, 0, :], 0).then_inc(pad_set, 1)
                pool.memset(pad[:, 1, :], FAR).then_inc(pad_set, 1)
                pool.memset(X[:, FULL:BLOCKS, :], 0.0).then_inc(x_zero, 1)
                pool.memset(ones[:, :], 1.0).then_inc(const_set, 1)
                pool.iota(tile_no[:, :], pattern=[[1, TILES - 1]], base=0, channel_multiplier=0,
                          allow_small_or_imprecise_dtypes=True).then_inc(const_set, 1)
                pool.iota(slot_no[:, :], pattern=[[RP, RUNS]], base=0, channel_multiplier=1,
                          allow_small_or_imprecise_dtypes=True).then_inc(const_set, 1)
                pool.iota(lane[:, :], pattern=[[1, P]], base=0, channel_multiplier=0,
                          allow_small_or_imprecise_dtypes=True).then_inc(const_set, 1)
                pool.iota(number[:, :], pattern=[[P, BLOCKS]], base=0, channel_multiplier=1,
                          allow_small_or_imprecise_dtypes=True).then_inc(const_set, 1)
                pool.memset(before[:, :], 1.0).then_inc(id_zero, 1)
                pool.memset(ident[:, :], 0.0).then_inc(id_zero, 1)
                pool.wait_ge(id_zero, 2)
                pool.affine_select(out=before[:, :], in_=before[:, :], compare_op=ALU.is_gt, fill=0.0,
                                   base=0, pattern=[[1, P]], channel_multiplier=-1).then_inc(const_set, 1)
                pool.affine_select(out=ident[:, :], in_=ident[:, :], compare_op=ALU.not_equal, fill=1.0,
                                   base=0, pattern=[[-1, P]], channel_multiplier=1).then_inc(const_set, 1)
                pool.wait_ge(edges_out, 96 if ETAIL < P else 64)
                pool.wait_ge(t_set, 1)
                for r in range(RUNS):
                    at = bass.IndirectOffsetOnAxis(ap=t_i[0:RP, r:r + 1], axis=0)
                    pool.indirect_dma_start(ed[0:RP, r, :], None, dst_d[:, :], at).then_inc(tiles_in, 16)
                    pool.indirect_dma_start(es[0:RP, r, :], None, src_d[:, :], at).then_inc(tiles_in, 16)

            @block.vector
            def _(dve):
                link = Chain(dve, t_chain)
                dve.wait_ge(last_in, 16)
                link(nc.vector.tensor_scalar(last_b[:, :], last_i[:, :], 7, None, ALU.arith_shift_right))
                link(nc.vector.tensor_copy(last_f[:, :], last_b[:, :]))
                dve.wait_ge(const_set, 7)
                link(nc.vector.tensor_scalar(real[:, :], number[:, :], float(N), None, ALU.is_lt))
                nc.vector.tensor_tensor(last_f[:, :], last_f[:, :], tile_no[:, :], ALU.add).then_inc(last_set, 1)
                dve.wait_ge(spread, 1)
                for r in range(RUNS):
                    link(nc.vector.tensor_scalar(less[0:RP, :], pb[0][0:RP, 0:TILES - 1], slot_no[0:RP, r:r + 1], None,
                                                 ALU.is_lt))
                    link(nc.vector.tensor_reduce(t_f[0:RP, r:r + 1], less[0:RP, :], AX.X, ALU.add))
                nc.vector.tensor_copy(t_i[0:RP, :], t_f[0:RP, :]).then_inc(t_set, 1)
                link(nc.vector.tensor_tensor(b_f[0:RP, :], slot_no[0:RP, :], t_f[0:RP, :], ALU.subtract))
                for m, width in enumerate((P, D, AW)):
                    nc.vector.tensor_scalar(b_i[0:RP, m, :], b_f[0:RP, :], float(width), None, ALU.mult).then_inc(b_set, 1)
                link(nc.vector.tensor_scalar(b_m[0:RP, :], b_f[0:RP, :], -float(P), None, ALU.mult))
                dve.wait_ge(tiles_in, 2 * RUNS * 16)
                link(nc.vector.tensor_copy(edf[0:RP, :, :], ed[0:RP, :, :]))
                link(nc.vector.tensor_copy(esf[0:RP, :, :], es[0:RP, :, :]))
                link(nc.vector.tensor_tensor(edl[0:RP, :, :], edf[0:RP, :, :],
                                             b_m[0:RP, :].unsqueeze(2).broadcast_to([RP, RUNS, P]), ALU.add))
                link(nc.vector.tensor_scalar(inside[0:RP, :, :], edl[0:RP, :, :], 0.0, None, ALU.is_ge))
                link(nc.vector.scalar_tensor_tensor(out=inside[0:RP, :, :], in0=edl[0:RP, :, :], scalar=float(P),
                                                    in1=inside[0:RP, :, :], op0=ALU.is_lt, op1=ALU.mult))
                nc.vector.scalar_tensor_tensor(out=key[0:RP, :, :], in0=edf[0:RP, :, :], scalar=1.0,
                                               in1=inside[0:RP, :, :], op0=ALU.add, op1=ALU.mult).then_inc(key_set, 1)

            @block.tensor
            def _(pe):
                pe.wait_ge(last_set, 1)
                nc.tensor.matmul(pb[0][:, 0:TILES - 1], ones[0:1, :], last_f[:, :], start=True, stop=True).then_inc(spread, 1)
                pe.wait_ge(key_set, 1)
                for m, t in ((1, edl), (2, esf)):
                    for r in range(RUNS):
                        nc.tensor.transpose(pb[m][:, r * RP:(r + 1) * RP], t[0:RP, r, :], ident[0:RP, 0:RP])\
                            .then_inc(turned, 1)

        def norm_stats(phase, in_t):
            with ExitStack() as ph:
                chain, var_set, root_set = sem(f"{phase}_chain"), sem(f"{phase}_var"), sem(f"{phase}_root")
                counted = sem(f"{phase}_counted")
                block = ph.enter_context(nc.Block())

                @block.vector
                def _(dve):
                    link = Chain(dve, chain)
                    with dve.Fori(0, PAIRS) as i:
                        for k in range(2):
                            nc.vector.bn_stats(halves[:, bass.ds(2 * i + k, 1), :].rearrange("p o f -> p (o f)"),
                                               in_t[:, bass.ds(2 * i + k, 1), :].rearrange("p o f -> p (o f)"))\
                                .then_inc(counted, 1)
                    dve.wait_ge(counted, BLOCKS)
                    even, odd = halves[:, :, 1], halves[:, :, 4]
                    link(nc.vector.tensor_tensor(shift[:, :], even, odd, ALU.add))
                    link(nc.vector.tensor_tensor(scale[:, :], even, odd, ALU.subtract))
                    link(nc.vector.tensor_tensor(scale[:, :], scale[:, :], scale[:, :], ALU.mult))
                    link(nc.vector.tensor_tensor(stat[:, :], halves[:, :, 2], halves[:, :, 5], ALU.add))
                    link(nc.vector.tensor_scalar(stat[:, :], stat[:, :], 1.0 / D, EPS, ALU.mult, ALU.add))
                    nc.vector.scalar_tensor_tensor(out=stat[:, :], in0=scale[:, :], scalar=0.25, in1=stat[:, :],
                                                   op0=ALU.mult, op1=ALU.add).then_inc(var_set, 1)
                    dve.wait_ge(root_set, 1)
                    link(nc.vector.reciprocal(scale[:, :], stat[:, :]))
                    link(nc.vector.scalar_tensor_tensor(out=shift[:, :], in0=shift[:, :], scalar=-0.5, in1=scale[:, :],
                                                        op0=ALU.mult, op1=ALU.mult))

                @block.scalar
                def _(act):
                    act.wait_ge(var_set, 1)
                    nc.scalar.activation(stat[:, :], stat[:, :], ACT.Sqrt).then_inc(root_set, 1)

        with ExitStack() as ph:
            oh = ph.enter_context(nc.sbuf_tensor("deg_oh", [P, U, P], F32))
            ps = ph.enter_context(nc.psum_tensor("deg_ps", [P, BLOCKS], F32))
            oh_ready, counted, deg_root, deg_sqrt = sem("deg_oh_ready"), sem("deg_counted"), sem("deg_root"), sem("deg_sqrt")
            deg_done = sem("deg_done")
            block = ph.enter_context(nc.Block())

            @block.vector
            def _(dve):
                def step(it):
                    for h in range(2):
                        wait_count(dve, counted, U * it + HALF * (h + 1) - U)
                        nc.vector.tensor_tensor(
                            oh[:, HALF * h:HALF * (h + 1), :], lane[:, :].unsqueeze(1).broadcast_to([P, HALF, P]),
                            dl[:, bass.ds(U * it + HALF * h, HALF)].unsqueeze(2).broadcast_to([P, HALF, P]),
                            ALU.is_equal).then_inc(oh_ready, 1)
                step(0)
                with dve.Fori(1, STEPS) as it:
                    step(it)
                dve.wait_ge(deg_root, 1)
                nc.vector.reciprocal(dinv[:, :], stat[:, :]).then_inc(deg_done, 1)
                dve.wait_ge(deg_done, 1)

            @block.tensor
            def _(pe):
                nc.tensor.matmul(ps[:, :], ident[:, :], ones[:, 0:BLOCKS], start=True, stop=False, skip_group_check=True)

                def step(it):
                    _, at = nc.values_load_multi_w_load_instructions(
                        blk1[0:1, bass.ds(U * it, U)], engines=PE_ONLY, min_val=0, max_val=(BLOCKS - 1) * P,
                        skip_runtime_bounds_check_because="a slot's block is below BLOCKS")
                    for k in range(U):
                        if k % HALF == 0:
                            pe.wait_ge(oh_ready, 2 * it + k // HALF + 1)
                        nc.tensor.matmul(ps[:, bass.ds(at[k] // P, 1)], oh[:, k, :], ones[:, 0:1],
                                         start=False, stop=False, skip_group_check=True).then_inc(counted, 1)
                step(0)
                with pe.Fori(1, STEPS) as it:
                    step(it)

            @block.scalar
            def _(act):
                act.wait_ge(counted, SLOTS)
                nc.scalar.activation(stat[:, :], ps[:, :], ACT.Sqrt).then_inc(deg_root, 1)

        recycle()

        norm_stats("ln0", X)

        def project(phase, in_t, kc, weights, evacuate, parts, norm_of=None, save_t=None):
            with ExitStack() as ph:
                stage = ph.enter_context(nc.sbuf_tensor(f"{phase}_stage", [P, 2, kc, P], F32))
                zt = ph.enter_context(nc.sbuf_tensor(f"{phase}_zt", [P, 2, kc, P], F32))
                pt = [ph.enter_context(nc.psum_tensor(f"{phase}_pt{k}", [P, kc, P], F32)) for k in range(2)]
                width = sum(w for _, w in weights)
                banks = -(-width // 512)
                po = [ph.enter_context(nc.psum_tensor(f"{phase}_po{k}", [P, banks * 512], F32)) for k in range(2)]
                staged, turned_, zt_set, product, taken = (
                    sem(f"{phase}_staged"), sem(f"{phase}_turned"), sem(f"{phase}_zt"), sem(f"{phase}_product"),
                    sem(f"{phase}_taken"))
                chain, normed, may_stage = sem(f"{phase}_chain"), sem(f"{phase}_normed"), sem(f"{phase}_may_stage")
                block = ph.enter_context(nc.Block())

                @block.gpsimd
                def _(pool):
                    def step(i):
                        for k in range(2):
                            b = 2 * i + k
                            if norm_of is not None:
                                pool.wait_ge(normed, b + 1)
                                pool.sem_inc(may_stage, 1)
                            wait_count(pool, turned_, b - 1)
                            pool.sem_inc(may_stage, 1)
                            nc.gpsimd.tensor_copy(stage[:, k, :, :],
                                                  in_t[:, bass.ds(b, 1), :].rearrange("p o (c f) -> p (o c) f", c=kc))\
                                .then_inc(staged, 1)
                    step(0)
                    with pool.Fori(1, PAIRS) as i:
                        step(i)

                @block.tensor
                def _(pe):
                    def turn(b, k):
                        pe.wait_ge(staged, b + 1)
                        wait_count(pe, zt_set, b - 1)
                        for c in range(kc):
                            last = nc.tensor.transpose(pt[k][:, c, :], stage[:, k, c, :], ident[:, :])
                        last.then_inc(turned_, 1)

                    def multiply(b, k):
                        pe.wait_ge(zt_set, b + 1)
                        wait_count(pe, taken, b - 1)
                        at = 0
                        for w, n in weights:
                            for c in range(kc):
                                last = nc.tensor.matmul(po[k][:, at:at + n], zt[:, k, c, :], w[:, c, :],
                                                        start=(c == 0), stop=(c == kc - 1))
                            at += n
                        last.then_inc(product, 1)
                    turn(0, 0)
                    turn(1, 1)
                    multiply(0, 0)
                    with pe.Fori(1, PAIRS) as i:
                        turn(2 * i, 0)
                        multiply(2 * i - 1, 1)
                        turn(2 * i + 1, 1)
                        multiply(2 * i, 0)
                    multiply(BLOCKS - 1, 1)

                @block.scalar
                def _(act):
                    def normalise(b):
                        nc.scalar.activation(in_t[:, bass.ds(b, 1), :], norm_of[:, bass.ds(b, 1), :], ACT.Identity,
                                             scale=scale[:, bass.ds(b, 1)], bias=shift[:, bass.ds(b, 1)]).then_inc(normed, 1)

                    def step(i, more):
                        for k in range(2):
                            b = 2 * i + k
                            act.wait_ge(turned_, b + 1)
                            wait_count(act, product, b - 1)
                            nc.scalar.activation(zt[:, k, :, :], pt[k][:, :, :], ACT.Copy).then_inc(zt_set, 1)
                            if save_t is not None:
                                act.wait_ge(zt_set, b + 1)
                                nc.scalar.activation(save_t[:, :, bass.ds(b * P, P)], zt[:, k, :, :], ACT.Copy)
                            if norm_of is not None and more:
                                normalise(b + 2)
                    if norm_of is not None:
                        normalise(0)
                        normalise(1)
                    step(0, True)
                    with act.Fori(1, PAIRS - 1) as i:
                        step(i, True)
                    step(PAIRS - 1, False)

                @block.vector
                def _(dve):
                    def step(i):
                        for k in range(2):
                            b = 2 * i + k
                            dve.wait_ge(product, b + 1)
                            evacuate(dve, b, po[k], chain, parts * b).then_inc(taken, 1)
                    step(0)
                    with dve.Fori(1, PAIRS) as i:
                        step(i)

        def load_weights(phase, loads):
            with ExitStack() as ph:
                done = sem(f"{phase}_in")
                block = ph.enter_context(nc.Block())

                @block.sync
                def _(sp):
                    for f in loads:
                        f(sp, done)
                    sp.wait_ge(done, 16 * len(loads))

        def matrix(tile, w):
            return lambda sp, done: sp.dma_start(tile, w.rearrange("(c p) f -> p c f", p=P),
                                                   allow_slow_non_contiguous=w.shape[1] == 1).then_inc(done, 16)

        def vector(tile, v):
            return lambda sp, done: load_broadcast(sp, tile[:, :], v, done)

        def store_rows(phase, table, tile):
            with ExitStack() as ph:
                done = sem(f"{phase}_out")
                block = ph.enter_context(nc.Block())

                @block.sync
                def _(sp):
                    sp.dma_start(rows(table), tile[:, :, :]).then_inc(done, 16)
                    sp.wait_ge(done, 16)

        def convolve(phase, table, own, out_t):
            with ExitStack() as ph:
                oh = ph.enter_context(nc.sbuf_tensor(f"{phase}_oh", [P, U, P], F32))
                ring = ph.enter_context(nc.sbuf_tensor(f"{phase}_ring", [P, U, HID], F32))
                ix = ph.enter_context(nc.sbuf_tensor(f"{phase}_ix", [P, U], I32))
                acc = ph.enter_context(nc.psum_tensor(f"{phase}_acc", [P, 8 * 512], F32))
                landed = [sem(f"{phase}_landed{k}") for k in range(U)]
                may_gather = sem(f"{phase}_may_gather")
                oh_ready, ix_ready, summed, scaled = (
                    sem(f"{phase}_oh_ready"), sem(f"{phase}_ix_ready"), sem(f"{phase}_summed"), sem(f"{phase}_scaled"))
                block = ph.enter_context(nc.Block())

                @block.gpsimd
                def _(pool):
                    def step(it):
                        for h in range(2):
                            pool.wait_ge(ix_ready, 2 * it + h + 1)
                            pool.sem_inc(may_gather, 1)
                            for k in range(HALF * h, HALF * (h + 1)):
                                pool.indirect_dma_start(
                                    ring[:, k, :], None, table[:, :],
                                    bass.IndirectOffsetOnAxis(ap=ix[:, k:k + 1], axis=0)).then_inc(landed[k], 16)
                    with pool.Fori(0, STEPS) as it:
                        step(it)

                @block.vector
                def _(dve):
                    def step(it):
                        for h in range(2):
                            mine = slice(HALF * h, HALF * (h + 1))
                            wait_count(dve, summed, U * it + HALF * (h + 1) - U)
                            nc.vector.tensor_copy(ix[:, mine], src_i[:, bass.ds(U * it + HALF * h, HALF)]).then_inc(ix_ready, 1)
                            nc.vector.tensor_tensor(
                                oh[:, mine, :], lane[:, :].unsqueeze(1).broadcast_to([P, HALF, P]),
                                dl[:, bass.ds(U * it + HALF * h, HALF)].unsqueeze(2).broadcast_to([P, HALF, P]),
                                ALU.is_equal).then_inc(oh_ready, 1)
                    step(0)
                    with dve.Fori(1, STEPS) as it:
                        step(it)
                    dve.wait_ge(summed, SLOTS)
                    nc.vector.tensor_tensor(out_t[:, :, :],
                                            acc[:, 0:BLOCKS * HID].rearrange("p (b f) -> p b f", f=HID),
                                            dinv[:, :].unsqueeze(2).broadcast_to([P, BLOCKS, HID]), ALU.mult).then_inc(scaled, 1)
                    dve.wait_ge(scaled, 1)

                @block.tensor
                def _(pe):
                    for b in range(0, BLOCKS, 512 // HID):
                        n = min(512 // HID, BLOCKS - b)
                        nc.tensor.matmul(acc[:, b * HID:(b + n) * HID], ident[:, :], own[:, b:b + n, :],
                                         start=True, stop=False, skip_group_check=True)

                    def step(it):
                        _, at = nc.values_load_multi_w_load_instructions(
                            blk1[0:1, bass.ds(U * it, U)], engines=PE_ONLY, min_val=0, max_val=(BLOCKS - 1) * P,
                            skip_runtime_bounds_check_because="a slot's block is below BLOCKS")
                        for k in range(U):
                            if k % HALF == 0:
                                pe.wait_ge(oh_ready, 2 * it + k // HALF + 1)
                            pe.wait_ge(landed[k], 16 * it + 16)
                            nc.tensor.matmul(acc[:, bass.ds(at[k], HID)], oh[:, k, :], ring[:, k, :],
                                             start=False, stop=False, skip_group_check=True).then_inc(summed, 1)
                    step(0)
                    with pe.Fori(1, STEPS) as it:
                        step(it)

        MT = (2 * N + EXP * (P - 1)) // P
        MT += MT % 2
        HC = EH // P
        WROW = KC * EH
        GROUP = 5
        PART = KC * EH
        assert HC * D == PART and (FULL + 1) % GROUP == 0
        zs_d = nc.dram_tensor("zs_d", [(MT + 2) * P, D], F32, kind="Internal").ap()
        y_d = nc.dram_tensor("y_d", [(MT + 2) * P, D], F32, kind="Internal").ap()
        with ExitStack() as ph:
            def sb(name, shape, dt=F32):
                return ph.enter_context(nc.sbuf_tensor(name, shape, dt))

            w1 = sb("m_w1", [P, EXP * PART])
            w2 = sb("m_w2", [P, EXP * PART])
            b1 = sb("m_b1", [P, EXP * EH])
            b2 = sb("m_b2", [P, EXP * D])
            wg = sb("m_wg", [P, KC, EXP])
            bg = sb("m_bg", [P, EXP])
            bias = sb("m_bias", [P, EXP])
            zero = sb("m_zero", [P, D])
            logit = sb("m_logit", [P, BLOCKS, EXP])
            rest = sb("m_rest", [P, BLOCKS, EXP])
            order = sb("m_order", [P, BLOCKS, EXP])
            pick = [sb(f"m_pick{i}", [P, BLOCKS, EXP]) for i in range(2)]
            both = sb("m_both", [P, BLOCKS, EXP])
            top_v = [sb(f"m_top{i}", [P, BLOCKS]) for i in range(2)]
            share = [sb(f"m_share{i}", [P, BLOCKS]) for i in range(2)]
            place_i = sb("m_place_i", [P, BLOCKS, 2], I32)
            expert_of = sb("m_expert_of", [1, MT + 2], I32)

            with ExitStack() as ph2:
                zero_set, rows_zero = sem("m_zero_set"), sem("m_rows_zero")
                block = ph2.enter_context(nc.Block())

                @block.gpsimd
                def _(pool):
                    pool.memset(zero[:, :], 0.0).then_inc(zero_set, 1)

                @block.sync
                def _(sp):
                    sp.dma_start(wg[:, :, :], a["L0_ffn_Wg"].rearrange("(c p) f -> p c f", p=P)).then_inc(moe_in, 16)
                    load_broadcast(sp, bg[:, :], a["L0_ffn_bg"], moe_in)
                    load_broadcast(sp, bias[:, :], a["L0_ffn_bias"], moe_in)
                    load_broadcast(sp, b1[:, :], a["L0_ffn_b1"].rearrange("e f -> (e f)"), moe_in)
                    load_broadcast(sp, b2[:, :], a["L0_ffn_b2"].rearrange("e f -> (e f)"), moe_in)
                    for e in range(EXP):
                        sp.dma_start(w1[:, e * PART:(e + 1) * PART].rearrange("p (c f) -> p c f", c=KC),
                                     a["L0_ffn_W1"][e].rearrange("(c p) f -> p c f", p=P)).then_inc(moe_in, 16)
                        sp.dma_start(w2[:, e * PART:(e + 1) * PART].rearrange("p (c f) -> p c f", c=HC),
                                     a["L0_ffn_W2"][e].rearrange("(c p) f -> p c f", p=P)).then_inc(moe_in, 16)
                    sp.wait_ge(zero_set, 1)
                    sp.dma_start(zs_d.rearrange("(t p) f -> p t f", p=P),
                                 zero[:, :].unsqueeze(1).broadcast_to([P, MT + 2, D])).then_inc(moe_in, 16)
                    sp.dma_start(y_d[MT * P:(MT + 2) * P, :].rearrange("(t p) f -> p t f", p=P),
                                 zero[:, :].unsqueeze(1).broadcast_to([P, 2, D])).then_inc(moe_in, 16)

            with ExitStack() as ph:
                G = ph.enter_context(nc.sbuf_tensor("G", [P, BLOCKS, HID], F32))
                A = Z[:, :, 0:HID]

                project("h1", Z, KC, [(gw1, HID)], lambda dve, b, po, chain, at: nc.vector.tensor_scalar(
                    G[:, bass.ds(b, 1), :], po[:, 0:HID].unsqueeze(1), dinv[:, bass.ds(b, 1)], None, ALU.mult), 0, norm_of=X)
                store_rows("g1", g1_d, G)
                convolve("cv1", g1_d, G, A)

                with ExitStack() as ph2:
                    chain = sem("relu_chain")
                    block = ph2.enter_context(nc.Block())

                    @block.vector
                    def _(dve):
                        link = Chain(dve, chain)
                        link(nc.vector.tensor_tensor(A[:, :, :], A[:, :, :],
                                                     gb1[:, :].unsqueeze(1).broadcast_to([P, BLOCKS, HID]), ALU.add))
                        link(nc.vector.scalar_tensor_tensor(
                            out=G[:, :, :], in0=A[:, :, :], scalar=0.0,
                            in1=dinv[:, :].unsqueeze(2).broadcast_to([P, BLOCKS, HID]), op0=ALU.max, op1=ALU.mult))
                store_rows("g2", g2_d, G)
                convolve("cv2", g2_d, G, A)

                def add_conv(dve, b, po, chain, at):
                    nc.vector.tensor_tensor(X[:, bass.ds(b, 1), :], X[:, bass.ds(b, 1), :], gb2[:, :].unsqueeze(1), ALU.add)\
                        .then_inc(chain, 1)
                    dve.wait_ge(chain, at + 1)
                    return nc.vector.tensor_tensor(X[:, bass.ds(b, 1), :], X[:, bass.ds(b, 1), :], po[:, 0:D].unsqueeze(1), ALU.add)
                project("h2", A, 1, [(gw2, D)], add_conv, 1)

            norm_stats("ln1", X)
            recycle()

            with ExitStack() as ph2:
                block = ph2.enter_context(nc.Block())

                @block.sync
                def _(sp):
                    sp.wait_ge(moe_in, 16 * (7 + 2 * EXP))


            def add_bg(dve, b, po, chain, at):
                nc.vector.tensor_tensor(logit[:, bass.ds(b, 1), :], po[:, 0:EXP].unsqueeze(1), bg[:, :].unsqueeze(1), ALU.add)\
                    .then_inc(chain, 1)
                dve.wait_ge(chain, at + 1)
                return nc.vector.tensor_tensor(logit[:, bass.ds(b, 1), :], logit[:, bass.ds(b, 1), :],
                                               bias[:, :].unsqueeze(1), ALU.add)
            project("gate", Z, KC, [(wg, EXP)], add_bg, 1, norm_of=X)

            with ExitStack() as ph2:
                def sb2(name, shape, dt=F32):
                    return ph2.enter_context(nc.sbuf_tensor(name, shape, dt))

                first = sb2("m_first", [P, BLOCKS])
                gap = sb2("m_gap", [P, BLOCKS])
                counts = sb2("m_counts", [P, EXP, BLOCKS])
                until = sb2("m_until", [P, EXP, BLOCKS])
                resets = sb2("m_resets", [P, EXP, BLOCKS])
                pairs_i = sb2("m_pairs_i", [P, EXP], I32)
                tiles_f = sb2("m_tiles_f", [P, EXP])
                tiles_to = sb2("m_tiles_to", [P, EXP])
                start = sb2("m_start", [P, EXP])
                place = sb2("m_place", [P, BLOCKS, EXP])
                mine = sb2("m_mine", [P, BLOCKS, EXP])
                place_f = sb2("m_place_f", [P, BLOCKS, 2])
                spare = sb2("m_spare", [P, BLOCKS, 2])
                tile_of = sb2("m_tile_of", [P, MT + 2, EXP])
                passed = sb2("m_passed", [1, MT + 2])
                pr = ph2.enter_context(nc.psum_tensor("m_pr", [P, BLOCKS, EXP], F32))
                pc = ph2.enter_context(nc.psum_tensor("m_pc", [P, BLOCKS, EXP], F32))
                chain, gap_set, gap_exp, order_set, both_set, rank_set = (
                    sem("pick_chain"), sem("gap_set"), sem("gap_exp"), sem("order_set"), sem("both_set"), sem("rank_set"))
                block = ph2.enter_context(nc.Block())

                @block.gpsimd
                def _(pool):
                    pool.iota(order[:, :, :], pattern=[[0, BLOCKS], [1, EXP]], base=0, channel_multiplier=0,
                              allow_small_or_imprecise_dtypes=True).then_inc(order_set, 1)
                    pool.iota(spare[:, :, :], pattern=[[0, BLOCKS], [P, 2]], base=MT * P, channel_multiplier=1,
                              allow_small_or_imprecise_dtypes=True).then_inc(order_set, 1)
                    pool.iota(tile_of[:, :, :], pattern=[[1, MT + 2], [0, EXP]], base=0, channel_multiplier=0,
                              allow_small_or_imprecise_dtypes=True).then_inc(order_set, 1)

                @block.vector
                def _(dve):
                    link = Chain(dve, chain)

                    def wide(t):
                        return t[:, :].unsqueeze(2).broadcast_to([P, BLOCKS, EXP])

                    dve.wait_ge(order_set, 3)
                    left = logit
                    for i in range(2):
                        link(nc.vector.tensor_reduce(top_v[i][:, :], left[:, :, :], AX.X, ALU.max))
                        link(nc.vector.tensor_tensor(pick[i][:, :, :], left[:, :, :], wide(top_v[i]), ALU.not_equal))
                        link(nc.vector.scalar_tensor_tensor(out=pick[i][:, :, :], in0=pick[i][:, :, :], scalar=float(EXP),
                                                            in1=order[:, :, :], op0=ALU.mult, op1=ALU.add))
                        link(nc.vector.tensor_reduce(first[:, :], pick[i][:, :, :], AX.X, ALU.min))
                        link(nc.vector.tensor_tensor(pick[i][:, :, :], order[:, :, :], wide(first), ALU.is_equal))
                        if i == 0:
                            link(nc.vector.scalar_tensor_tensor(out=rest[:, :, :], in0=pick[0][:, :, :], scalar=-BIG,
                                                                in1=logit[:, :, :], op0=ALU.mult, op1=ALU.add))
                            left = rest
                    nc.vector.tensor_tensor(gap[:, :], top_v[1][:, :], top_v[0][:, :], ALU.subtract).then_inc(gap_set, 1)
                    for i in range(2):
                        link(nc.vector.tensor_tensor(pick[i][:, :, :], pick[i][:, :, :], wide(real), ALU.mult))
                    nc.vector.tensor_tensor(both[:, :, :], pick[0][:, :, :], pick[1][:, :, :], ALU.add).then_inc(both_set, 1)
                    dve.wait_ge(gap_exp, 1)
                    link(nc.vector.tensor_scalar(first[:, :], gap[:, :], 1.0, None, ALU.add))
                    link(nc.vector.reciprocal(share[0][:, :], first[:, :]))
                    link(nc.vector.tensor_tensor(share[1][:, :], gap[:, :], share[0][:, :], ALU.mult))
                    link(nc.vector.memset(resets[:, :, :], 1.0))
                    link(nc.vector.memset(resets[:, :, 0:1], 0.0))
                    dve.wait_ge(rank_set, 2)
                    link(nc.vector.tensor_copy(counts[:, :, :].rearrange("p e b -> p b e"), pc[:, :, :]))
                    link(nc.vector.tensor_tensor_scan(until[:, :, :].rearrange("p e b -> p (e b)"),
                                                      resets[:, :, :].rearrange("p e b -> p (e b)"),
                                                      counts[:, :, :].rearrange("p e b -> p (e b)"), 0.0, ALU.mult, ALU.add))
                    link(nc.vector.tensor_scalar(pairs_i[:, :], until[:, :, BLOCKS - 1], float(P - 1), None, ALU.add))
                    link(nc.vector.tensor_scalar(pairs_i[:, :], pairs_i[:, :], 7, None, ALU.arith_shift_right))
                    link(nc.vector.tensor_copy(tiles_f[:, :], pairs_i[:, :]))
                    link(nc.vector.memset(resets[:, 0, 0:EXP], 1.0))
                    link(nc.vector.tensor_tensor_scan(tiles_to[:, :], resets[:, 0, 0:EXP], tiles_f[:, :], 0.0, ALU.mult, ALU.add))
                    link(nc.vector.tensor_tensor(start[:, :], tiles_to[:, :], tiles_f[:, :], ALU.subtract))
                    link(nc.vector.tensor_scalar(start[:, :], start[:, :], float(P), None, ALU.mult))
                    link(nc.vector.tensor_tensor(until[:, :, :], until[:, :, :], counts[:, :, :], ALU.subtract))
                    link(nc.vector.tensor_tensor(place[:, :, :], until[:, :, :].rearrange("p e b -> p b e"), pr[:, :, :], ALU.add))
                    link(nc.vector.tensor_tensor(place[:, :, :], place[:, :, :],
                                                 start[:, :].unsqueeze(1).broadcast_to([P, BLOCKS, EXP]), ALU.add))
                    for i in range(2):
                        link(nc.vector.tensor_tensor(mine[:, :, :], pick[i][:, :, :], place[:, :, :], ALU.mult))
                        link(nc.vector.tensor_reduce(place_f[:, :, i:i + 1], mine[:, :, :], AX.X, ALU.add))
                    link(nc.vector.tensor_scalar(first[:, :], real[:, :], -1.0, 1.0, ALU.mult, ALU.add))
                    link(nc.vector.tensor_tensor(spare[:, :, :], spare[:, :, :],
                                                 first[:, :].unsqueeze(2).broadcast_to([P, BLOCKS, 2]), ALU.mult))
                    link(nc.vector.tensor_tensor(place_f[:, :, :], place_f[:, :, :], spare[:, :, :], ALU.add))
                    link(nc.vector.tensor_copy(place_i[:, :, :], place_f[:, :, :]))
                    link(nc.vector.tensor_tensor(tile_of[:, :, :], tile_of[:, :, :],
                                                 tiles_to[:, :].unsqueeze(1).broadcast_to([P, MT + 2, EXP]), ALU.is_ge))
                    link(nc.vector.tensor_reduce(passed[:, :], tile_of[0:1, :, :], AX.X, ALU.add))
                    link(nc.vector.tensor_scalar(expert_of[:, :], passed[:, :], float(EXP - 1), float(PART), ALU.min, ALU.mult))

                @block.scalar
                def _(act):
                    act.wait_ge(gap_set, 1)
                    nc.scalar.activation(gap[:, :], gap[:, :], ACT.Exp).then_inc(gap_exp, 1)

                @block.tensor
                def _(pe):
                    pe.wait_ge(both_set, 1)
                    nc.tensor.matmul(pr[:, :, :], before[:, :], both[:, :, :], start=True, stop=True).then_inc(rank_set, 1)
                    nc.tensor.matmul(pc[:, :, :], ones[:, :], both[:, :, :], start=True, stop=True).then_inc(rank_set, 1)

            with ExitStack() as ph2:
                stage = ph2.enter_context(nc.sbuf_tensor("o_stage", [P, GROUP, D], F32))
                ix = ph2.enter_context(nc.sbuf_tensor("o_ix", [P, GROUP, 2], I32))
                sent = [sem(f"o_sent{k}") for k in range(GROUP)]
                staged, may_send = sem("o_staged"), sem("o_may_send")
                block = ph2.enter_context(nc.Block())

                @block.scalar
                def _(act):
                    def step(i):
                        for k in range(GROUP):
                            b = GROUP * i + k
                            wait_count(act, sent[k], 32 * i)
                            nc.scalar.activation(ix[:, k:k + 1, :], place_i[:, bass.ds(b, 1), :], ACT.Copy)
                            nc.scalar.activation(stage[:, k:k + 1, :], Z[:, bass.ds(b, 1), :], ACT.Copy).then_inc(staged, 1)
                    step(0)
                    with act.Fori(1, (FULL + 1) // GROUP) as i:
                        step(i)

                @block.gpsimd
                def _(pool):
                    with pool.Fori(0, (FULL + 1) // GROUP) as i:
                        for k in range(GROUP):
                            pool.wait_ge(staged, GROUP * i + k + 1)
                            pool.sem_inc(may_send, 1)
                            for m in range(2):
                                pool.indirect_dma_start(zs_d[:, :], bass.IndirectOffsetOnAxis(ap=ix[:, k, m:m + 1], axis=0),
                                                        stage[:, k, :], None).then_inc(sent[k], 16)
                    for k in range(GROUP):
                        pool.wait_ge(sent[k], 32 * ((FULL + 1) // GROUP))

            with ExitStack() as ph2:
                zin = ph2.enter_context(nc.sbuf_tensor("m_zin", [P, 2, D], F32))
                zt = ph2.enter_context(nc.sbuf_tensor("m_zt", [P, 2, KC, P], F32))
                hid = ph2.enter_context(nc.sbuf_tensor("m_hid", [P, 2, EH], F32))
                ht = ph2.enter_context(nc.sbuf_tensor("m_ht", [P, 2, HC, P], F32))
                y = ph2.enter_context(nc.sbuf_tensor("m_y", [P, 2, D], F32))
                pz = [ph2.enter_context(nc.psum_tensor(f"m_pz{k}", [P, KC, P], F32)) for k in range(2)]
                phid = [ph2.enter_context(nc.psum_tensor(f"m_ph{k}", [P, EH], F32)) for k in range(2)]
                pht = [ph2.enter_context(nc.psum_tensor(f"m_pht{k}", [P, HC, P], F32)) for k in range(2)]
                py = [ph2.enter_context(nc.psum_tensor(f"m_py{k}", [P, 512], F32)) for k in range(2)]
                z_in, y_out = [sem(f"m_z_in{k}") for k in range(2)], [sem(f"m_y_out{k}") for k in range(2)]
                z_turned, zt_set, h_set, hid_set, h_turned, ht_set, y_set, y_ready = (
                    sem(f"m_{n}") for n in ("z_turned", "zt_set", "h_set", "hid_set", "h_turned", "ht_set", "y_set", "y_ready"))
                block = ph2.enter_context(nc.Block())
                reason = "a tile's expert is below EXP"

                def tile_rows(t, n):
                    return t[bass.ds(n * P, P), :]

                @block.sync
                def _(sp):
                    def load(n, k, turns):
                        wait_count(sp, z_turned, turns)
                        sp.dma_start(zin[:, k, :], tile_rows(zs_d, n)).then_inc(z_in[k], 16)

                    def store(n, k):
                        sp.wait_ge(y_ready, n + 1)
                        sp.dma_start(tile_rows(y_d, n), y[:, k, :]).then_inc(y_out[k], 16)
                    load(0, 0, 0)
                    load(1, 1, 0)
                    with sp.Fori(0, MT // 2 - 1) as i:
                        for k in range(2):
                            load(2 * i + k + 2, k, 2 * i + k + 1)
                            store(2 * i + k, k)
                    for k in range(2):
                        store(MT - 2 + k, k)
                        sp.wait_ge(y_out[k], 16 * (MT // 2))

                @block.tensor
                def _(pe):
                    def turn_z(n, k, i):
                        pe.wait_ge(z_in[k], 16 * (i + 1))
                        wait_count(pe, zt_set, n - 1)
                        for c in range(KC):
                            last = nc.tensor.transpose(pz[k][:, c, :], zin[:, k, c * P:(c + 1) * P], ident[:, :])
                        last.then_inc(z_turned, 1)

                    def hidden(n, k, at):
                        pe.wait_ge(zt_set, n + 1)
                        wait_count(pe, hid_set, n - 1)
                        for c in range(KC):
                            last = nc.tensor.matmul(phid[k][:, :], zt[:, k, c, :], w1[:, bass.ds(at + c * EH, EH)],
                                                    start=(c == 0), stop=(c == KC - 1))
                        last.then_inc(h_set, 1)

                    def turn_h(n, k):
                        pe.wait_ge(hid_set, n + 1)
                        wait_count(pe, ht_set, n - 1)
                        for c in range(HC):
                            last = nc.tensor.transpose(pht[k][:, c, :], hid[:, k, c * P:(c + 1) * P], ident[:, :])
                        last.then_inc(h_turned, 1)

                    def result(n, k, at):
                        pe.wait_ge(ht_set, n + 1)
                        wait_count(pe, y_ready, n - 1)
                        for c in range(HC):
                            last = nc.tensor.matmul(py[k][:, 0:D], ht[:, k, c, :], w2[:, bass.ds(at + c * D, D)],
                                                    start=(c == 0), stop=(c == HC - 1))
                        last.then_inc(y_set, 1)

                    def experts(n, count):
                        return nc.values_load_multi_w_load_instructions(
                            expert_of[0:1, bass.ds(n, count)], engines=PE_ONLY, min_val=0, max_val=(EXP - 1) * PART,
                            skip_runtime_bounds_check_because=reason)[1]

                    def pair(i, more):
                        at = experts(2 * i, 3)
                        for k in range(2):
                            n = 2 * i + k
                            turn_h(n, k)
                            if more or k == 0:
                                hidden(n + 1, 1 - k, at[k + 1])
                            if more:
                                turn_z(n + 2, k, i + 1)
                            result(n, k, at[k])
                    turn_z(0, 0, 0)
                    turn_z(1, 1, 0)
                    hidden(0, 0, experts(0, 1)[0])
                    pair(0, True)
                    with pe.Fori(1, MT // 2 - 1) as i:
                        pair(i, True)
                    pair(MT // 2 - 1, False)

                @block.scalar
                def _(act):
                    def copy_z(n, k):
                        act.wait_ge(z_turned, n + 1)
                        wait_count(act, h_set, n - 1)
                        nc.scalar.activation(zt[:, k, :, :], pz[k][:, :, :], ACT.Copy).then_inc(zt_set, 1)

                    def relu_h(n, k):
                        act.wait_ge(h_turned, n + 1)
                        wait_count(act, y_set, n - 1)
                        nc.scalar.activation(ht[:, k, :, :], pht[k][:, :, :], ACT.Relu).then_inc(ht_set, 1)

                    def pair(i, more):
                        for k in range(2):
                            relu_h(2 * i + k, k)
                            if more:
                                copy_z(2 * i + k + 2, k)
                    copy_z(0, 0)
                    copy_z(1, 1)
                    pair(0, True)
                    with act.Fori(1, MT // 2 - 1) as i:
                        pair(i, True)
                    pair(MT // 2 - 1, False)

                @block.vector
                def _(dve):
                    def take_h(n, k, at):
                        dve.wait_ge(h_set, n + 1)
                        wait_count(dve, h_turned, n - 1)
                        nc.vector.tensor_tensor(hid[:, k, :], phid[k][:, :], b1[:, bass.ds(at // (PART // EH), EH)], ALU.add)\
                            .then_inc(hid_set, 1)

                    def take_y(n, k, at, i):
                        dve.wait_ge(y_set, n + 1)
                        wait_count(dve, y_out[k], 16 * i)
                        nc.vector.tensor_tensor(y[:, k, :], py[k][:, 0:D], b2[:, bass.ds(at // (PART // D), D)], ALU.add)\
                            .then_inc(y_ready, 1)

                    def experts(n, count):
                        return nc.values_load_multi_w_load_instructions(
                            expert_of[0:1, bass.ds(n, count)], engines=DVE_ONLY, min_val=0, max_val=(EXP - 1) * PART,
                            skip_runtime_bounds_check_because=reason)[1]

                    def pair(i, more):
                        at = experts(2 * i, 3)
                        for k in range(2):
                            if more or k == 0:
                                take_h(2 * i + k + 1, 1 - k, at[k + 1])
                            take_y(2 * i + k, k, at[k], i)
                    take_h(0, 0, experts(0, 1)[0])
                    pair(0, True)
                    with dve.Fori(1, MT // 2 - 1) as i:
                        pair(i, True)
                    pair(MT // 2 - 1, False)

            with ExitStack() as ph2:
                ring = ph2.enter_context(nc.sbuf_tensor("i_ring", [P, GROUP, 2, D], F32))
                ix = ph2.enter_context(nc.sbuf_tensor("i_ix", [P, GROUP, 2], I32))
                landed = [sem(f"i_landed{k}") for k in range(GROUP)]
                staged, may_gather, chain = sem("i_staged"), sem("i_may_gather"), sem("i_chain")
                block = ph2.enter_context(nc.Block())

                @block.gpsimd
                def _(pool):
                    with pool.Fori(0, (FULL + 1) // GROUP) as i:
                        for k in range(GROUP):
                            pool.wait_ge(staged, GROUP * i + k + 1)
                            pool.sem_inc(may_gather, 1)
                            for m in range(2):
                                pool.indirect_dma_start(ring[:, k, m, :], None, y_d[:, :],
                                                        bass.IndirectOffsetOnAxis(ap=ix[:, k, m:m + 1], axis=0))\
                                    .then_inc(landed[k], 16)

                @block.vector
                def _(dve):
                    def stage(i, k):
                        nc.vector.tensor_copy(ix[:, k:k + 1, :], place_i[:, bass.ds(GROUP * i + k, 1), :]).then_inc(staged, 1)

                    def add(i, k):
                        b = bass.ds(GROUP * i + k, 1)
                        dve.wait_ge(landed[k], 32 * (i + 1))
                        for m in range(2):
                            nc.vector.scalar_tensor_tensor(out=X[:, b, :], in0=ring[:, k, m:m + 1, :], scalar=share[m][:, b],
                                                           in1=X[:, b, :], op0=ALU.mult, op1=ALU.add).then_inc(chain, 1)
                            dve.wait_ge(chain, 2 * (GROUP * i + k) + m + 1)
                    for k in range(GROUP):
                        stage(0, k)
                    with dve.Fori(0, (FULL + 1) // GROUP - 1) as i:
                        for k in range(GROUP):
                            add(i, k)
                            stage(i + 1, k)
                    for k in range(GROUP):
                        add((FULL + 1) // GROUP - 1, k)

        norm_stats("ln2", X)

        recycle()

        SCALE = float(HD) ** -0.5
        with ExitStack() as at_ph:
            skip = at_ph.enter_context(nc.sbuf_tensor("a_skip", [P, BLOCKS, D], F32))
            L = at_ph.enter_context(nc.sbuf_tensor("a_L", [P, HEADS, SLOTS], F32))
            with ExitStack() as q_ph:
                Q = q_ph.enter_context(nc.sbuf_tensor("a_Q", [P, BLOCKS, D], F32))
                with ExitStack() as ph:
                    K = ph.enter_context(nc.sbuf_tensor("a_K", [P, BLOCKS, D], F32))
                    V = ph.enter_context(nc.sbuf_tensor("a_V", [P, BLOCKS, D], F32))
                    with ExitStack() as ph2:
                        block = ph2.enter_context(nc.Block())

                        @block.sync
                        def _(sp):
                            sp.wait_ge(attn_in, 16 * 2 * len(attn))

                    def add_biases(dve, b, po, chain, at):
                        for m, t in enumerate((Q, K, V, skip)):
                            last = nc.vector.tensor_tensor(t[:, bass.ds(b, 1), :], po[:, m * D:(m + 1) * D].unsqueeze(1),
                                                           ab[m][:, :].unsqueeze(1), ALU.add)
                        return last
                    project("qkvs", Z, KC, [(t, D) for t in aw], add_biases, 0, norm_of=X)
                    store_rows("k", k_d, K)
                    store_rows("v", v_d, V)

                with ExitStack() as ph:
                    oh = ph.enter_context(nc.sbuf_tensor("l_oh", [P, U, P], F32))
                    oht = ph.enter_context(nc.sbuf_tensor("l_oht", [P, U, P], F32))
                    ring = ph.enter_context(nc.sbuf_tensor("l_ring", [P, U, D], F32))
                    prod = ph.enter_context(nc.sbuf_tensor("l_prod", [P, HALF, D], F32))
                    ix = ph.enter_context(nc.sbuf_tensor("l_ix", [P, U], I32))
                    pt = [ph.enter_context(nc.psum_tensor(f"l_pt{h}", [P, HALF, P], F32)) for h in range(2)]
                    pq = [ph.enter_context(nc.psum_tensor(f"l_pq{h}", [P, HALF, D], F32)) for h in range(2)]
                    landed = [sem(f"l_landed{k}") for k in range(U)]
                    may_gather = sem("l_may_gather")
                    oh_ready, ix_ready, turned_, oht_set, q_set, multiplied, reduced = (
                        sem("l_oh_ready"), sem("l_ix_ready"), sem("l_turned"), sem("l_oht_set"), sem("l_q_set"),
                        sem("l_multiplied"), sem("l_reduced"))
                    block = ph.enter_context(nc.Block())

                    @block.gpsimd
                    def _(pool):
                        with pool.Fori(0, STEPS) as it:
                            for h in range(2):
                                pool.wait_ge(ix_ready, 2 * it + h + 1)
                                pool.sem_inc(may_gather, 1)
                                for k in range(HALF * h, HALF * (h + 1)):
                                    pool.indirect_dma_start(
                                        ring[:, k, :], None, k_d[:, :],
                                        bass.IndirectOffsetOnAxis(ap=ix[:, k:k + 1], axis=0)).then_inc(landed[k], 16)

                    @block.vector
                    def _(dve):
                        def prepare(it, h):
                            mine = slice(HALF * h, HALF * (h + 1))
                            wait_count(dve, multiplied, 2 * it + h - 1)
                            nc.vector.tensor_copy(ix[:, mine], src_i[:, bass.ds(U * it + HALF * h, HALF)]).then_inc(ix_ready, 1)
                            wait_count(dve, turned_, 2 * it + h - 1)
                            nc.vector.tensor_tensor(
                                oh[:, mine, :], lane[:, :].unsqueeze(1).broadcast_to([P, HALF, P]),
                                dl[:, bass.ds(U * it + HALF * h, HALF)].unsqueeze(2).broadcast_to([P, HALF, P]),
                                ALU.is_equal).then_inc(oh_ready, 1)

                        def use(it, h):
                            dve.wait_ge(q_set, 2 * it + h + 1)
                            for k in range(HALF * h, HALF * (h + 1)):
                                dve.wait_ge(landed[k], 16 * it + 16)
                            wait_count(dve, reduced, 2 * it + h)
                            nc.vector.tensor_tensor(prod[:, :, :], pq[h][:, :, :], ring[:, HALF * h:HALF * (h + 1), :],
                                                    ALU.mult).then_inc(multiplied, 1)
                            dve.wait_ge(multiplied, 2 * it + h + 1)
                            nc.vector.tensor_reduce(
                                L[:, :, bass.ds(U * it + HALF * h, HALF)].rearrange("p n k -> p k n"),
                                prod[:, :, :].rearrange("p k (n d) -> p k n d", d=HD), AX.X, ALU.add).then_inc(reduced, 1)
                        prepare(0, 0)
                        prepare(0, 1)
                        for h in range(2):
                            use(0, h)
                            prepare(1, h)
                        with dve.Fori(1, STEPS - 1) as it:
                            for h in range(2):
                                use(it, h)
                                prepare(it + 1, h)
                        use(STEPS - 1, 0)
                        use(STEPS - 1, 1)
                        dve.wait_ge(reduced, 2 * STEPS)

                    @block.tensor
                    def _(pe):
                        def step(it):
                            _, at = nc.values_load_multi_w_load_instructions(
                                blk2[0:1, bass.ds(U * it, U)], engines=PE_ONLY, min_val=0, max_val=(BLOCKS - 1) * D,
                                skip_runtime_bounds_check_because="a slot's block is below BLOCKS")
                            q_rows = Q[:, :, :].rearrange("p b f -> p (b f)")
                            for h in range(2):
                                pe.wait_ge(oh_ready, 2 * it + h + 1)
                                wait_count(pe, oht_set, 2 * it + h - 1)
                                for k in range(HALF):
                                    last = nc.tensor.transpose(pt[h][:, k, :], oh[:, HALF * h + k, :], ident[:, :])
                                last.then_inc(turned_, 1)
                            for h in range(2):
                                pe.wait_ge(oht_set, 2 * it + h + 1)
                                wait_count(pe, multiplied, 2 * it + h - 1)
                                for k in range(HALF):
                                    last = nc.tensor.matmul(pq[h][:, k, :], oht[:, HALF * h + k, :],
                                                            q_rows[:, bass.ds(at[HALF * h + k], D)], start=True, stop=True)
                                last.then_inc(q_set, 1)
                        step(0)
                        with pe.Fori(1, STEPS) as it:
                            step(it)

                    @block.scalar
                    def _(act):
                        def step(it):
                            for h in range(2):
                                act.wait_ge(turned_, 2 * it + h + 1)
                                wait_count(act, q_set, 2 * it + h - 1)
                                nc.scalar.activation(oht[:, HALF * h:HALF * (h + 1), :], pt[h][:, :, :], ACT.Copy)\
                                    .then_inc(oht_set, 1)
                        step(0)
                        with act.Fori(1, STEPS) as it:
                            step(it)

            with ExitStack() as ph:
                def sb(name, shape, dt=F32):
                    return ph.enter_context(nc.sbuf_tensor(name, shape, dt))

                LT = sb("s_LT", [P, CS, P])
                FT = sb("s_FT", [P, CS, P])
                MT = sb("s_MT", [P, CS, P])
                KT = sb("s_KT", [P, CS, P])
                brk = sb("s_brk", [P, SEQ + 1])
                cols = sb("s_cols", [P, 4])
                row = sb("s_row", [1, 2, HEADS, CH])
                pen_f = sb("s_pen_f", [1, HEADS, CH])
                pen_b = sb("s_pen_b", [1, HEADS, CH])
                link_f = sb("s_link_f", [1, HEADS, CH])
                link_b = sb("s_link_b", [1, HEADS, CH])
                ends = sb("s_ends", [1, HEADS, CH])
                run_max = sb("s_run_max", [1, HEADS, CH])
                carry = sb("s_carry", [1, HEADS, CH])
                init = sb("s_init", [P, 2])
                NT = 4
                groups = [(g, min(NT, CS - g)) for g in range(0, CS, NT)]
                pt = [ph.enter_context(nc.psum_tensor(f"s_pt{i}", [P, NT, P], F32)) for i in range(2)]
                pr = ph.enter_context(nc.psum_tensor("s_pr", [1, 512], F32))
                pc = ph.enter_context(nc.psum_tensor("s_pc", [P, 2], F32))
                key_in, s_turned, s_copied, col_set, row_set, row_copied, carry_set, init_set = (
                    sem("key_in"), sem("s_turned"), sem("s_copied"), sem("col_set"), sem("row_set"), sem("row_copied"),
                    sem("carry_set"), sem("init_set"))
                s_chain, less_max, s_exp, e_turned, e_copied = (
                    sem("s_chain"), sem("less_max"), sem("s_exp"), sem("e_turned"), sem("e_copied"))
                block = ph.enter_context(nc.Block())
                lt, ft, mt, kt = (t[:, :, :].rearrange("p j e -> p (j e)") for t in (LT, FT, MT, KT))

                @block.sync
                def _(sp):
                    for h in range(HEADS):
                        sp.dma_start(KT[h * CH:(h + 1) * CH, :, :].rearrange("c j e -> c (j e)"),
                                     key_d.rearrange("(c j) e -> c (j e)", j=CS)).then_inc(key_in, 16)
                    sp.wait_ge(key_in, 16 * HEADS)

                @block.tensor
                def _(pe):
                    by_j = L[:, :, :].rearrange("p h (c j) -> p j (h c)", j=CS)
                    for g, (j0, n) in enumerate(groups):
                        wait_count(pe, s_copied, g - 1)
                        for j in range(n):
                            last = nc.tensor.transpose(pt[g % 2][:, j, :], by_j[:, j0 + j, :], ident[:, :])
                        last.then_inc(s_turned, 1)
                    for n, m in enumerate((0, 1, 2, 3)):
                        pe.wait_ge(col_set, n + 1)
                        nc.tensor.matmul(pr[0:1, m * P:(m + 1) * P], cols[:, m:m + 1], ident[:, :], start=True, stop=True)\
                            .then_inc(row_set, 1)
                        if m >= 2:
                            pe.wait_ge(carry_set, m - 1)
                            nc.tensor.matmul(pc[:, m - 2:m - 1], carry[:, :, :].rearrange("o h c -> o (h c)"), ones[0:1, 0:1],
                                             start=True, stop=True).then_inc(init_set, 1)
                    pe.wait_ge(s_exp, 1)
                    for g, (j0, n) in enumerate(groups):
                        wait_count(pe, e_copied, g - 1)
                        for j in range(n):
                            last = nc.tensor.transpose(pt[g % 2][:, j, :], MT[:, j0 + j, :], ident[:, :])
                        last.then_inc(e_turned, 1)

                @block.scalar
                def _(act):
                    for g, (j0, n) in enumerate(groups):
                        act.wait_ge(s_turned, g + 1)
                        nc.scalar.activation(LT[:, j0:j0 + n, :], pt[g % 2][:, 0:n, :], ACT.Copy).then_inc(s_copied, 1)
                    act.wait_ge(less_max, 1)
                    nc.scalar.activation(MT[:, :, :], MT[:, :, :], ACT.Exp, scale=SCALE).then_inc(s_exp, 1)
                    by_j = L[:, :, :].rearrange("p h (c j) -> p j (h c)", j=CS)
                    for g, (j0, n) in enumerate(groups):
                        act.wait_ge(e_turned, g + 1)
                        for j in range(n):
                            last = nc.scalar.activation(by_j[:, j0 + j, :], pt[g % 2][:, j, :], ACT.Copy)
                        last.then_inc(e_copied, 1)

                @block.vector
                def _(dve):
                    link = Chain(dve, s_chain)
                    dve.wait_ge(key_in, 16 * HEADS)
                    link(nc.vector.memset(brk[:, 0:1], 0.0))
                    link(nc.vector.memset(brk[:, SEQ:SEQ + 1], 0.0))
                    link(nc.vector.tensor_tensor(brk[:, 1:SEQ], kt[:, 1:SEQ], kt[:, 0:SEQ - 1], ALU.not_equal))
                    link(nc.vector.tensor_scalar(brk[:, 1:SEQ], brk[:, 1:SEQ], -BIG, None, ALU.mult))
                    nc.vector.tensor_copy(cols[:, 0:1], kt[:, 0:1]).then_inc(col_set, 1)
                    nc.vector.tensor_copy(cols[:, 1:2], kt[:, SEQ - 1:SEQ]).then_inc(col_set, 1)
                    dve.wait_ge(row_set, 2)
                    first, final = (pr[0:1, m * P:(m + 1) * P].rearrange("o (h c) -> o h c", h=HEADS) for m in (0, 1))
                    row0, row1 = (row[:, m, :, :] for m in (0, 1))
                    link(nc.vector.tensor_copy(row0, first))
                    link(nc.vector.tensor_copy(row1, final))
                    link(nc.vector.memset(link_f[:, :, :], -BIG))
                    link(nc.vector.memset(link_b[:, :, :], -BIG))
                    link(nc.vector.tensor_tensor(link_f[:, :, 1:CH], row0[:, :, 1:CH], row1[:, :, 0:CH - 1], ALU.not_equal))
                    link(nc.vector.tensor_scalar(link_f[:, :, 1:CH], link_f[:, :, 1:CH], -BIG, None, ALU.mult))
                    link(nc.vector.tensor_copy(link_b[:, :, 0:CH - 1], link_f[:, :, 1:CH]))
                    link(nc.vector.tensor_tensor(ends[:, :, :], row0, row1, ALU.not_equal))
                    link(nc.vector.scalar_tensor_tensor(out=pen_f[:, :, :], in0=ends[:, :, :], scalar=-BIG, in1=link_f[:, :, :],
                                                        op0=ALU.mult, op1=ALU.add))
                    link(nc.vector.scalar_tensor_tensor(out=pen_b[:, :, :], in0=ends[:, :, :], scalar=-BIG, in1=link_b[:, :, :],
                                                        op0=ALU.mult, op1=ALU.add))
                    dve.wait_ge(s_copied, len(groups))

                    def flat(t):
                        return t[:, :, :].rearrange("o h c -> o (h c)")

                    link(nc.vector.tensor_tensor_scan(ft, brk[:, 0:SEQ], lt, -BIG, ALU.add, ALU.max))
                    nc.vector.tensor_copy(cols[:, 2:3], ft[:, SEQ - 1:SEQ]).then_inc(col_set, 1)
                    dve.wait_ge(row_set, 3)
                    link(nc.vector.tensor_copy(ends[:, :, :], pr[0:1, 2 * P:3 * P].rearrange("o (h c) -> o h c", h=HEADS)))
                    link(nc.vector.tensor_tensor_scan(flat(run_max), flat(pen_f), flat(ends), -BIG, ALU.add, ALU.max))
                    link(nc.vector.memset(carry[:, :, :], -BIG))
                    nc.vector.tensor_tensor(carry[:, :, 1:CH], run_max[:, :, 0:CH - 1],
                                            link_f[:, :, 1:CH], ALU.add).then_inc(carry_set, 1)
                    dve.wait_ge(init_set, 1)
                    link(nc.vector.tensor_copy(init[:, 0:1], pc[:, 0:1]))
                    link(nc.vector.tensor_tensor_scan(ft, brk[:, 0:SEQ], lt, init[:, 0:1], ALU.add, ALU.max))
                    back = brk[:, SEQ:0:-1]
                    link(nc.vector.tensor_tensor_scan(mt[:, ::-1], back, ft[:, ::-1], -BIG, ALU.add, ALU.max))
                    nc.vector.tensor_copy(cols[:, 3:4], mt[:, 0:1]).then_inc(col_set, 1)
                    dve.wait_ge(row_set, 4)
                    link(nc.vector.tensor_copy(ends[:, :, :], pr[0:1, 3 * P:4 * P].rearrange("o (h c) -> o h c", h=HEADS)))
                    link(nc.vector.tensor_tensor_scan(flat(run_max)[:, ::-1], flat(pen_b)[:, ::-1], flat(ends)[:, ::-1],
                                                      -BIG, ALU.add, ALU.max))
                    link(nc.vector.memset(carry[:, :, :], -BIG))
                    nc.vector.tensor_tensor(carry[:, :, 0:CH - 1], run_max[:, :, 1:CH],
                                            link_b[:, :, 0:CH - 1], ALU.add).then_inc(carry_set, 1)
                    dve.wait_ge(init_set, 2)
                    link(nc.vector.tensor_copy(init[:, 1:2], pc[:, 1:2]))
                    link(nc.vector.tensor_tensor_scan(mt[:, ::-1], back, ft[:, ::-1], init[:, 1:2], ALU.add, ALU.max))
                    nc.vector.tensor_tensor(mt, lt, mt, ALU.subtract).then_inc(less_max, 1)

            with ExitStack() as sum_ph:
                total = sum_ph.enter_context(nc.sbuf_tensor("a_total", [P, BLOCKS * AW], F32))
                with ExitStack() as ph:
                    oh = ph.enter_context(nc.sbuf_tensor("v_oh", [P, U, P], F32))
                    ring = ph.enter_context(nc.sbuf_tensor("v_ring", [P, U, D], F32))
                    msg = ph.enter_context(nc.sbuf_tensor("v_msg", [P, U, AW], F32))
                    ix = ph.enter_context(nc.sbuf_tensor("v_ix", [P, U], I32))
                    pm = [ph.enter_context(nc.psum_tensor(f"v_pm{k}", [P, 512], F32)) for k in range(U)]
                    landed = [sem(f"v_landed{k}") for k in range(U)]
                    may_gather = sem("v_may_gather")
                    oh_ready, ix_ready, msg_set, weight_set, product, added, cleared = (
                        sem("v_oh_ready"), sem("v_ix_ready"), sem("v_msg_set"), sem("v_weight_set"), sem("v_product"),
                        sem("v_added"), sem("v_cleared"))
                    block = ph.enter_context(nc.Block())

                    @block.gpsimd
                    def _(pool):
                        pool.memset(total[:, :], 0.0).then_inc(cleared, 1)
                        with pool.Fori(0, STEPS) as it:
                            for h in range(2):
                                pool.wait_ge(ix_ready, 2 * it + h + 1)
                                pool.sem_inc(may_gather, 1)
                                for k in range(HALF * h, HALF * (h + 1)):
                                    pool.indirect_dma_start(
                                        ring[:, k, :], None, v_d[:, :],
                                        bass.IndirectOffsetOnAxis(ap=ix[:, k:k + 1], axis=0)).then_inc(landed[k], 16)

                    @block.scalar
                    def _(act):
                        def step(it):
                            for h in range(2):
                                wait_count(act, product, U * it + HALF * (h + 1) - U)
                                nc.scalar.activation(msg[:, HALF * h:HALF * (h + 1), D:AW],
                                                     L[:, :, bass.ds(U * it + HALF * h, HALF)].rearrange("p n k -> p k n"), ACT.Copy).then_inc(weight_set, 1)
                        step(0)
                        with act.Fori(1, STEPS) as it:
                            step(it)

                    @block.vector
                    def _(dve):
                        def stage(it, h):
                            nc.vector.tensor_copy(ix[:, HALF * h:HALF * (h + 1)],
                                                  src_i[:, bass.ds(U * it + HALF * h, HALF)]).then_inc(ix_ready, 1)

                        def messages(it, h, more):
                            mine = slice(HALF * h, HALF * (h + 1))
                            slots = bass.ds(U * it + HALF * h, HALF)
                            wait_count(dve, product, U * it + HALF * (h + 1) - U)
                            nc.vector.tensor_tensor(
                                oh[:, mine, :], lane[:, :].unsqueeze(1).broadcast_to([P, HALF, P]),
                                dl[:, slots].unsqueeze(2).broadcast_to([P, HALF, P]), ALU.is_equal).then_inc(oh_ready, 1)
                            for k in range(HALF * h, HALF * (h + 1)):
                                dve.wait_ge(landed[k], 16 * it + 16)
                            nc.vector.tensor_tensor(
                                msg[:, mine, 0:D].rearrange("p k (n d) -> p k n d", d=HD),
                                ring[:, mine, :].rearrange("p k (n d) -> p k n d", d=HD),
                                L[:, :, slots].rearrange("p n k -> p k n").unsqueeze(3).broadcast_to([P, HALF, HEADS, HD]), ALU.mult).then_inc(msg_set, 1)
                            if more:
                                dve.wait_ge(msg_set, 2 * it + h + 1)
                                stage(it + 1, h)

                        def add(it, h, at):
                            for k in range(HALF * h, HALF * (h + 1)):
                                dve.wait_ge(product, U * it + k + 1)
                                where = total[:, bass.ds(at[k], AW)]
                                wait_count(dve, added, U * it + k)
                                nc.vector.tensor_tensor(where, where, pm[k][:, 0:AW], ALU.add).then_inc(added, 1)

                        def blocks_of(it):
                            return nc.values_load_multi_w_load_instructions(
                                blk3[0:1, bass.ds(U * it, U)], engines=DVE_ONLY, min_val=0, max_val=(BLOCKS - 1) * AW,
                                skip_runtime_bounds_check_because="a slot's block is below BLOCKS")[1]
                        dve.wait_ge(cleared, 1)
                        stage(0, 0)
                        stage(0, 1)
                        messages(0, 0, True)
                        messages(0, 1, True)
                        with dve.Fori(1, STEPS - 1) as it:
                            at = blocks_of(it - 1)
                            for h in range(2):
                                add(it - 1, h, at)
                                messages(it, h, True)
                        at = blocks_of(STEPS - 2)
                        for h in range(2):
                            add(STEPS - 2, h, at)
                            messages(STEPS - 1, h, False)
                        at = blocks_of(STEPS - 1)
                        for h in range(2):
                            add(STEPS - 1, h, at)
                        dve.wait_ge(added, SLOTS)

                    @block.tensor
                    def _(pe):
                        def step(it):
                            for k in range(U):
                                if k % HALF == 0:
                                    pe.wait_ge(oh_ready, 2 * it + k // HALF + 1)
                                    pe.wait_ge(msg_set, 2 * it + k // HALF + 1)
                                    pe.wait_ge(weight_set, 2 * it + k // HALF + 1)
                                wait_count(pe, added, U * it + k - U + 1)
                                nc.tensor.matmul(pm[k][:, 0:AW], oh[:, k, :], msg[:, k, :], start=True, stop=True)\
                                    .then_inc(product, 1)
                        step(0)
                        with pe.Fori(1, STEPS) as it:
                            step(it)

                gamma = sum_ph.enter_context(nc.sbuf_tensor("a_gamma", [P, D], F32))
                beta = sum_ph.enter_context(nc.sbuf_tensor("a_beta", [P, D], F32))
                load_weights("agb", [vector(gamma, a["L1_gnn_gamma"]), vector(beta, a["L1_gnn_beta"])])
                with ExitStack() as ph:
                    den = ph.enter_context(nc.sbuf_tensor("f_den", [P, BLOCKS, HEADS], F32))
                    chain, out_set, gelu_set = sem("f_chain"), sem("f_out_set"), sem("f_gelu_set")
                    block = ph.enter_context(nc.Block())
                    by_block = total[:, :].rearrange("p (b f) -> p b f", f=AW)

                    @block.vector
                    def _(dve):
                        link = Chain(dve, chain)
                        link(nc.vector.tensor_scalar(den[:, :, :], by_block[:, :, D:AW], 1e-30, None, ALU.max))
                        link(nc.vector.reciprocal(den[:, :, :], den[:, :, :]))
                        values = by_block[:, :, 0:D].rearrange("p b (n d) -> p b n d", d=HD)
                        link(nc.vector.tensor_tensor(values, values, den[:, :, :].unsqueeze(3).broadcast_to([P, BLOCKS, HEADS, HD]),
                                                     ALU.mult))
                        nc.vector.tensor_tensor(skip[:, :, :], skip[:, :, :], by_block[:, :, 0:D], ALU.add).then_inc(out_set, 1)
                        dve.wait_ge(gelu_set, 1)
                        link(nc.vector.tensor_tensor(skip[:, :, :], skip[:, :, :], Z[:, :, :], ALU.add))

                    @block.scalar
                    def _(act):
                        act.wait_ge(out_set, 1)
                        nc.scalar.activation(skip[:, :, :], skip[:, :, :], ACT.Gelu).then_inc(gelu_set, 1)
                norm_stats("lna", skip)
                with ExitStack() as ph:
                    applied, scaled, moved = sem("g_applied"), sem("g_scaled"), sem("g_moved")
                    block = ph.enter_context(nc.Block())

                    @block.scalar
                    def _(act):
                        with act.Fori(0, PAIRS) as i:
                            for k in range(2):
                                b = bass.ds(2 * i + k, 1)
                                nc.scalar.activation(skip[:, b, :], skip[:, b, :], ACT.Identity, scale=scale[:, b],
                                                     bias=shift[:, b]).then_inc(applied, 1)

                    @block.vector
                    def _(dve):
                        with dve.Fori(0, PAIRS) as i:
                            for k in range(2):
                                b = bass.ds(2 * i + k, 1)
                                dve.wait_ge(applied, 2 * i + k + 1)
                                nc.vector.tensor_tensor(skip[:, b, :], skip[:, b, :], gamma[:, :].unsqueeze(1), ALU.mult)\
                                    .then_inc(scaled, 1)
                                dve.wait_ge(scaled, 2 * i + k + 1)
                                nc.vector.tensor_tensor(skip[:, b, :], skip[:, b, :], beta[:, :].unsqueeze(1), ALU.add)\
                                    .then_inc(moved, 1)

                    @block.gpsimd
                    def _(pool):
                        with pool.Fori(0, PAIRS) as i:
                            for k in range(2):
                                b = bass.ds(2 * i + k, 1)
                                pool.wait_ge(moved, 2 * i + k + 1)
                                nc.gpsimd.tensor_tensor(X[:, b, :], X[:, b, :], skip[:, b, :], ALU.add)


        norm_stats("ln3", X)

        recycle()

        FC = FH // P
        with ExitStack() as ph:
            def sb(name, shape, dt=F32):
                return ph.enter_context(nc.sbuf_tensor(name, shape, dt))

            zt_all = sb("r_zt_all", [P, KC, NODES])
            wr = sb("r_wr", [P, KC, 1])
            br = sb("r_br", [P, 1])
            w1 = sb("r_w1", [P, KC, FH])
            w2 = sb("r_w2", [P, FC, D])
            b1 = sb("r_b1", [P, FC])
            b2 = sb("r_b2", [P, D])
            weight = sb("r_weight", [P, BLOCKS])
            every = sb("r_every", [P, NODES])
            load_weights("rw", [
                matrix(wr[:, :, :], a["L1_ffn_wr"]), vector(br, a["L1_ffn_br"]), matrix(w1[:, :, :], a["L1_ffn_w1"]),
                matrix(w2[:, :, :], a["L1_ffn_w2"]), vector(b2, a["L1_ffn_b2"]),
                lambda sp, done: sp.dma_start(b1[:, :], a["L1_ffn_b1"].rearrange("(c p) -> p c", p=P),
                                              allow_slow_non_contiguous=True).then_inc(done, 16)])
            project("route", Z, KC, [(wr, 1)], lambda dve, b, po, chain, at: nc.vector.tensor_tensor(
                weight[:, bass.ds(b, 1)], po[:, 0:1], br[:, :], ALU.add), 0, norm_of=X, save_t=zt_all)

            with ExitStack() as ph2:
                def sb2(name, shape, dt=F32):
                    return ph2.enter_context(nc.sbuf_tensor(name, shape, dt))

                ht = sb2("r_ht", [P, FC, 2 * P])
                y = sb2("r_y", [P, BLOCKS, D])
                wt = sb2("r_wt", [BLOCKS, P])
                larger = sb2("r_larger", [P, 2, NODES], mybir.dt.bfloat16)
                above = sb2("r_above", [P, BLOCKS])
                kept = sb2("r_kept", [P, BLOCKS])
                last_of = sb2("r_last_of", [P, BLOCKS])
                tie_count = sb2("r_tie_count", [P, BLOCKS])
                tie_until = sb2("r_tie_until", [P, BLOCKS])
                coef = sb2("r_coef", [P, BLOCKS])
                top_col = sb2("r_top_col", [P, 1])
                top_row = sb2("r_top_row", [1, P])
                top_one = sb2("r_top_one", [1, 1])
                top_all = sb2("r_top_all", [P, 1])
                ps_h = [ph2.enter_context(nc.psum_tensor(f"r_ps_h{c}", [P, 512], F32)) for c in range(4)]
                ps_y = [ph2.enter_context(nc.psum_tensor(f"r_ps_y{k}", [P, 512], F32)) for k in range(2)]
                pw = ph2.enter_context(nc.psum_tensor("r_pw", [P, 512], F32))
                (w_turned, wt_set, w_out, every_in, every_set, h_set, h_gelu, y_set, y_copied, chain, counted, base_set,
                 x_set, x_out, tie_step, tie_back, y_ready) = (sem(f"r_{n}") for n in (
                     "w_turned", "wt_set", "w_out", "every_in", "every_set", "h_set", "h_gelu", "y_set", "y_copied",
                     "chain", "counted", "base_set", "x_set", "x_out", "tie_step", "tie_back", "y_ready"))
                block = ph2.enter_context(nc.Block())
                TIE_AT = PAIRS - 1

                @block.tensor
                def _(pe):
                    nc.tensor.transpose(pw[0:BLOCKS, 0:P], weight[:, :], ident[:, :]).then_inc(w_turned, 1)

                    def step(n):
                        for h in range(FC):
                            wait_count(pe, h_gelu, FC * n + h - 3)
                            for c in range(KC):
                                last = nc.tensor.matmul(ps_h[h % 4][:, 0:2 * P], w1[:, c, h * P:(h + 1) * P],
                                                        zt_all[:, c, bass.ds(n * 2 * P, 2 * P)],
                                                        start=(c == 0), stop=(c == KC - 1))
                            last.then_inc(h_set, 1)
                        for m in range(2):
                            wait_count(pe, y_copied, 2 * n + m - 1)
                            for h in range(FC):
                                pe.wait_ge(h_gelu, FC * n + h + 1)
                                last = nc.tensor.matmul(ps_y[m][:, 0:D], ht[:, h, m * P:(m + 1) * P], w2[:, h, :],
                                                        start=(h == 0), stop=(h == FC - 1))
                            last.then_inc(y_set, 1)
                    step(0)
                    with pe.Fori(1, TIE_AT) as n:
                        step(n)
                    pe.wait_ge(tie_step, 1)
                    nc.tensor.transpose(pw[0:1, 0:P], top_col[:, :], ident[:, :]).then_inc(tie_back, 1)
                    pe.wait_ge(tie_step, 2)
                    nc.tensor.matmul(pw[:, 128:129], ones[0:1, :], top_one[:, :], start=True, stop=True).then_inc(tie_back, 1)
                    pe.wait_ge(tie_step, 3)
                    nc.tensor.matmul(pw[:, 256:256 + BLOCKS], before[:, :], last_of[:, :], start=True, stop=True)
                    nc.tensor.matmul(pw[:, 384:384 + BLOCKS], ones[:, :], last_of[:, :], start=True, stop=True).then_inc(tie_back, 1)
                    for n in range(TIE_AT, PAIRS):
                        step(n)

                @block.scalar
                def _(act):
                    act.wait_ge(w_turned, 1)
                    nc.scalar.activation(wt[:, :], pw[0:BLOCKS, 0:P], ACT.Copy).then_inc(wt_set, 1)

                    def copy_y(n):
                        for m in range(2):
                            act.wait_ge(y_set, 2 * n + m + 1)
                            nc.scalar.activation(y[:, bass.ds(2 * n + m, 1), :], ps_y[m][:, 0:D].unsqueeze(1), ACT.Copy)\
                                .then_inc(y_copied, 1)

                    def step(n):
                        for h in range(FC):
                            act.wait_ge(h_set, FC * n + h + 1)
                            nc.scalar.activation(ht[:, h, :], ps_h[h % 4][:, 0:2 * P], ACT.Gelu_apprx_tanh,
                                                 bias=b1[:, h:h + 1]).then_inc(h_gelu, 1)
                        copy_y(n)
                    step(0)
                    with act.Fori(1, PAIRS) as n:
                        step(n)

                @block.sync
                def _(sp):
                    sp.wait_ge(wt_set, 1)
                    sp.dma_start(w_d[:, :], wt[:, :]).then_inc(w_out, 16)
                    sp.wait_ge(w_out, 16)
                    sp.dma_start(every[:, :], w_d.rearrange("(o b) p -> o (b p)", o=1).broadcast_to([P, NODES]))\
                        .then_inc(every_in, 16)
                    with sp.Fori(0, FULL) as b:
                        sp.wait_ge(x_set, b + 1)
                        sp.dma_start(out[bass.ds(b * P, P), :], X[:, bass.ds(b, 1), :].rearrange("p o f -> p (o f)"))\
                            .then_inc(x_out, 16)
                    sp.wait_ge(x_set, FULL + 1)
                    sp.dma_start(out[FULL * P:N, :], X[0:TAIL, FULL, :]).then_inc(x_out, 16)
                    sp.wait_ge(x_out, 16 * (FULL + 1))

                @block.gpsimd
                def _(pool):
                    with pool.Fori(0, BLOCKS) as b:
                        nc.gpsimd.tensor_tensor(X[:, bass.ds(b, 1), :], X[:, bass.ds(b, 1), :], Z[:, bass.ds(b, 1), :], ALU.add)\
                            .then_inc(base_set, 1)

                @block.vector
                def _(dve):
                    link = Chain(dve, chain)
                    dve.wait_ge(every_in, 16)
                    link(nc.vector.memset(every[:, N:NODES], -3.0e38))

                    def count(b, k):
                        wait_count(dve, counted, b - 1)
                        nc.vector.tensor_scalar(larger[:, k, :], every[:, :], weight[:, bass.ds(b, 1)], 0.0, ALU.is_gt,
                                                ALU.add, accum_out=above[:, bass.ds(b, 1)]).then_inc(counted, 1)
                    count(0, 0)
                    count(1, 1)
                    with dve.Fori(1, PAIRS) as i:
                        for k in range(2):
                            count(2 * i + k, k)
                    dve.wait_ge(counted, BLOCKS)
                    link(nc.vector.tensor_scalar(kept[:, :], above[:, :], float(KEEP), None, ALU.is_lt))
                    link(nc.vector.tensor_tensor(kept[:, :], kept[:, :], real[:, :], ALU.mult))
                    link(nc.vector.tensor_scalar(above[:, :], above[:, :], 1.0, None, ALU.add))
                    link(nc.vector.tensor_tensor(coef[:, :], above[:, :], kept[:, :], ALU.mult))
                    nc.vector.tensor_reduce(top_col[:, :], coef[:, :], AX.X, ALU.max).then_inc(tie_step, 1)
                    dve.wait_ge(tie_back, 1)
                    link(nc.vector.tensor_copy(top_row[:, :], pw[0:1, 0:P]))
                    nc.vector.tensor_reduce(top_one[:, :], top_row[:, :], AX.X, ALU.max).then_inc(tie_step, 1)
                    dve.wait_ge(tie_back, 2)
                    link(nc.vector.tensor_copy(top_all[:, :], pw[:, 128:129]))
                    nc.vector.scalar_tensor_tensor(out=last_of[:, :], in0=above[:, :], scalar=top_all[:, 0:1], in1=real[:, :],
                                                   op0=ALU.is_equal, op1=ALU.mult).then_inc(tie_step, 1)
                    dve.wait_ge(tie_back, 3)
                    link(nc.vector.tensor_copy(tie_count[:, :], pw[:, 384:384 + BLOCKS]))
                    link(nc.vector.tensor_tensor_scan(tie_until[:, :], ones[:, 0:BLOCKS], tie_count[:, :], 0.0, ALU.mult, ALU.add))
                    link(nc.vector.tensor_tensor(tie_until[:, :], tie_until[:, :], tie_count[:, :], ALU.subtract))
                    link(nc.vector.tensor_tensor(tie_until[:, :], tie_until[:, :], pw[:, 256:256 + BLOCKS], ALU.add))
                    link(nc.vector.tensor_tensor(tie_until[:, :], tie_until[:, :], last_of[:, :], ALU.mult))
                    link(nc.vector.tensor_tensor(above[:, :], above[:, :], tie_until[:, :], ALU.add))
                    link(nc.vector.scalar_tensor_tensor(out=coef[:, :], in0=above[:, :], scalar=float(KEEP) + 0.5,
                                                        in1=weight[:, :], op0=ALU.is_lt, op1=ALU.mult))
                    with dve.Fori(0, BLOCKS) as b:
                        one = bass.ds(b, 1)
                        dve.wait_ge(y_copied, b + 1)
                        nc.vector.tensor_tensor(y[:, one, :], y[:, one, :], b2[:, :].unsqueeze(1), ALU.add).then_inc(y_ready, 1)
                        dve.wait_ge(y_ready, b + 1)
                        dve.wait_ge(base_set, b + 1)
                        nc.vector.scalar_tensor_tensor(out=X[:, one, :], in0=y[:, one, :], scalar=coef[:, one],
                                                       in1=X[:, one, :], op0=ALU.mult, op1=ALU.add).then_inc(x_set, 1)


_INS = ["x", "src", "dst", "L0_gnn_W1", "L0_gnn_b1", "L0_gnn_W2", "L0_gnn_b2", "L0_ffn_Wg", "L0_ffn_bg", "L0_ffn_bias",
        "L0_ffn_W1", "L0_ffn_b1", "L0_ffn_W2", "L0_ffn_b2", "L1_gnn_Wq", "L1_gnn_bq", "L1_gnn_Wk", "L1_gnn_bk",
        "L1_gnn_Wv", "L1_gnn_bv", "L1_gnn_Wskip", "L1_gnn_bskip", "L1_gnn_gamma", "L1_gnn_beta",
        "L1_ffn_wr", "L1_ffn_br", "L1_ffn_w1", "L1_ffn_b1", "L1_ffn_w2", "L1_ffn_b2"]


def kernel(**inputs):
    import numpy as _np
    import concourse.bacc as _bacc
    from concourse.bass_utils import run_bass_kernel_spmd as _run

    nc = _bacc.Bacc("TRN2", target_bir_lowering=False, num_devices=1)
    arrays, args = {}, {}
    for name in _INS:
        a = _np.ascontiguousarray(inputs[name])
        arrays[f"in_{name}"] = a
        args[name] = nc.dram_tensor(f"in_{name}", a.shape, mybir.dt.from_np(a.dtype), kind="ExternalInput").ap()
    out = nc.dram_tensor("out_x", inputs["x"].shape, F32, kind="ExternalOutput").ap()
    gnn_program(nc, args, out)
    r = _run(nc, [arrays], core_ids=[0])
    return r.results[0]["out_x"]
```

```python
from contextlib import ExitStack
from math import prod

import concourse.bass as bass
from concourse import mybir

P = 128
F32 = mybir.dt.float32
I32 = mybir.dt.int32
ALU = mybir.AluOpType
ACT = mybir.ActivationFunctionType
AX = mybir.AxisListType
PE_ONLY = (mybir.EngineType.PE,)
DVE_ONLY = (mybir.EngineType.DVE,)

U = 8
HALF = U // 2
BIG = 1.0e30
EPS = 1e-5


class Chain:

    def __init__(self, eng, sem):
        self.eng, self.sem, self.n = eng, sem, 0

    def __call__(self, ins):
        self.n += 1
        ins.then_inc(self.sem, 1)
        self.eng.wait_ge(self.sem, self.n)


def wait_count(eng, sem, value):
    if isinstance(value, int) and value <= 0:
        return
    eng.wait_ge(sem, value)


def gnn_program(nc, a, out):
    N, D = a["x"].shape
    E = a["src"].shape[0]
    HID = a["L0_gnn_W1"].shape[1]
    EXP, _, EH = a["L0_ffn_W1"].shape
    FH = a["L1_ffn_w1"].shape[1]
    HEADS = 8
    HD = D // HEADS
    KC = D // P
    KEEP = max(1, int(0.5 * N)) - 1
    FULL = N // P
    TAIL = N - FULL * P
    BLOCKS = FULL + 1 + (FULL + 1) % 2
    PAIRS = BLOCKS // 2
    NODES = BLOCKS * P
    TILES = -(-E // P)
    ETAIL = E - (TILES - 1) * P
    SLOTS = -(-(TILES + FULL) // 16) * 16
    STEPS = SLOTS // U
    RUNS = 4
    RP = SLOTS // RUNS
    FAR = 1 << 14
    AW = D + HEADS
    assert STEPS % 4 == 0 and STEPS > BLOCKS and RP <= P and KC == 2 and HID == P and FULL < BLOCKS

    with ExitStack() as top:
        x_in = top.enter_context(nc.semaphore("x_in"))
        gnn_in = top.enter_context(nc.semaphore("gnn_in"))
        attn_in = top.enter_context(nc.semaphore("attn_in"))
        moe_in = top.enter_context(nc.semaphore("moe_in"))
        route_in = top.enter_context(nc.semaphore("route_in"))
        in_use = []

        def sem(name):
            in_use.append(nc.alloc_semaphore(name=name))
            return in_use[-1]

        def recycle():
            nc.all_engine_barrier()
            nc.clear_and_free_semaphores(in_use)
            nc.all_engine_barrier()
            in_use.clear()

        def keep(name, shape, dt=F32):
            return top.enter_context(nc.sbuf_tensor(name, shape, dt))

        src_d = nc.dram_tensor("src_d", [TILES, P], I32, kind="Internal").ap()
        dst_d = nc.dram_tensor("dst_d", [TILES, P], I32, kind="Internal").ap()
        key_d = nc.dram_tensor("key_d", [SLOTS, P], F32, kind="Internal").ap()
        blk_d = nc.dram_tensor("blk_d", [3, SLOTS], I32, kind="Internal").ap()
        g1_d = nc.dram_tensor("g1_d", [NODES, HID], F32, kind="Internal").ap()
        g2_d = nc.dram_tensor("g2_d", [NODES, HID], F32, kind="Internal").ap()
        kv_d = nc.dram_tensor("kv_d", [NODES, 2 * D], F32, kind="Internal").ap()
        brk_d = nc.dram_tensor("brk_d", [SLOTS + 1, P], F32, kind="Internal").ap()
        link_d = nc.dram_tensor("link_d", [2, SLOTS + 1], F32, kind="Internal").ap()
        first_d = nc.dram_tensor("first_d", [SLOTS], F32, kind="Internal").ap()
        w_d = nc.dram_tensor("w_d", [BLOCKS, P], F32, kind="Internal").ap()

        ident = keep("ident", [P, P])
        ones = keep("ones", [P, P])
        lane = keep("lane", [P, P])
        before = keep("before", [P, P])
        number = keep("number", [P, BLOCKS])
        real = keep("real", [P, BLOCKS])
        last_f = keep("last_f", [1, TILES - 1])
        X = keep("X", [P, BLOCKS, D])
        src_i = keep("src_i", [P, SLOTS], I32)
        dl = keep("dl", [P, SLOTS])
        blk1 = keep("blk1", [1, SLOTS], I32)
        blk2 = keep("blk2", [1, SLOTS], I32)
        blk3 = keep("blk3", [1, SLOTS], I32)
        dinv = keep("dinv", [P, BLOCKS])
        stat = keep("stat", [P, BLOCKS])
        halves = keep("halves", [P, BLOCKS, 6])
        scale = keep("scale", [P, BLOCKS])
        shift = keep("shift", [P, BLOCKS])
        attn = ("skip", "q", "k", "v")
        aw_skip = keep("aw_skip", [P, KC, D])
        ab_skip = keep("ab_skip", [P, D])
        first8 = keep("first8", [HEADS, STEPS])
        link8 = keep("link8", [HEADS, SLOTS + 1])
        pen_f = keep("pen_f", [HEADS, SLOTS])
        pen_b = keep("pen_b", [HEADS, SLOTS])
        EARLY = BLOCKS * D + KC * HID + HID + D + D + 3 * (KC * D + D)
        early = keep("early", [P, EARLY])

        def carver(tile, size):
            used = [0]

            def carve(shape):
                width = prod(shape[1:])
                at = used[0]
                used[0] += width
                assert used[0] <= size
                t = tile[0:shape[0], at:at + width]
                if len(shape) == 3:
                    return t.rearrange("p (i j) -> p i j", j=shape[2])
                if len(shape) == 4:
                    return t.rearrange("p (i j k) -> p i j k", j=shape[2], k=shape[3])
                return t
            return carve
        carve = carver(early, EARLY)
        gw1 = carve([P, KC, HID])
        gb1 = carve([P, HID])
        gw2 = carve([P, 1, D])
        gb2 = carve([P, D])
        aw = [aw_skip] + [carve([P, KC, D]) for m in attn[1:]]
        ab = [ab_skip] + [carve([P, D]) for m in attn[1:]]
        Z = carve([P, BLOCKS, D])

        def rows(t, blocks=BLOCKS):
            return t.rearrange("(b p) f -> p b f", p=P)[:, 0:blocks, :]

        def load_broadcast(eng, tile, vector, done):
            eng.dma_start(tile, vector.rearrange("(o f) -> o f", o=1).broadcast_to([P, vector.shape[0]])).then_inc(done, 16)

        with ExitStack() as ph:
            def sb(name, shape, dt=F32):
                return ph.enter_context(nc.sbuf_tensor(name, shape, dt))

            pb = [ph.enter_context(nc.psum_tensor(f"t_ps{i}", [P, 512], F32)) for i in range(3)]
            last_i = sb("last_i", [1, TILES - 1], I32)
            last_b = sb("last_b", [1, TILES - 1], I32)
            last_s = sb("last_s", [1, TILES - 1])
            tile_no = sb("tile_no", [1, TILES - 1])
            slot_no = sb("slot_no", [P, RUNS])
            less = sb("less", [P, TILES - 1])
            t_f = sb("t_f", [P, RUNS])
            t_i = sb("t_i", [P, RUNS], I32)
            b_f = sb("b_f", [P, RUNS])
            b_m = sb("b_m", [P, RUNS])
            b_i = sb("b_i", [P, 3, RUNS], I32)
            pad = sb("pad", [1, 2, P], I32)
            ed = sb("ed", [P, RUNS, P], I32)
            es = sb("es", [P, RUNS, P], I32)
            edf = sb("edf", [P, RUNS, P])
            esf = sb("esf", [P, RUNS, P])
            edl = sb("edl", [P, RUNS, P])
            inside = sb("inside", [P, RUNS, P])
            key = sb("key", [P, RUNS, P])
            last_in, pad_set, edges_out = sem("last_in"), sem("pad_set"), sem("edges_out")
            const_set, id_zero, x_zero = sem("const_set"), sem("id_zero"), sem("x_zero")
            t_chain, last_set, spread, t_set, tiles_in = (
                sem("t_chain"), sem("last_set"), sem("spread"), sem("t_set"), sem("tiles_in"))
            b_set, key_set, tables_out, turned, tables_in, copied = (
                sem("b_set"), sem("key_set"), sem("tables_out"), sem("turned"), sem("tables_in"), sem("copied"))
            block = ph.enter_context(nc.Block())

            @block.sync
            def _(sp):
                sp.dma_start(last_i[:, :], a["dst"][0:(TILES - 1) * P].rearrange("(t e) -> e t", e=P)[P - 1:P, :],
                             allow_slow_non_contiguous=True).then_inc(last_in, 16)
                for t, d in (("src", src_d), ("dst", dst_d)):
                    sp.dma_start(d[0:TILES - 1, :], a[t][0:(TILES - 1) * P].rearrange("(t e) -> t e", e=P))\
                        .then_inc(edges_out, 16)
                    sp.dma_start(d[TILES - 1:TILES, 0:ETAIL], a[t][(TILES - 1) * P:E].rearrange("(o e) -> o e", o=1))\
                        .then_inc(edges_out, 16)
                sp.wait_ge(pad_set, 2)
                if ETAIL < P:
                    sp.dma_start(src_d[TILES - 1:TILES, ETAIL:P], pad[:, 0, ETAIL:P]).then_inc(edges_out, 16)
                    sp.dma_start(dst_d[TILES - 1:TILES, ETAIL:P], pad[:, 1, ETAIL:P]).then_inc(edges_out, 16)
                sp.wait_ge(b_set, 3)
                for m in range(3):
                    sp.dma_start(blk_d[m, :].rearrange("(r p) -> p r", p=RP), b_i[0:RP, m, :],
                                 allow_slow_non_contiguous=True).then_inc(tables_out, 16)
                sp.wait_ge(key_set, 1)
                sp.dma_start(key_d.rearrange("(r p) e -> p r e", p=RP), key[0:RP, :, :]).then_inc(tables_out, 16)
                sp.dma_start(first_d.rearrange("(r p) -> p r", p=RP), edl[0:RP, :, 0],
                             allow_slow_non_contiguous=True).then_inc(tables_out, 16)
                sp.wait_ge(tables_out, 80)
                for m, t in enumerate((blk1, blk2, blk3)):
                    sp.dma_start(t[:, :], blk_d[m:m + 1, :]).then_inc(tables_in, 16)
                sp.wait_ge(tables_in, 48)
                sp.wait_ge(edges_out, 96 if ETAIL < P else 64)

            @block.scalar
            def _(act):
                act.wait_ge(x_zero, 1)
                act.dma_start(X[:, 0:FULL, :], a["x"][0:FULL * P, :].rearrange("(b p) f -> p b f", p=P)).then_inc(x_in, 16)
                act.dma_start(X[0:TAIL, FULL, :], a["x"][FULL * P:N, :]).then_inc(x_in, 16)
                act.dma_start(gw1[:, :, :], a["L0_gnn_W1"].rearrange("(c p) f -> p c f", p=P)).then_inc(gnn_in, 16)
                act.dma_start(gw2[:, :, :], a["L0_gnn_W2"].rearrange("(c p) f -> p c f", p=P)).then_inc(gnn_in, 16)
                load_broadcast(act, gb1[:, :], a["L0_gnn_b1"], gnn_in)
                load_broadcast(act, gb2[:, :], a["L0_gnn_b2"], gnn_in)
                for m, name in enumerate(attn):
                    act.dma_start(aw[m][:, :, :], a["L1_gnn_W" + name].rearrange("(c p) f -> p c f", p=P)).then_inc(attn_in, 16)
                    load_broadcast(act, ab[m][:, :], a["L1_gnn_b" + name], attn_in)
                act.wait_ge(turned, 2 * RUNS)
                nc.scalar.activation(dl[:, :], pb[1][:, 0:SLOTS], ACT.Copy).then_inc(copied, 1)
                nc.scalar.activation(src_i[:, :], pb[2][:, 0:SLOTS], ACT.Copy).then_inc(copied, 1)
                act.wait_ge(copied, 2)
                act.wait_ge(x_in, 32)
                act.wait_ge(gnn_in, 64)

            @block.gpsimd
            def _(pool):
                pool.memset(pad[:, 0, :], 0).then_inc(pad_set, 1)
                pool.memset(pad[:, 1, :], FAR).then_inc(pad_set, 1)
                pool.memset(X[:, FULL:BLOCKS, :], 0.0).then_inc(x_zero, 1)
                pool.memset(ones[:, :], 1.0).then_inc(const_set, 1)
                pool.iota(tile_no[:, :], pattern=[[1, TILES - 1]], base=0, channel_multiplier=0,
                          allow_small_or_imprecise_dtypes=True).then_inc(const_set, 1)
                pool.iota(slot_no[:, :], pattern=[[RP, RUNS]], base=0, channel_multiplier=1,
                          allow_small_or_imprecise_dtypes=True).then_inc(const_set, 1)
                pool.iota(lane[:, :], pattern=[[1, P]], base=0, channel_multiplier=0,
                          allow_small_or_imprecise_dtypes=True).then_inc(const_set, 1)
                pool.iota(number[:, :], pattern=[[P, BLOCKS]], base=0, channel_multiplier=1,
                          allow_small_or_imprecise_dtypes=True).then_inc(const_set, 1)
                pool.memset(before[:, :], 1.0).then_inc(id_zero, 1)
                pool.memset(ident[:, :], 0.0).then_inc(id_zero, 1)
                pool.wait_ge(id_zero, 2)
                pool.affine_select(out=before[:, :], in_=before[:, :], compare_op=ALU.is_gt, fill=0.0,
                                   base=0, pattern=[[1, P]], channel_multiplier=-1).then_inc(const_set, 1)
                pool.affine_select(out=ident[:, :], in_=ident[:, :], compare_op=ALU.not_equal, fill=1.0,
                                   base=0, pattern=[[-1, P]], channel_multiplier=1).then_inc(const_set, 1)
                pool.wait_ge(edges_out, 96 if ETAIL < P else 64)
                pool.wait_ge(t_set, 1)
                for r in range(RUNS):
                    at = bass.IndirectOffsetOnAxis(ap=t_i[0:RP, r:r + 1], axis=0)
                    pool.indirect_dma_start(ed[0:RP, r, :], None, dst_d[:, :], at).then_inc(tiles_in, 16)
                    pool.indirect_dma_start(es[0:RP, r, :], None, src_d[:, :], at).then_inc(tiles_in, 16)

            @block.vector
            def _(dve):
                link = Chain(dve, t_chain)
                dve.wait_ge(last_in, 16)
                link(nc.vector.tensor_scalar(last_b[:, :], last_i[:, :], 7, None, ALU.arith_shift_right))
                link(nc.vector.tensor_copy(last_s[:, :], last_b[:, :]))
                link(nc.vector.tensor_copy(last_f[:, :], last_i[:, :]))
                dve.wait_ge(const_set, 7)
                link(nc.vector.tensor_scalar(real[:, :], number[:, :], float(N), None, ALU.is_lt))
                nc.vector.tensor_tensor(last_s[:, :], last_s[:, :], tile_no[:, :], ALU.add).then_inc(last_set, 1)
                dve.wait_ge(spread, 1)
                for r in range(RUNS):
                    link(nc.vector.tensor_scalar(less[0:RP, :], pb[0][0:RP, 0:TILES - 1], slot_no[0:RP, r:r + 1], None,
                                                 ALU.is_lt))
                    link(nc.vector.tensor_reduce(t_f[0:RP, r:r + 1], less[0:RP, :], AX.X, ALU.add))
                nc.vector.tensor_copy(t_i[0:RP, :], t_f[0:RP, :]).then_inc(t_set, 1)
                link(nc.vector.tensor_tensor(b_f[0:RP, :], slot_no[0:RP, :], t_f[0:RP, :], ALU.subtract))
                for m, width in enumerate((P, D, AW)):
                    nc.vector.tensor_scalar(b_i[0:RP, m, :], b_f[0:RP, :], float(width), None, ALU.mult).then_inc(b_set, 1)
                link(nc.vector.tensor_scalar(b_m[0:RP, :], b_f[0:RP, :], -float(P), None, ALU.mult))
                dve.wait_ge(tiles_in, 2 * RUNS * 16)
                link(nc.vector.tensor_copy(edf[0:RP, :, :], ed[0:RP, :, :]))
                link(nc.vector.tensor_copy(esf[0:RP, :, :], es[0:RP, :, :]))
                link(nc.vector.tensor_tensor(edl[0:RP, :, :], edf[0:RP, :, :],
                                             b_m[0:RP, :].unsqueeze(2).broadcast_to([RP, RUNS, P]), ALU.add))
                link(nc.vector.tensor_scalar(inside[0:RP, :, :], edl[0:RP, :, :], 0.0, None, ALU.is_ge))
                link(nc.vector.scalar_tensor_tensor(out=inside[0:RP, :, :], in0=edl[0:RP, :, :], scalar=float(P),
                                                    in1=inside[0:RP, :, :], op0=ALU.is_lt, op1=ALU.mult))
                nc.vector.scalar_tensor_tensor(out=key[0:RP, :, :], in0=edf[0:RP, :, :], scalar=1.0,
                                               in1=inside[0:RP, :, :], op0=ALU.add, op1=ALU.mult).then_inc(key_set, 1)

            @block.tensor
            def _(pe):
                pe.wait_ge(last_set, 1)
                nc.tensor.matmul(pb[0][:, 0:TILES - 1], ones[0:1, :], last_s[:, :], start=True, stop=True).then_inc(spread, 1)
                pe.wait_ge(key_set, 1)
                for m, t in ((1, edl), (2, esf)):
                    for r in range(RUNS):
                        nc.tensor.transpose(pb[m][:, r * RP:(r + 1) * RP], t[0:RP, r, :], ident[0:RP, 0:RP])\
                            .then_inc(turned, 1)

        def stats_of(in_t, b):
            return nc.vector.bn_stats(halves[:, bass.ds(b, 1), :].rearrange("p o f -> p (o f)"),
                                      in_t[:, bass.ds(b, 1), :].rearrange("p o f -> p (o f)"))

        def norm_ends(dve, link, var_set, root_set):
            even, odd = halves[:, :, 1], halves[:, :, 4]
            link(nc.vector.tensor_tensor(scale[:, :], even, odd, ALU.subtract))
            link(nc.vector.tensor_tensor(scale[:, :], scale[:, :], scale[:, :], ALU.mult))
            link(nc.vector.tensor_tensor(stat[:, :], halves[:, :, 2], halves[:, :, 5], ALU.add))
            link(nc.vector.tensor_scalar(stat[:, :], stat[:, :], 1.0 / D, EPS, ALU.mult, ALU.add))
            nc.vector.scalar_tensor_tensor(out=stat[:, :], in0=scale[:, :], scalar=0.25, in1=stat[:, :],
                                           op0=ALU.mult, op1=ALU.add).then_inc(var_set, 1)
            link(nc.vector.tensor_tensor(shift[:, :], even, odd, ALU.add))
            dve.wait_ge(root_set, 1)
            link(nc.vector.reciprocal(scale[:, :], stat[:, :]))
            link(nc.vector.scalar_tensor_tensor(out=shift[:, :], in0=shift[:, :], scalar=-0.5, in1=scale[:, :],
                                                op0=ALU.mult, op1=ALU.mult))

        def norm_stats(phase):
            with ExitStack() as ph:
                chain, var_set, root_set = sem(f"{phase}_chain"), sem(f"{phase}_var"), sem(f"{phase}_root")
                block = ph.enter_context(nc.Block())

                @block.vector
                def _(dve):
                    norm_ends(dve, Chain(dve, chain), var_set, root_set)

                @block.scalar
                def _(act):
                    act.wait_ge(var_set, 1)
                    nc.scalar.activation(stat[:, :], stat[:, :], ACT.Sqrt).then_inc(root_set, 1)

        with ExitStack() as ph:
            def sb(name, shape, dt=F32):
                return ph.enter_context(nc.sbuf_tensor(name, shape, dt))

            passed = sb("d_passed", [P, 2, TILES - 1])
            tiles_f = sb("d_tiles_f", [P, BLOCKS])
            tiles_i = sb("d_tiles_i", [P, BLOCKS], I32)
            nexts = sb("d_nexts", [P, BLOCKS, P], I32)
            within = sb("d_within", [P, BLOCKS, P])
            ends = sb("d_ends", [P, BLOCKS])
            key = sb("d_key", [P, RUNS, P])
            key_prev = sb("key_prev", [P, RUNS])
            brk = sb("brk", [P, RUNS, P])
            last_brk = sb("last_brk", [1, P])
            parts = sb("parts", [P, RUNS])
            up = sb("d_up", [P, P])
            corner = sb("d_corner", [P, P])
            pl = ph.enter_context(nc.psum_tensor("d_pl", [P, 512], F32))
            pp = ph.enter_context(nc.psum_tensor("d_pp", [P, 512], F32))
            (spread, tiles_set, counted, blank, moves_set, rows_in, ends_set, moved, deg_set, deg_root, chain, n_chain,
             var_set, root_set) = (sem(f"d_{n}") for n in (
                 "spread", "tiles_set", "counted", "blank", "moves_set", "rows_in", "ends_set", "moved", "deg_set",
                 "deg_root", "chain", "n_chain", "var_set", "root_set"))
            no_prev, prev_in, brk_set, brk_out, first_in = (
                sem("no_prev"), sem("prev_in"), sem("brk_set"), sem("brk_out"), sem("first_in"))
            key_in = sem("key_in")
            block = ph.enter_context(nc.Block())

            @block.sync
            def _(sp):
                sp.dma_start(key[0:RP, :, :], key_d.rearrange("(r p) e -> p r e", p=RP)).then_inc(key_in, 16)
                sp.wait_ge(no_prev, 1)
                for r in range(RUNS):
                    lo = 1 if r == 0 else 0
                    sp.dma_start(key_prev[lo:RP, r:r + 1], key_d[r * RP + lo - 1:(r + 1) * RP - 1, P - 1:P],
                                 allow_slow_non_contiguous=True).then_inc(prev_in, 16)
                sp.dma_start(first8[:, :], first_d.rearrange("(c k) -> k c", k=U)[0:1, :].broadcast_to([HEADS, STEPS]),
                             allow_slow_non_contiguous=True).then_inc(first_in, 16)
                sp.wait_ge(brk_set, 2)
                sp.dma_start(brk_d[0:SLOTS, :].rearrange("(r p) e -> p r e", p=RP), brk[0:RP, :, :]).then_inc(brk_out, 16)
                sp.dma_start(brk_d[SLOTS:SLOTS + 1, :], last_brk[:, :]).then_inc(brk_out, 16)
                for r in range(RUNS):
                    sp.dma_start(link_d[0, r * RP:(r + 1) * RP].rearrange("(p o) -> p o", o=1), brk[0:RP, r, 0:1],
                                 allow_slow_non_contiguous=True).then_inc(brk_out, 16)
                sp.dma_start(link_d[0:1, SLOTS:SLOTS + 1], last_brk[:, 0:1]).then_inc(brk_out, 16)
                sp.wait_ge(brk_set, 3)
                sp.dma_start(link_d[1, 0:SLOTS].rearrange("(r p) -> p r", p=RP), parts[0:RP, :],
                             allow_slow_non_contiguous=True).then_inc(brk_out, 16)
                sp.wait_ge(brk_out, 16 * (4 + RUNS))
                sp.dma_start(link8[:, :], link_d[0:1, :].broadcast_to([HEADS, SLOTS + 1])).then_inc(first_in, 16)
                sp.dma_start(pen_f[:, :], link_d[1:2, 0:SLOTS].broadcast_to([HEADS, SLOTS])).then_inc(first_in, 16)
                sp.wait_ge(first_in, 48)

            @block.tensor
            def _(pe):
                nc.tensor.matmul(pl[:, 0:TILES - 1], ones[0:1, :], last_f[:, :], start=True, stop=True).then_inc(spread, 1)
                pe.wait_ge(moves_set, 2)
                pe.wait_ge(ends_set, 1)
                nc.tensor.matmul(pp[:, 0:BLOCKS], up[:, :], ends[:, :], start=True, stop=False, skip_group_check=True)
                nc.tensor.matmul(pp[:, 1:BLOCKS], corner[:, :], ends[:, 0:BLOCKS - 1], start=False, stop=True,
                                 skip_group_check=True).then_inc(moved, 1)

            @block.gpsimd
            def _(pool):
                pool.memset(up[:, :], 0.0).then_inc(blank, 1)
                pool.memset(corner[:, :], 0.0).then_inc(blank, 1)
                pool.wait_ge(blank, 2)
                pool.affine_select(out=up[:, :], in_=up[:, :], compare_op=ALU.not_equal, fill=1.0,
                                   base=1, pattern=[[-1, P]], channel_multiplier=1).then_inc(moves_set, 1)
                pool.affine_select(out=corner[:, :], in_=corner[:, :], compare_op=ALU.not_equal, fill=1.0,
                                   base=-(P - 1), pattern=[[-1, P]], channel_multiplier=1).then_inc(moves_set, 1)
                pool.wait_ge(tiles_set, 1)
                for b in range(BLOCKS):
                    pool.indirect_dma_start(nexts[:, b, :], None, dst_d[:, :],
                                            bass.IndirectOffsetOnAxis(ap=tiles_i[:, b:b + 1], axis=0)).then_inc(rows_in, 16)

            @block.vector
            def _(dve):
                link = Chain(dve, chain)
                nc.vector.memset(key_prev[0:1, 0:1], -1.0).then_inc(no_prev, 1)
                nc.vector.memset(last_brk[:, :], -BIG).then_inc(brk_set, 1)
                dve.wait_ge(spread, 1)

                def count(b, k):
                    wait_count(dve, counted, b - 1)
                    nc.vector.tensor_scalar(passed[:, k, :], pl[:, 0:TILES - 1], number[:, bass.ds(b, 1)], 0.0, ALU.is_le,
                                            ALU.add, accum_out=tiles_f[:, bass.ds(b, 1)]).then_inc(counted, 1)
                count(0, 0)
                count(1, 1)
                with dve.Fori(1, PAIRS) as i:
                    for k in range(2):
                        count(2 * i + k, k)
                dve.wait_ge(counted, BLOCKS)
                nc.vector.tensor_copy(tiles_i[:, :], tiles_f[:, :]).then_inc(tiles_set, 1)
                with dve.Fori(0, BLOCKS) as b:
                    stats_of(X, b).then_inc(counted, 1)
                dve.wait_ge(counted, 2 * BLOCKS)
                norm_ends(dve, Chain(dve, n_chain), var_set, root_set)
                dve.wait_ge(key_in, 16)
                link(nc.vector.tensor_tensor(brk[0:RP, :, 1:P], key[0:RP, :, 1:P], key[0:RP, :, 0:P - 1], ALU.not_equal))
                dve.wait_ge(prev_in, 16 * RUNS)
                link(nc.vector.tensor_tensor(brk[0:RP, :, 0:1], key[0:RP, :, 0:1], key_prev[0:RP, :].unsqueeze(2),
                                             ALU.not_equal))
                nc.vector.tensor_scalar(brk[0:RP, :, :], brk[0:RP, :, :], -BIG, None, ALU.mult).then_inc(brk_set, 1)
                link(nc.vector.tensor_tensor(parts[0:RP, :].unsqueeze(2), key[0:RP, :, 0:1], key[0:RP, :, P - 1:P],
                                             ALU.not_equal))
                nc.vector.tensor_scalar(parts[0:RP, :], parts[0:RP, :], -BIG, None, ALU.mult).then_inc(brk_set, 1)
                dve.wait_ge(rows_in, 16 * BLOCKS)
                link(nc.vector.tensor_tensor(within[:, :, :], nexts[:, :, :],
                                             number[:, :].unsqueeze(2).broadcast_to([P, BLOCKS, P]), ALU.is_le))
                link(nc.vector.tensor_reduce(ends[:, :], within[:, :, :], AX.X, ALU.add))
                nc.vector.scalar_tensor_tensor(out=ends[:, :], in0=tiles_f[:, :], scalar=float(P), in1=ends[:, :],
                                               op0=ALU.mult, op1=ALU.add).then_inc(ends_set, 1)
                dve.wait_ge(ends_set, 1)
                dve.wait_ge(moved, 1)
                nc.vector.scalar_tensor_tensor(out=dinv[:, :], in0=ends[:, :], scalar=1.0, in1=pp[:, 0:BLOCKS],
                                               op0=ALU.add, op1=ALU.subtract).then_inc(deg_set, 1)
                dve.wait_ge(deg_root, 1)
                link(nc.vector.reciprocal(dinv[:, :], dinv[:, :]))

            @block.scalar
            def _(act):
                act.wait_ge(var_set, 1)
                nc.scalar.activation(stat[:, :], stat[:, :], ACT.Sqrt).then_inc(root_set, 1)
                act.wait_ge(deg_set, 1)
                nc.scalar.activation(dinv[:, :], dinv[:, :], ACT.Sqrt).then_inc(deg_root, 1)

        recycle()

        def project(phase, in_t, kc, weights, evacuate, parts, norm_of=None, save_t=None, stores=(),
                    ringed=None, meanwhile=None, keeps=True):
            with ExitStack() as ph:
                stage = ph.enter_context(nc.sbuf_tensor(f"{phase}_stage", [P, 2, kc, P], F32))
                zt = ph.enter_context(nc.sbuf_tensor(f"{phase}_zt", [P, 2, kc, P], F32))
                pt = [ph.enter_context(nc.psum_tensor(f"{phase}_pt{k}", [P, kc, P], F32)) for k in range(2)]
                width = sum(w for _, w in weights)
                banks = -(-width // 512)
                po = [ph.enter_context(nc.psum_tensor(f"{phase}_po{k}", [P, banks * 512], F32)) for k in range(2)]
                staged, turned_, zt_set, product, taken = (
                    sem(f"{phase}_staged"), sem(f"{phase}_turned"), sem(f"{phase}_zt"), sem(f"{phase}_product"),
                    sem(f"{phase}_taken"))
                chain, kept, stored = sem(f"{phase}_chain"), sem(f"{phase}_kept"), sem(f"{phase}_stored")
                sent = [sem(f"{phase}_sent{k}") for k in range(2)]
                block = ph.enter_context(nc.Block())

                if stores:
                    @block.sync
                    def _(sp):
                        with sp.Fori(0, BLOCKS) as b:
                            sp.wait_ge(taken, b + 1)
                            for table, t in stores:
                                sp.dma_start(table[bass.ds(b * P, P), :], t[:, bass.ds(b, 1), :].rearrange("p o f -> p (o f)"))\
                                    .then_inc(stored, 16)
                        sp.wait_ge(stored, 16 * BLOCKS * len(stores))

                if meanwhile:
                    @block.sync
                    def _(sp):
                        meanwhile(sp)

                if ringed:
                    tile, tables = ringed

                    @block.sync
                    def _(sp):
                        with sp.Fori(0, PAIRS) as i:
                            for k in range(2):
                                b = 2 * i + k
                                sp.wait_ge(taken, b + 1)
                                for m, table in enumerate(tables):
                                    sp.dma_start(table[bass.ds(b * P, P), :], tile[:, k, m, :]).then_inc(sent[k], 16)
                        for k in range(2):
                            sp.wait_ge(sent[k], 16 * len(tables) * PAIRS)

                @block.tensor
                def _(pe):
                    def turn(b, k):
                        pe.wait_ge(staged, b + 1)
                        wait_count(pe, zt_set, b - 1)
                        for c in range(kc):
                            last = nc.tensor.transpose(pt[k][:, c, :], stage[:, k, c, :], ident[:, :])
                        last.then_inc(turned_, 1)

                    def multiply(b, k):
                        pe.wait_ge(zt_set, b + 1)
                        wait_count(pe, taken, b - 1)
                        at = 0
                        for w, n in weights:
                            for c in range(kc):
                                last = nc.tensor.matmul(po[k][:, at:at + n], zt[:, k, c, :], w[:, c, :],
                                                        start=(c == 0), stop=(c == kc - 1))
                            at += n
                        last.then_inc(product, 1)
                    turn(0, 0)
                    turn(1, 1)
                    multiply(0, 0)
                    with pe.Fori(1, PAIRS) as i:
                        turn(2 * i, 0)
                        multiply(2 * i - 1, 1)
                        turn(2 * i + 1, 1)
                        multiply(2 * i, 0)
                    multiply(BLOCKS - 1, 1)

                @block.scalar
                def _(act):
                    def fetch(b, k):
                        to = stage[:, k:k + 1, :, :].rearrange("p o c f -> p o (c f)")
                        if norm_of is None:
                            nc.scalar.activation(to, in_t[:, bass.ds(b, 1), :], ACT.Copy).then_inc(staged, 1)
                        else:
                            if keeps:
                                wait_count(act, kept, b - 1)
                            nc.scalar.activation(to, norm_of[:, bass.ds(b, 1), :], ACT.Identity,
                                                 scale=scale[:, bass.ds(b, 1)], bias=shift[:, bass.ds(b, 1)]).then_inc(staged, 1)

                    def step(i, more):
                        for k in range(2):
                            b = 2 * i + k
                            act.wait_ge(turned_, b + 1)
                            wait_count(act, product, b - 1)
                            nc.scalar.activation(zt[:, k, :, :], pt[k][:, :, :], ACT.Copy).then_inc(zt_set, 1)
                            if more:
                                fetch(b + 2, k)
                            if save_t is not None:
                                act.wait_ge(zt_set, b + 1)
                                nc.scalar.activation(save_t[:, :, bass.ds(b * P, P)], zt[:, k, :, :], ACT.Copy)
                    fetch(0, 0)
                    fetch(1, 1)
                    step(0, True)
                    with act.Fori(1, PAIRS - 1) as i:
                        step(i, True)
                    step(PAIRS - 1, False)

                @block.vector
                def _(dve):
                    def keep_row(b, k):
                        if norm_of is not None and keeps:
                            dve.wait_ge(staged, b + 1)
                            nc.vector.tensor_copy(in_t[:, bass.ds(b, 1), :].rearrange("p o (c f) -> p (o c) f", c=kc),
                                                  stage[:, k, :, :]).then_inc(kept, 1)

                    def step(i, more=True):
                        for k in range(2):
                            b = 2 * i + k
                            if more or k == 0:
                                keep_row(b + 1, 1 - k)
                            dve.wait_ge(product, b + 1)
                            if ringed:
                                wait_count(dve, sent[k], 16 * len(ringed[1]) * i)
                                evacuate(dve, b, po[k], chain, parts * b, k).then_inc(taken, 1)
                            else:
                                evacuate(dve, b, po[k], chain, parts * b).then_inc(taken, 1)
                    keep_row(0, 0)
                    step(0)
                    with dve.Fori(1, PAIRS - 1) as i:
                        step(i)
                    step(PAIRS - 1, False)

        def convolve(phase, table, own, finish, turned_out=False, in_step=None):
            with ExitStack() as ph:
                oh = ph.enter_context(nc.sbuf_tensor(f"{phase}_oh", [P, U, P], F32))
                ring = ph.enter_context(nc.sbuf_tensor(f"{phase}_ring", [P, U, HID], F32))
                ix = ph.enter_context(nc.sbuf_tensor(f"{phase}_ix", [P, U], I32))
                acc = ph.enter_context(nc.psum_tensor(f"{phase}_acc", [P, 8 * 512], F32))
                landed = [sem(f"{phase}_landed{k}") for k in range(U)]
                may_gather = sem(f"{phase}_may_gather")
                oh_ready, ix_ready, summed = sem(f"{phase}_oh_ready"), sem(f"{phase}_ix_ready"), sem(f"{phase}_summed")
                block = ph.enter_context(nc.Block())
                last_steps = finish(block, acc, summed)

                @block.gpsimd
                def _(pool):
                    def step(it):
                        for h in range(2):
                            pool.wait_ge(ix_ready, 2 * it + h + 1)
                            pool.sem_inc(may_gather, 1)
                            for k in range(HALF * h, HALF * (h + 1)):
                                pool.indirect_dma_start(
                                    ring[:, k, :], None, table[:, :],
                                    bass.IndirectOffsetOnAxis(ap=ix[:, k:k + 1], axis=0)).then_inc(landed[k], 16)
                    with pool.Fori(0, STEPS) as it:
                        step(it)

                @block.vector
                def _(dve):
                    def step(it):
                        for h in range(2):
                            mine = slice(HALF * h, HALF * (h + 1))
                            wait_count(dve, summed, U * it + HALF * (h + 1) - U)
                            nc.vector.tensor_copy(ix[:, mine], src_i[:, bass.ds(U * it + HALF * h, HALF)]).then_inc(ix_ready, 1)
                            nc.vector.tensor_tensor(
                                oh[:, mine, :], lane[:, :].unsqueeze(1).broadcast_to([P, HALF, P]),
                                dl[:, bass.ds(U * it + HALF * h, HALF)].unsqueeze(2).broadcast_to([P, HALF, P]),
                                ALU.is_equal).then_inc(oh_ready, 1)
                    step(0)
                    alone = 1
                    if in_step is not None:
                        alone = BLOCKS + 1
                        with dve.Fori(1, alone) as it:
                            step(it)
                            in_step(it - 1)
                    with dve.Fori(alone, STEPS) as it:
                        step(it)
                    dve.wait_ge(summed, SLOTS)
                    last_steps(dve)

                @block.tensor
                def _(pe):
                    per_bank = 512 // HID
                    for b in range(0, BLOCKS, per_bank):
                        n = min(per_bank, BLOCKS - b)
                        if not turned_out:
                            nc.tensor.matmul(acc[:, b * HID:(b + n) * HID], ident[:, :], own[:, b:b + n, :],
                                             start=True, stop=False, skip_group_check=True)
                        else:
                            for m in range(b, b + n):
                                nc.tensor.matmul(acc[:, m * P:(m + 1) * P], own[:, m, :], ident[:, :],
                                                 start=(m == b), stop=False, skip_group_check=True)

                    def step(it):
                        _, at = nc.values_load_multi_w_load_instructions(
                            blk1[0:1, bass.ds(U * it, U)], engines=PE_ONLY, min_val=0, max_val=(BLOCKS - 1) * P,
                            skip_runtime_bounds_check_because="a slot's block is below BLOCKS")
                        for k in range(U):
                            if k % HALF == 0:
                                pe.wait_ge(oh_ready, 2 * it + k // HALF + 1)
                            pe.wait_ge(landed[k], 16 * it + 16)
                            rows_, nodes = ring[:, k, :], oh[:, k, :]
                            nc.tensor.matmul(acc[:, bass.ds(at[k], HID)], *((rows_, nodes) if turned_out else (nodes, rows_)),
                                             start=False, stop=False, skip_group_check=True).then_inc(summed, 1)
                    step(0)
                    with pe.Fori(1, STEPS) as it:
                        step(it)

        MT = (2 * N + EXP * (P - 1)) // P
        MT += MT % 2
        HC = EH // P
        GROUP = 5
        PART = KC * EH
        assert HC * D == PART and (FULL + 1) % GROUP == 0
        zs_d = nc.dram_tensor("zs_d", [(MT + 2) * P, D], F32, kind="Internal").ap()
        y_d = nc.dram_tensor("y_d", [(MT + 2) * P, D], F32, kind="Internal").ap()
        with ExitStack() as ph:
            def sb(name, shape, dt=F32):
                return ph.enter_context(nc.sbuf_tensor(name, shape, dt))

            w1 = sb("m_w1", [P, EXP * PART])
            w2 = sb("m_w2", [P, EXP * PART])
            b1 = sb("m_b1", [P, EXP * EH])
            b2 = sb("m_b2", [P, EXP * D])
            wg = sb("m_wg", [P, KC, EXP])
            bg = sb("m_bg", [P, EXP])
            bias = sb("m_bias", [P, EXP])
            zero = sb("m_zero", [P, D])
            logit = sb("m_logit", [P, BLOCKS, EXP])
            rest = sb("m_rest", [P, BLOCKS, EXP])
            order = sb("m_order", [P, BLOCKS, EXP])
            pick = [sb(f"m_pick{i}", [P, BLOCKS, EXP]) for i in range(2)]
            both = sb("m_both", [P, BLOCKS, EXP])
            top_v = [sb(f"m_top{i}", [P, BLOCKS]) for i in range(2)]
            share = [sb(f"m_share{i}", [P, BLOCKS]) for i in range(2)]
            place_i = sb("m_place_i", [P, BLOCKS, 2], I32)
            expert_of = sb("m_expert_of", [1, MT + 2], I32)

            zero_set = sem("m_zero_set")

            ZT = 8
            ZERO_PARTS = -(-(MT + 2) // ZT)

            def moe_loads(sp, summed):
                sp.dma_start(wg[:, :, :], a["L0_ffn_Wg"].rearrange("(c p) f -> p c f", p=P)).then_inc(moe_in, 16)
                load_broadcast(sp, bg[:, :], a["L0_ffn_bg"], moe_in)
                load_broadcast(sp, bias[:, :], a["L0_ffn_bias"], moe_in)
                for e in range(EXP):
                    sp.wait_ge(summed, SLOTS // (2 * EXP) * e + 1)
                    sp.dma_start(w1[:, e * PART:(e + 1) * PART].rearrange("p (c f) -> p c f", c=KC),
                                 a["L0_ffn_W1"][e].rearrange("(c p) f -> p c f", p=P)).then_inc(moe_in, 16)
                    sp.dma_start(w2[:, e * PART:(e + 1) * PART].rearrange("p (c f) -> p c f", c=HC),
                                 a["L0_ffn_W2"][e].rearrange("(c p) f -> p c f", p=P)).then_inc(moe_in, 16)
                sp.wait_ge(summed, SLOTS // 2)
                load_broadcast(sp, b1[:, :], a["L0_ffn_b1"].rearrange("e f -> (e f)"), moe_in)
                sp.wait_ge(summed, SLOTS // 2 + SLOTS // (6 * ZERO_PARTS))
                load_broadcast(sp, b2[:, :], a["L0_ffn_b2"].rearrange("e f -> (e f)"), moe_in)
                sp.wait_ge(zero_set, 1)
                for n, t in enumerate(range(0, MT + 2, ZT)):
                    m = min(ZT, MT + 2 - t)
                    sp.wait_ge(summed, SLOTS // 2 + SLOTS // (3 * ZERO_PARTS) * n)
                    sp.dma_start(zs_d.rearrange("(t p) f -> p t f", p=P)[:, t:t + m, :],
                                 zero[:, :].unsqueeze(1).broadcast_to([P, m, D])).then_inc(moe_in, 16)
                sp.dma_start(y_d[MT * P:(MT + 2) * P, :].rearrange("(t p) f -> p t f", p=P),
                             zero[:, :].unsqueeze(1).broadcast_to([P, 2, D])).then_inc(moe_in, 16)

            with ExitStack() as ph:
                G = ph.enter_context(nc.sbuf_tensor("G", [P, BLOCKS, HID], F32))
                A = Z[:, :, 0:HID]

                with ExitStack() as ph2:
                    block = ph2.enter_context(nc.Block())

                    @block.gpsimd
                    def _(pool):
                        pool.memset(zero[:, :], 0.0).then_inc(zero_set, 1)

                project("h1", Z, KC, [(gw1, HID)], lambda dve, b, po, chain, at: nc.vector.tensor_scalar(
                    G[:, bass.ds(b, 1), :], po[:, 0:HID].unsqueeze(1), dinv[:, bass.ds(b, 1)], None, ALU.mult), 0, norm_of=X,
                    stores=[(g1_d, G)], keeps=False)
                biased, rows_set, rows_out = sem("biased"), sem("rows_set"), sem("rows_out")

                def finish_first(block, acc, summed):
                    @block.sync
                    def _(sp):
                        moe_loads(sp, summed)
                        some = -(-BLOCKS // 4)
                        for lo in range(0, BLOCKS, some):
                            hi = min(lo + some, BLOCKS)
                            sp.wait_ge(rows_set, hi)
                            sp.dma_start(rows(g2_d)[:, lo:hi, :], G[:, lo:hi, :]).then_inc(rows_out, 16)
                        sp.wait_ge(rows_out, 16 * -(-BLOCKS // some))

                    @block.scalar
                    def _(act):
                        with act.Fori(0, BLOCKS) as b:
                            one = bass.ds(b, 1)
                            act.wait_ge(biased, b + 1)
                            nc.scalar.activation(G[:, one, :], A[:, one, :], ACT.Relu, scale=dinv[:, one]).then_inc(rows_set, 1)

                    def last_steps(dve):
                        with dve.Fori(0, BLOCKS) as b:
                            one = bass.ds(b, 1)
                            nc.vector.scalar_tensor_tensor(out=A[:, one, :], in0=acc[:, bass.ds(b * HID, HID)].unsqueeze(1),
                                                           scalar=dinv[:, one], in1=gb1[:, :].unsqueeze(1), op0=ALU.mult,
                                                           op1=ALU.add).then_inc(biased, 1)
                    return last_steps
                convolve("cv1", g1_d, G, finish_first)

                AT = Z[:, :, HID:2 * HID]
                at_set = sem("at_set")

                def finish_second(block, acc, summed):
                    here = BLOCKS // 2 // 4 * 4

                    def part(lo, hi):
                        return AT[:, lo:hi, :], acc[:, lo * P:hi * P].rearrange("p (b f) -> p b f", f=P)

                    @block.scalar
                    def _(act):
                        act.wait_ge(summed, SLOTS)
                        nc.scalar.activation(*part(here, BLOCKS), ACT.Copy).then_inc(at_set, 1)

                    def last_steps(dve):
                        nc.vector.tensor_copy(*part(0, here)).then_inc(at_set, 1)
                    return last_steps

                def add_gb2(b):
                    one = bass.ds(b, 1)
                    nc.vector.tensor_tensor(X[:, one, :], X[:, one, :], gb2[:, :].unsqueeze(1), ALU.add)
                convolve("cv2", g2_d, G, finish_second, turned_out=True, in_step=add_gb2)

                with ExitStack() as ph2:
                    po = [ph2.enter_context(nc.psum_tensor(f"h2_po{k}", [P, 512], F32)) for k in range(4)]
                    product, taken = sem("h2_product"), sem("h2_taken")
                    block = ph2.enter_context(nc.Block())

                    @block.tensor
                    def _(pe):
                        for b in range(BLOCKS):
                            wait_count(pe, taken, b - 3)
                            nc.tensor.matmul(po[b % 4][:, 0:D], AT[:, b, :], gw2[:, 0, :], start=True, stop=True)\
                                .then_inc(product, 1)

                    @block.vector
                    def _(dve):
                        for b in range(BLOCKS):
                            dve.wait_ge(product, b + 1)
                            nc.vector.scalar_tensor_tensor(out=X[:, b:b + 1, :], in0=po[b % 4][:, 0:D].unsqueeze(1),
                                                           scalar=dinv[:, b:b + 1], in1=X[:, b:b + 1, :], op0=ALU.mult,
                                                           op1=ALU.add).then_inc(taken, 1)
                            if b > 0:
                                dve.wait_ge(taken, b)
                                stats_of(X, b - 1)
                        dve.wait_ge(taken, BLOCKS)
                        stats_of(X, BLOCKS - 1)

            norm_stats("ln1")
            recycle()

            with ExitStack() as ph2:
                block = ph2.enter_context(nc.Block())

                @block.sync
                def _(sp):
                    sp.wait_ge(moe_in, 16 * (6 + ZERO_PARTS + 2 * EXP))


            def add_bg(dve, b, po, chain, at):
                nc.vector.tensor_tensor(logit[:, bass.ds(b, 1), :], po[:, 0:EXP].unsqueeze(1), bg[:, :].unsqueeze(1), ALU.add)\
                    .then_inc(chain, 1)
                dve.wait_ge(chain, at + 1)
                return nc.vector.tensor_tensor(logit[:, bass.ds(b, 1), :], logit[:, bass.ds(b, 1), :],
                                               bias[:, :].unsqueeze(1), ALU.add)
            project("gate", Z, KC, [(wg, EXP)], add_bg, 1, norm_of=X)

            with ExitStack() as ph2:
                def sb2(name, shape, dt=F32):
                    return ph2.enter_context(nc.sbuf_tensor(name, shape, dt))

                first = sb2("m_first", [P, BLOCKS])
                gap = sb2("m_gap", [P, BLOCKS])
                counts = sb2("m_counts", [P, EXP, BLOCKS])
                until = sb2("m_until", [P, EXP, BLOCKS])
                resets = sb2("m_resets", [P, EXP, BLOCKS])
                pairs_i = sb2("m_pairs_i", [P, EXP], I32)
                tiles_f = sb2("m_tiles_f", [P, EXP])
                tiles_to = sb2("m_tiles_to", [P, EXP])
                start = sb2("m_start", [P, EXP])
                place = sb2("m_place", [P, BLOCKS, EXP])
                mine = sb2("m_mine", [P, BLOCKS, EXP])
                place_f = sb2("m_place_f", [P, BLOCKS, 2])
                spare = sb2("m_spare", [P, BLOCKS, 2])
                tile_of = sb2("m_tile_of", [P, MT + 2, EXP])
                passed = sb2("m_passed", [1, MT + 2])
                pr = ph2.enter_context(nc.psum_tensor("m_pr", [P, BLOCKS, EXP], F32))
                pc = ph2.enter_context(nc.psum_tensor("m_pc", [P, BLOCKS, EXP], F32))
                chain, gap_set, gap_exp, order_set, both_set, rank_set = (
                    sem("pick_chain"), sem("gap_set"), sem("gap_exp"), sem("order_set"), sem("both_set"), sem("rank_set"))
                block = ph2.enter_context(nc.Block())

                @block.gpsimd
                def _(pool):
                    pool.iota(order[:, :, :], pattern=[[0, BLOCKS], [1, EXP]], base=0, channel_multiplier=0,
                              allow_small_or_imprecise_dtypes=True).then_inc(order_set, 1)
                    pool.iota(spare[:, :, :], pattern=[[0, BLOCKS], [P, 2]], base=MT * P, channel_multiplier=1,
                              allow_small_or_imprecise_dtypes=True).then_inc(order_set, 1)
                    pool.iota(tile_of[:, :, :], pattern=[[1, MT + 2], [0, EXP]], base=0, channel_multiplier=0,
                              allow_small_or_imprecise_dtypes=True).then_inc(order_set, 1)

                @block.vector
                def _(dve):
                    link = Chain(dve, chain)

                    def wide(t):
                        return t[:, :].unsqueeze(2).broadcast_to([P, BLOCKS, EXP])

                    dve.wait_ge(order_set, 3)
                    left = logit
                    for i in range(2):
                        link(nc.vector.tensor_reduce(top_v[i][:, :], left[:, :, :], AX.X, ALU.max))
                        link(nc.vector.tensor_tensor(pick[i][:, :, :], left[:, :, :], wide(top_v[i]), ALU.not_equal))
                        link(nc.vector.scalar_tensor_tensor(out=pick[i][:, :, :], in0=pick[i][:, :, :], scalar=float(EXP),
                                                            in1=order[:, :, :], op0=ALU.mult, op1=ALU.add))
                        link(nc.vector.tensor_reduce(first[:, :], pick[i][:, :, :], AX.X, ALU.min))
                        link(nc.vector.tensor_tensor(pick[i][:, :, :], order[:, :, :], wide(first), ALU.is_equal))
                        if i == 0:
                            link(nc.vector.scalar_tensor_tensor(out=rest[:, :, :], in0=pick[0][:, :, :], scalar=-BIG,
                                                                in1=logit[:, :, :], op0=ALU.mult, op1=ALU.add))
                            left = rest
                    nc.vector.tensor_tensor(gap[:, :], top_v[1][:, :], top_v[0][:, :], ALU.subtract).then_inc(gap_set, 1)
                    for i in range(2):
                        link(nc.vector.tensor_tensor(pick[i][:, :, :], pick[i][:, :, :], wide(real), ALU.mult))
                    nc.vector.tensor_tensor(both[:, :, :], pick[0][:, :, :], pick[1][:, :, :], ALU.add).then_inc(both_set, 1)
                    dve.wait_ge(gap_exp, 1)
                    link(nc.vector.tensor_scalar(first[:, :], gap[:, :], 1.0, None, ALU.add))
                    link(nc.vector.reciprocal(share[0][:, :], first[:, :]))
                    link(nc.vector.tensor_tensor(share[1][:, :], gap[:, :], share[0][:, :], ALU.mult))
                    link(nc.vector.memset(resets[:, :, :], 1.0))
                    link(nc.vector.memset(resets[:, :, 0:1], 0.0))
                    dve.wait_ge(rank_set, 2)
                    link(nc.vector.tensor_copy(counts[:, :, :].rearrange("p e b -> p b e"), pc[:, :, :]))
                    link(nc.vector.tensor_tensor_scan(until[:, :, :].rearrange("p e b -> p (e b)"),
                                                      resets[:, :, :].rearrange("p e b -> p (e b)"),
                                                      counts[:, :, :].rearrange("p e b -> p (e b)"), 0.0, ALU.mult, ALU.add))
                    link(nc.vector.tensor_scalar(pairs_i[:, :], until[:, :, BLOCKS - 1], float(P - 1), None, ALU.add))
                    link(nc.vector.tensor_scalar(pairs_i[:, :], pairs_i[:, :], 7, None, ALU.arith_shift_right))
                    link(nc.vector.tensor_copy(tiles_f[:, :], pairs_i[:, :]))
                    link(nc.vector.memset(resets[:, 0, 0:EXP], 1.0))
                    link(nc.vector.tensor_tensor_scan(tiles_to[:, :], resets[:, 0, 0:EXP], tiles_f[:, :], 0.0, ALU.mult, ALU.add))
                    link(nc.vector.tensor_tensor(start[:, :], tiles_to[:, :], tiles_f[:, :], ALU.subtract))
                    link(nc.vector.tensor_scalar(start[:, :], start[:, :], float(P), None, ALU.mult))
                    link(nc.vector.tensor_tensor(until[:, :, :], until[:, :, :], counts[:, :, :], ALU.subtract))
                    link(nc.vector.tensor_tensor(place[:, :, :], until[:, :, :].rearrange("p e b -> p b e"), pr[:, :, :], ALU.add))
                    link(nc.vector.tensor_tensor(place[:, :, :], place[:, :, :],
                                                 start[:, :].unsqueeze(1).broadcast_to([P, BLOCKS, EXP]), ALU.add))
                    for i in range(2):
                        link(nc.vector.tensor_tensor(mine[:, :, :], pick[i][:, :, :], place[:, :, :], ALU.mult))
                        link(nc.vector.tensor_reduce(place_f[:, :, i:i + 1], mine[:, :, :], AX.X, ALU.add))
                    link(nc.vector.tensor_scalar(first[:, :], real[:, :], -1.0, 1.0, ALU.mult, ALU.add))
                    link(nc.vector.tensor_tensor(spare[:, :, :], spare[:, :, :],
                                                 first[:, :].unsqueeze(2).broadcast_to([P, BLOCKS, 2]), ALU.mult))
                    link(nc.vector.tensor_tensor(place_f[:, :, :], place_f[:, :, :], spare[:, :, :], ALU.add))
                    link(nc.vector.tensor_copy(place_i[:, :, :], place_f[:, :, :]))
                    link(nc.vector.tensor_tensor(tile_of[:, :, :], tile_of[:, :, :],
                                                 tiles_to[:, :].unsqueeze(1).broadcast_to([P, MT + 2, EXP]), ALU.is_ge))
                    link(nc.vector.tensor_reduce(passed[:, :], tile_of[0:1, :, :], AX.X, ALU.add))
                    link(nc.vector.tensor_scalar(expert_of[:, :], passed[:, :], float(EXP - 1), float(PART), ALU.min, ALU.mult))

                @block.scalar
                def _(act):
                    act.wait_ge(gap_set, 1)
                    nc.scalar.activation(gap[:, :], gap[:, :], ACT.Exp).then_inc(gap_exp, 1)

                @block.tensor
                def _(pe):
                    pe.wait_ge(both_set, 1)
                    nc.tensor.matmul(pr[:, :, :], before[:, :], both[:, :, :], start=True, stop=True).then_inc(rank_set, 1)
                    nc.tensor.matmul(pc[:, :, :], ones[:, :], both[:, :, :], start=True, stop=True).then_inc(rank_set, 1)

            with ExitStack() as ph2:
                stage = ph2.enter_context(nc.sbuf_tensor("o_stage", [P, GROUP, D], F32))
                ix = ph2.enter_context(nc.sbuf_tensor("o_ix", [P, GROUP, 2], I32))
                sent = [sem(f"o_sent{k}") for k in range(GROUP)]
                staged, may_send = sem("o_staged"), sem("o_may_send")
                block = ph2.enter_context(nc.Block())

                @block.scalar
                def _(act):
                    def step(i):
                        for k in range(GROUP):
                            b = GROUP * i + k
                            wait_count(act, sent[k], 32 * i)
                            nc.scalar.activation(ix[:, k:k + 1, :], place_i[:, bass.ds(b, 1), :], ACT.Copy)
                            nc.scalar.activation(stage[:, k:k + 1, :], Z[:, bass.ds(b, 1), :], ACT.Copy).then_inc(staged, 1)
                    step(0)
                    with act.Fori(1, (FULL + 1) // GROUP) as i:
                        step(i)

                @block.gpsimd
                def _(pool):
                    with pool.Fori(0, (FULL + 1) // GROUP) as i:
                        for k in range(GROUP):
                            pool.wait_ge(staged, GROUP * i + k + 1)
                            pool.sem_inc(may_send, 1)
                            for m in range(2):
                                pool.indirect_dma_start(zs_d[:, :], bass.IndirectOffsetOnAxis(ap=ix[:, k, m:m + 1], axis=0),
                                                        stage[:, k, :], None).then_inc(sent[k], 16)
                    for k in range(GROUP):
                        pool.wait_ge(sent[k], 32 * ((FULL + 1) // GROUP))

            with ExitStack() as ph2:
                zin = ph2.enter_context(nc.sbuf_tensor("m_zin", [P, 2, D], F32))
                zt = ph2.enter_context(nc.sbuf_tensor("m_zt", [P, 2, KC, P], F32))
                hid = ph2.enter_context(nc.sbuf_tensor("m_hid", [P, 2, EH], F32))
                ht = ph2.enter_context(nc.sbuf_tensor("m_ht", [P, 2, HC, P], F32))
                y = ph2.enter_context(nc.sbuf_tensor("m_y", [P, 2, D], F32))
                pz = [ph2.enter_context(nc.psum_tensor(f"m_pz{k}", [P, KC, P], F32)) for k in range(2)]
                phid = [ph2.enter_context(nc.psum_tensor(f"m_ph{k}", [P, EH], F32)) for k in range(2)]
                pht = [ph2.enter_context(nc.psum_tensor(f"m_pht{k}", [P, HC, P], F32)) for k in range(2)]
                py = [ph2.enter_context(nc.psum_tensor(f"m_py{k}", [P, 512], F32)) for k in range(2)]
                z_in, y_out = [sem(f"m_z_in{k}") for k in range(2)], [sem(f"m_y_out{k}") for k in range(2)]
                z_turned, zt_set, h_set, hid_set, h_turned, ht_set, y_set, y_ready = (
                    sem(f"m_{n}") for n in ("z_turned", "zt_set", "h_set", "hid_set", "h_turned", "ht_set", "y_set", "y_ready"))
                may_store = sem("m_may_store")
                block = ph2.enter_context(nc.Block())
                reason = "a tile's expert is below EXP"

                def tile_rows(t, n):
                    return t[bass.ds(n * P, P), :]

                @block.sync
                def _(sp):
                    def load(n, k, turns):
                        wait_count(sp, z_turned, turns)
                        sp.dma_start(zin[:, k, :], tile_rows(zs_d, n)).then_inc(z_in[k], 16)

                    load(0, 0, 0)
                    load(1, 1, 0)
                    with sp.Fori(0, MT // 2 - 1) as i:
                        for k in range(2):
                            load(2 * i + k + 2, k, 2 * i + k + 1)

                @block.gpsimd
                def _(pool):
                    with pool.Fori(0, MT // 2) as i:
                        for k in range(2):
                            pool.wait_ge(y_ready, 2 * i + k + 1)
                            pool.sem_inc(may_store, 1)
                            pool.dma_start(tile_rows(y_d, 2 * i + k), y[:, k, :]).then_inc(y_out[k], 16)
                    for k in range(2):
                        pool.wait_ge(y_out[k], 16 * (MT // 2))

                @block.tensor
                def _(pe):
                    def turn_z(n, k, i):
                        pe.wait_ge(z_in[k], 16 * (i + 1))
                        wait_count(pe, zt_set, n - 1)
                        for c in range(KC):
                            last = nc.tensor.transpose(pz[k][:, c, :], zin[:, k, c * P:(c + 1) * P], ident[:, :])
                        last.then_inc(z_turned, 1)

                    def hidden(n, k, at):
                        pe.wait_ge(zt_set, n + 1)
                        wait_count(pe, hid_set, n - 1)
                        for c in range(KC):
                            last = nc.tensor.matmul(phid[k][:, :], zt[:, k, c, :], w1[:, bass.ds(at + c * EH, EH)],
                                                    start=(c == 0), stop=(c == KC - 1))
                        last.then_inc(h_set, 1)

                    def turn_h(n, k):
                        pe.wait_ge(hid_set, n + 1)
                        wait_count(pe, ht_set, n - 1)
                        for c in range(HC):
                            last = nc.tensor.transpose(pht[k][:, c, :], hid[:, k, c * P:(c + 1) * P], ident[:, :])
                        last.then_inc(h_turned, 1)

                    def result(n, k, at):
                        pe.wait_ge(ht_set, n + 1)
                        wait_count(pe, y_ready, n - 1)
                        for c in range(HC):
                            last = nc.tensor.matmul(py[k][:, 0:D], ht[:, k, c, :], w2[:, bass.ds(at + c * D, D)],
                                                    start=(c == 0), stop=(c == HC - 1))
                        last.then_inc(y_set, 1)

                    def experts(n, count):
                        return nc.values_load_multi_w_load_instructions(
                            expert_of[0:1, bass.ds(n, count)], engines=PE_ONLY, min_val=0, max_val=(EXP - 1) * PART,
                            skip_runtime_bounds_check_because=reason)[1]

                    def pair(i, more):
                        at = experts(2 * i, 3)
                        for k in range(2):
                            n = 2 * i + k
                            turn_h(n, k)
                            if more or k == 0:
                                hidden(n + 1, 1 - k, at[k + 1])
                            if more:
                                turn_z(n + 2, k, i + 1)
                            result(n, k, at[k])
                    turn_z(0, 0, 0)
                    turn_z(1, 1, 0)
                    hidden(0, 0, experts(0, 1)[0])
                    pair(0, True)
                    with pe.Fori(1, MT // 2 - 1) as i:
                        pair(i, True)
                    pair(MT // 2 - 1, False)

                @block.scalar
                def _(act):
                    def copy_z(n, k):
                        act.wait_ge(z_turned, n + 1)
                        wait_count(act, h_set, n - 1)
                        nc.scalar.activation(zt[:, k, :, :], pz[k][:, :, :], ACT.Copy).then_inc(zt_set, 1)

                    def relu_h(n, k):
                        act.wait_ge(h_turned, n + 1)
                        wait_count(act, y_set, n - 1)
                        nc.scalar.activation(ht[:, k, :, :], pht[k][:, :, :], ACT.Relu).then_inc(ht_set, 1)

                    def pair(i, more):
                        for k in range(2):
                            relu_h(2 * i + k, k)
                            if more:
                                copy_z(2 * i + k + 2, k)
                    copy_z(0, 0)
                    copy_z(1, 1)
                    pair(0, True)
                    with act.Fori(1, MT // 2 - 1) as i:
                        pair(i, True)
                    pair(MT // 2 - 1, False)

                @block.vector
                def _(dve):
                    def take_h(n, k, at):
                        dve.wait_ge(h_set, n + 1)
                        wait_count(dve, h_turned, n - 1)
                        nc.vector.tensor_tensor(hid[:, k, :], phid[k][:, :], b1[:, bass.ds(at // (PART // EH), EH)], ALU.add)\
                            .then_inc(hid_set, 1)

                    def take_y(n, k, at, i):
                        dve.wait_ge(y_set, n + 1)
                        wait_count(dve, y_out[k], 16 * i)
                        nc.vector.tensor_tensor(y[:, k, :], py[k][:, 0:D], b2[:, bass.ds(at // (PART // D), D)], ALU.add)\
                            .then_inc(y_ready, 1)

                    def experts(n, count):
                        return nc.values_load_multi_w_load_instructions(
                            expert_of[0:1, bass.ds(n, count)], engines=DVE_ONLY, min_val=0, max_val=(EXP - 1) * PART,
                            skip_runtime_bounds_check_because=reason)[1]

                    def pair(i, more):
                        at = experts(2 * i, 3)
                        for k in range(2):
                            if more or k == 0:
                                take_h(2 * i + k + 1, 1 - k, at[k + 1])
                            take_y(2 * i + k, k, at[k], i)
                    take_h(0, 0, experts(0, 1)[0])
                    pair(0, True)
                    with dve.Fori(1, MT // 2 - 1) as i:
                        pair(i, True)
                    pair(MT // 2 - 1, False)

            with ExitStack() as ph2:
                ring = ph2.enter_context(nc.sbuf_tensor("i_ring", [P, GROUP, 2, D], F32))
                ix = ph2.enter_context(nc.sbuf_tensor("i_ix", [P, GROUP, 2], I32))
                landed = [sem(f"i_landed{k}") for k in range(GROUP)]
                staged, may_gather, chain = sem("i_staged"), sem("i_may_gather"), sem("i_chain")
                block = ph2.enter_context(nc.Block())

                @block.gpsimd
                def _(pool):
                    with pool.Fori(0, (FULL + 1) // GROUP) as i:
                        for k in range(GROUP):
                            pool.wait_ge(staged, GROUP * i + k + 1)
                            pool.sem_inc(may_gather, 1)
                            for m in range(2):
                                pool.indirect_dma_start(ring[:, k, m, :], None, y_d[:, :],
                                                        bass.IndirectOffsetOnAxis(ap=ix[:, k, m:m + 1], axis=0))\
                                    .then_inc(landed[k], 16)

                @block.vector
                def _(dve):
                    def stage(i, k):
                        nc.vector.tensor_copy(ix[:, k:k + 1, :], place_i[:, bass.ds(GROUP * i + k, 1), :]).then_inc(staged, 1)

                    def add(i, k):
                        b = bass.ds(GROUP * i + k, 1)
                        dve.wait_ge(landed[k], 32 * (i + 1))
                        for m in range(2):
                            nc.vector.scalar_tensor_tensor(out=X[:, b, :], in0=ring[:, k, m:m + 1, :], scalar=share[m][:, b],
                                                           in1=X[:, b, :], op0=ALU.mult, op1=ALU.add).then_inc(chain, 1)
                            dve.wait_ge(chain, 2 * (GROUP * i + k) + m + 1)
                        stats_of(X, GROUP * i + k)
                    for k in range(GROUP):
                        stage(0, k)
                    for b in range(FULL + 1, BLOCKS):
                        stats_of(X, b)
                    with dve.Fori(0, (FULL + 1) // GROUP - 1) as i:
                        for k in range(GROUP):
                            add(i, k)
                            stage(i + 1, k)
                    for k in range(GROUP):
                        add((FULL + 1) // GROUP - 1, k)

        norm_stats("ln2")

        recycle()

        SCALE = float(HD) ** -0.5
        FC = FH // P
        LATE = KC + 1 + KC * FH + FC * D + FC + 3 * D
        late = keep("late", [P, LATE])

        with ExitStack() as sum_ph:
            total = sum_ph.enter_context(nc.sbuf_tensor("a_total", [P, BLOCKS * AW], F32))
            q_ph = ExitStack()
            Q = q_ph.enter_context(nc.sbuf_tensor("a_Q", [P, BLOCKS, D], F32))
            with ExitStack() as ph:
                kv = ph.enter_context(nc.sbuf_tensor("a_kv", [P, 2, 1, 2 * D], F32))
                with ExitStack() as ph2:
                    block = ph2.enter_context(nc.Block())

                    @block.sync
                    def _(sp):
                        sp.wait_ge(attn_in, 16 * 2 * len(attn))

                def add_biases(dve, b, po, chain, at, k):
                    for m, to in enumerate((Q[:, bass.ds(b, 1), :], kv[:, k, :, 0:D], kv[:, k, :, D:2 * D])):
                        last = nc.vector.tensor_tensor(to, po[:, m * D:(m + 1) * D].unsqueeze(1),
                                                       ab[m + 1][:, :].unsqueeze(1), ALU.add)
                    return last
                project("qkv", Z, KC, [(t, D) for t in aw[1:]], add_biases, 0, norm_of=X, ringed=(kv, (kv_d,)),
                        keeps=False)

            with ExitStack() as ph:
                def sb(name, shape, dt=F32):
                    return ph.enter_context(nc.sbuf_tensor(name, shape, dt))

                MINE = U - 4
                RING = 4
                CE = U * P
                carve = carver(early, EARLY)
                ring = [carver(late, LATE)([P, U, 2 * D])] + [sb(f"a_ring{m}", [P, U, 2 * D]) for m in range(1, RING)]
                oh = carve([P, RING, U, P])
                oht = carve([P, 2, 2, P])
                qk = carve([P, 2, 2, D])
                msg = carve([P, U, AW])
                ROWS = U * HEADS
                brk = carve([ROWS, 2, P + 1])
                LT = carve([ROWS, P])
                MT = carve([ROWS, P])
                of_head = carve([ROWS, P])
                of_slot = sb("a_of_slot", [ROWS, U])
                by_head = sb("a_by_head", [HEADS, U, HEADS])
                ends = sb("a_ends", [ROWS, 2, U])
                CROSS = U + 2
                cross = sb("a_cross", [HEADS, 2 * CROSS])
                picked = sb("a_picked", [ROWS, 2, U])
                starts = sb("a_starts", [ROWS, 2])
                L = carve([P, RING, U, HEADS])
                less = carve([P, U, HEADS])
                wx = carve([P, U, HEADS])
                going = sb("a_going", [HEADS, 1])
                grown = sb("a_grown", [HEADS, 1])
                factor = sb("a_factor", [HEADS, 1])
                at_first = carve([HEADS, P])
                elsewhere = carve([HEADS, P])
                grow = sb("a_grow", [P, HEADS])
                share8 = sb("a_share8", [HEADS, HEADS])
                ix = sb("a_ix", [P, RING, U], I32)
                pt = [ph.enter_context(nc.psum_tensor(f"a_pt{k}", [P, 2, P], F32)) for k in range(2)]
                pq = [ph.enter_context(nc.psum_tensor(f"a_pq{k}", [P, 2, D], F32)) for k in range(2)]
                pm = [ph.enter_context(nc.psum_tensor(f"a_pm{k}", [P, 512], F32)) for k in range(3)]
                pl = pt[1][0:ROWS, 0, :]
                pb = ph.enter_context(nc.psum_tensor("a_pb", [P, 4, U * HEADS], F32))
                landed = [sem(f"a_landed{m}") for m in range(RING)]
                brk_in = [sem(f"a_brk_in{half}") for half in range(2)]
                may_gather = sem("a_may_gather")
                (ix_ready, oh_ready, turned_, oht_set, q_set, multiplied, reduced, lt_turned, lt_set, scanned,
                 spread, ends_set, ends_in, cross_chain, cross_set, starts_in, start_chain, mt_set, grown_set, mt_turned, less_set, weight_set, factor_set, at_first_set, factors,
                 corrected, msg_set, product, added, cleared, grow_set,
                 apart_set, pool_msg_set) = (sem(f"a_{n}") for n in (
                     "ix_ready", "oh_ready", "turned", "oht_set", "q_set", "multiplied", "reduced", "lt_turned",
                     "lt_set", "scanned", "spread", "ends_set", "ends_in", "cross_chain", "cross_set",
                     "starts_in", "start_chain", "mt_set", "grown_set", "mt_turned", "less_set",
                     "weight_set", "factor_set", "at_first_set", "factors", "corrected", "msg_set", "product", "added",
                     "cleared", "grow_set", "apart_set", "pool_msg_set"))
                block = ph.enter_context(nc.Block())

                def steps(eng, step):
                    def one_step(i):
                        step(i, i % RING, i < STEPS, 1 <= i <= STEPS, i >= 2)
                    for i in range(RING):
                        one_step(i)
                    with eng.Fori(1, STEPS // RING - 1) as it:
                        for m in range(RING):
                            step(RING * it + m, m, True, True, True)
                    for i in range(STEPS - RING, STEPS + 2):
                        one_step(i)

                def message(eng, i, m2, k, done):
                    wait_count(eng, product, U * (i - 3) + k + 1)
                    eng.tensor_tensor(
                        msg[:, k, 0:D].rearrange("p (n d) -> p n d", d=HD),
                        ring[m2][:, k, D:2 * D].rearrange("p (n d) -> p n d", d=HD),
                        wx[:, k, :].unsqueeze(2).broadcast_to([P, HEADS, HD]), ALU.mult).then_inc(done, 1)

                @block.gpsimd
                def _(pool):
                    def ahead(c, m):
                        if not isinstance(c, int) or c > RING - 1:
                            pool.wait_ge(weight_set, 3 * (c - RING) + 1)
                            last_messages(c - RING, m)
                            pool.wait_ge(pool_msg_set, (U - MINE) * (c - RING + 1))
                        wait_count(pool, msg_set, MINE * (c - RING + 1))
                        nc.gpsimd.tensor_copy(ix[:, m, :], src_i[:, bass.ds(U * c, U)]).then_inc(ix_ready, 1)
                        pool.wait_ge(ix_ready, c + 1)
                        pool.sem_inc(may_gather, 1)
                        for k in range(U):
                            pool.indirect_dma_start(ring[m][:, k, :], None, kv_d[:, :],
                                                    bass.IndirectOffsetOnAxis(ap=ix[:, m, k:k + 1], axis=0))\
                                .then_inc(landed[m], 16)
                    def last_messages(c, m):
                        for k in range(MINE, U):
                            message(pool, c + 2, m, k, pool_msg_set)
                    for c in range(2 * RING):
                        ahead(c, c % RING)
                    with pool.Fori(2, STEPS // RING) as it:
                        for m in range(RING):
                            ahead(RING * it + m, m)
                    for c in range(STEPS - RING, STEPS):
                        pool.wait_ge(weight_set, 3 * c + 1)
                        last_messages(c, c % RING)

                @block.sync
                def _(sp):
                    brk_flat = brk_d.rearrange("s e -> (s e)").rearrange("(o f) -> o f", o=1)

                    def load(c, half):
                        wait_count(sp, mt_set, c - 1)
                        for k in range(U):
                            at = bass.ds(c * CE + k * P, P + 1)
                            sp.dma_start(brk[k * HEADS:(k + 1) * HEADS, half, :], brk_flat[0:1, at].broadcast_to([HEADS, P + 1]))\
                                .then_inc(brk_in[half], 16)
                    load(0, 0)
                    load(1, 1)
                    with sp.Fori(1, STEPS // 2) as n:
                        for half in range(2):
                            load(2 * n + half, half)
                    for half in range(2):
                        sp.wait_ge(brk_in[half], 16 * U * STEPS // 2)

                @block.tensor
                def _(pe):
                    q_rows = Q[:, :, :].rearrange("p b f -> p (b f)")

                    def blocks_of(slot):
                        return nc.values_load_multi_w_load_instructions(
                            blk2[0:1, bass.ds(slot, U)], engines=PE_ONLY, min_val=0, max_val=(BLOCKS - 1) * D,
                            skip_runtime_bounds_check_because="a slot's block is below BLOCKS")[1]

                    def turn(i, m, j):
                        p = 4 * i + j
                        pe.wait_ge(oh_ready, i + 1 + j // 4)
                        wait_count(pe, oht_set, p - 1)
                        if j == 7:
                            pe.wait_ge(lt_set, i + 1)
                        for k in range(2):
                            done = nc.tensor.transpose(pt[j % 2][:, k, :], oh[:, (m + j // 4) % RING, 2 * (j % 4) + k, :],
                                                       ident[:, :])
                        done.then_inc(turned_, 1)

                    def fetch(i, j, where):
                        p = 4 * i + j
                        pe.wait_ge(oht_set, p + 1)
                        wait_count(pe, multiplied, p - 1)
                        for k in range(2):
                            done = nc.tensor.matmul(pq[j % 2][:, k, :], oht[:, j % 2, k, :],
                                                    q_rows[:, bass.ds(where[k], D)], start=True, stop=True)
                        done.then_inc(q_set, 1)

                    def step(i, m, logits, maxima, sums):
                        more = not isinstance(i, int) or i + 1 < STEPS
                        m2 = (m - 2) % RING

                        def sum_up(k):
                            if k < MINE:
                                if k % 2 == 0:
                                    pe.wait_ge(msg_set, MINE * (i - 2) + min(k + 2, MINE))
                            elif k == MINE:
                                pe.wait_ge(pool_msg_set, (U - MINE) * (i - 1))
                            wait_count(pe, added, U * (i - 2) + k - (2 if k > 2 else 1 if k < 2 else 4))
                            nc.tensor.matmul(pm[k % 3][:, 0:AW], oh[:, m2, k, :], msg[:, k, :], start=True, stop=True)\
                                .then_inc(product, 1)
                        if logits:
                            where = blocks_of(U * i + U // 2) if more else blocks_of(SLOTS - U)[U // 2:]
                            fetch(i, 2, where[0:2])
                            fetch(i, 3, where[2:4])
                            if more:
                                turn(i, m, 4)
                        if sums:
                            pe.wait_ge(at_first_set, i - 1)
                            pe.wait_ge(less_set, i - 1)
                            nc.tensor.matmul(pb[:, 1, 0:HEADS], at_first[:, :], ident[0:HEADS, 0:HEADS], start=True, stop=False)
                            nc.tensor.matmul(pb[:, 1, 0:HEADS], elsewhere[:, :], share8[:, :], start=False, stop=True)\
                                .then_inc(factors, 1)
                        if maxima:
                            pe.wait_ge(ends_set, 2 * i)
                            nc.tensor.matmul(pb[:, 2, 0:2 * U], of_head[:, :], ends[:, :, :].rearrange("r m k -> r (m k)"),
                                             start=True, stop=True).then_inc(ends_in, 1)
                        if logits and more:
                            turn(i, m, 5)
                            fetch(i, 4, where[4:6])
                            turn(i, m, 6)
                        if sums:
                            pe.wait_ge(weight_set, 3 * (i - 1))
                            sum_up(0)
                        if maxima:
                            pe.wait_ge(cross_set, 2 * i)
                            nc.tensor.matmul(pb[0:ROWS, 3, 0:2 * U].rearrange("r (m k) -> r m k", m=2),
                                             by_head[:, :, :].rearrange("h k g -> h (k g)"),
                                             cross[:, :].rearrange("h (m k) -> h m k", m=2)[:, :, 0:U],
                                             start=True, stop=True).then_inc(starts_in, 1)
                        if sums:
                            sum_up(1)
                        if logits:
                            if more:
                                fetch(i, 5, where[6:8])
                            pe.wait_ge(reduced, 4 * i + 4)
                            wait_count(pe, oht_set, 4 * i + 6 if more else 4 * i + 4)
                            nc.tensor.matmul(pl, L[:, m, :, :].rearrange("p k n -> p (k n)"), ident[:, :], start=True,
                                             stop=True)\
                                .then_inc(lt_turned, 1)
                        if sums:
                            for k in range(2, U // 2):
                                sum_up(k)
                        if maxima:
                            pe.wait_ge(mt_set, i)
                            nc.tensor.matmul(pb[:, 0, :], MT[:, :], ident[0:ROWS, 0:ROWS], start=True, stop=True)\
                                .then_inc(mt_turned, 1)
                        if sums:
                            for k in range(U // 2, U - 2):
                                sum_up(k)
                        if logits and more:
                            turn(i, m, 7)
                        if sums:
                            for k in range(U - 2, U):
                                sum_up(k)
                    where = blocks_of(0)
                    turn(0, 0, 0)
                    turn(0, 0, 1)
                    fetch(0, 0, where[0:2])
                    turn(0, 0, 2)
                    fetch(0, 1, where[2:4])
                    turn(0, 0, 3)
                    steps(pe, step)

                @block.scalar
                def _(act):
                    def one_hots(c, m, turned_first=None):
                        for k in range(U):
                            wait_count(act, product, U * (c - RING) + k + 1)
                            nc.scalar.activation(oh[:, m, k, :], lane[:, :], ACT.Abs, scale=-1.0,
                                                 bias=dl[:, bass.ds(U * c + k, 1)]).then_inc(apart_set, 1)
                            if k == U - 3 and turned_first is not None:
                                copy_turned(turned_first, 7)
                        act.wait_ge(apart_set, U * c + U)
                        nc.scalar.activation(oh[:, m, :, :], oh[:, m, :, :], ACT.Relu, scale=-1.0, bias=ones[:, 0:1])\
                            .then_inc(oh_ready, 1)

                    def copy_turned(i, j):
                        p = 4 * i + j
                        act.wait_ge(turned_, p + 1)
                        wait_count(act, q_set, p - 1)
                        nc.scalar.activation(oht[:, j % 2, :, :], pt[j % 2][:, :, :], ACT.Copy).then_inc(oht_set, 1)

                    def step(i, m, logits, maxima, sums):
                        more = not isinstance(i, int) or i + 1 < STEPS
                        if sums:
                            act.wait_ge(less_set, i - 1)
                            wait_count(act, msg_set, MINE * (i - 2))
                            wait_count(act, pool_msg_set, (U - MINE) * (i - 2))
                            nc.scalar.activation(wx[:, :, :], less[:, :, :], ACT.Exp, scale=SCALE).then_inc(weight_set, 1)
                        if sums:
                            for h in range(2):
                                part = slice(U // 2 * h, U // 2 * (h + 1))
                                wait_count(act, product, U * (i - 3) + U // 2 * (h + 1))
                                nc.scalar.activation(msg[:, part, D:AW], less[:, part, :], ACT.Exp, scale=SCALE)\
                                    .then_inc(weight_set, 1)
                        if logits:
                            if more:
                                for j in range(4, 7):
                                    copy_turned(i, j)
                            act.wait_ge(lt_turned, i + 1)
                            wait_count(act, scanned, i)
                            nc.scalar.activation(LT[:, :], pl, ACT.Copy).then_inc(lt_set, 1)
                        if maxima:
                            act.wait_ge(grown_set, i)
                            wait_count(act, at_first_set, i - 1)
                            nc.scalar.activation(factor[:, :], grown[:, :], ACT.Exp, scale=SCALE).then_inc(factor_set, 1)
                        if not isinstance(i, int) or i + 2 < STEPS:
                            one_hots(i + 2, (m + 2) % RING, i)
                        elif more:
                            copy_turned(i, 7)
                    one_hots(0, 0)
                    one_hots(1, 1)
                    for j in range(4):
                        copy_turned(0, j)
                    steps(act, step)

                @block.vector
                def _(dve):
                    def multiply(i, m, j):
                        p = 4 * i + j
                        dve.wait_ge(q_set, p + 1)
                        wait_count(dve, reduced, p - 1)
                        nc.vector.tensor_tensor(qk[:, j % 2, :, :], pq[j % 2][:, :, :], ring[m][:, 2 * j:2 * j + 2, 0:D],
                                                ALU.mult).then_inc(multiplied, 1)

                    def first_multiply(i, m):
                        dve.wait_ge(landed[m], 16 * U * (i // RING + 1) if isinstance(i, int) else 4 * U * (i - m) + 16 * U)
                        multiply(i, m, 0)

                    def reduce(i, m, j):
                        dve.wait_ge(multiplied, 4 * i + j + 1)
                        nc.vector.tensor_reduce(L[:, m, 2 * j:2 * j + 2, :],
                                                qk[:, j % 2, :, :].rearrange("p k (n d) -> p k n d", d=HD), AX.X, ALU.add)\
                            .then_inc(reduced, 1)

                    def add(i, k, where):
                        slot = U * (i - 2) + k
                        dve.wait_ge(product, slot + 1)
                        wait_count(dve, added, slot)
                        rows_ = total[:, bass.ds(where, AW)]
                        nc.vector.tensor_tensor(rows_, rows_, pm[k % 3][:, 0:AW], ALU.add).then_inc(added, 1)

                    def step(i, m, logits, maxima, sums):
                        if sums:
                            where = nc.values_load_multi_w_load_instructions(
                                blk3[0:1, bass.ds(U * (i - 2), U)], engines=DVE_ONLY, min_val=0, max_val=(BLOCKS - 1) * AW,
                                skip_runtime_bounds_check_because="a slot's block is below BLOCKS")[1]
                            m2 = (m - 2) % RING
                            dve.wait_ge(mt_turned, i - 1)
                            wait_count(dve, weight_set, 3 * (i - 2))
                            nc.vector.tensor_tensor(less[:, :, :].rearrange("p k n -> p (k n)"),
                                                    L[:, m2, :, :].rearrange("p k n -> p (k n)"), pb[:, 0, :],
                                                    ALU.subtract).then_inc(less_set, 1)
                        if maxima:
                            dve.wait_ge(lt_set, i)
                            dve.wait_ge(brk_in[(m - 1) % 2], 16 * U * ((i + 1) // 2) if isinstance(i, int)
                                        else 8 * U * (i + (m % 2)))
                            wait_count(dve, mt_turned, i - 1)
                            nc.vector.tensor_tensor_scan(MT[:, :], brk[:, (m - 1) % 2, 0:P], LT[:, :], -BIG, ALU.add, ALU.max)\
                                .then_inc(scanned, 1)
                        if maxima:
                            dve.wait_ge(scanned, i)
                            nc.vector.tensor_tensor_scan(MT[:, ::-1], brk[:, (m - 1) % 2, P:0:-1], MT[:, ::-1], -BIG, ALU.add, ALU.max)\
                                .then_inc(spread, 1)
                        if sums:
                            dve.wait_ge(factors, i - 1)
                            wait_count(dve, corrected, 2 * (i - 2))
                            nc.vector.tensor_copy(grow[:, :], pb[:, 1, 0:HEADS]).then_inc(grow_set, 1)
                        if maxima:
                            dve.wait_ge(spread, i)
                            for n, at in enumerate((0, P - 1)):
                                nc.vector.tensor_scalar(ends[:, n, :], of_slot[:, :], MT[:, at:at + 1], None, ALU.mult)\
                                    .then_inc(ends_set, 1)
                            nc.vector.tensor_copy(cross[:, 0:1], cross[:, U:U + 1]).then_inc(cross_chain, 1)
                        if logits:
                            multiply(i, m, 2)
                            reduce(i, m, 1)
                        if sums:
                            dve.wait_ge(weight_set, 3 * (i - 2) + 1)
                            message(dve, i, m2, 0, msg_set)
                            message(dve, i, m2, 1, msg_set)
                        if logits:
                            multiply(i, m, 3)
                        if maxima:
                            dve.wait_ge(cross_chain, 2 * i - 1)
                            dve.wait_ge(ends_in, i)
                            nc.vector.tensor_tensor_scan(cross[:, 1:U + 1], pen_f[:, bass.ds(U * (i - 1), U)], pb[0:HEADS, 2, U:2 * U],
                                                         cross[:, 0:1], ALU.add, ALU.max).then_inc(cross_set, 1)
                            nc.vector.tensor_tensor_scan(cross[:, CROSS - 1:CROSS + U - 1][:, ::-1], pen_b[:, bass.ds(U * (i - 1), U)],
                                                         pb[0:HEADS, 2, 0:U][:, ::-1], -BIG, ALU.add, ALU.max).then_inc(cross_set, 1)
                            nc.vector.tensor_tensor(going[:, :], cross[:, 0:1], link8[:, bass.ds(U * (i - 1), 1)], ALU.add)\
                                .then_inc(cross_chain, 1)
                        if logits:
                            reduce(i, m, 2)
                        if maxima:
                            dve.wait_ge(cross_chain, 2 * i)
                            dve.wait_ge(cross_set, 2 * i)
                            wait_count(dve, factor_set, i - 1)
                            nc.vector.tensor_scalar(grown[:, :], going[:, :], cross[:, CROSS - 1:CROSS], 0.0, ALU.subtract,
                                                    ALU.min).then_inc(grown_set, 1)
                        if sums:
                            dve.wait_ge(grow_set, i - 1)
                            wait_count(dve, added, U * (i - 2))
                            sums_ = total[:, bass.ds(where[0], AW)]
                            values = sums_[:, 0:D].rearrange("p (n d) -> p n d", d=HD)
                            nc.vector.tensor_tensor(values, values, grow[:, :].unsqueeze(2).broadcast_to([P, HEADS, HD]),
                                                    ALU.mult).then_inc(corrected, 1)
                            nc.vector.tensor_tensor(sums_[:, D:AW], sums_[:, D:AW], grow[:, :], ALU.mult)\
                                .then_inc(corrected, 1)
                        if logits:
                            reduce(i, m, 3)
                        if sums:
                            message(dve, i, m2, 2, msg_set)
                        if maxima:
                            dve.wait_ge(starts_in, i)
                            nc.vector.tensor_tensor(picked[:, :, :], pb[0:ROWS, 3, 0:2 * U].rearrange("r (m k) -> r m k", m=2),
                                                    of_slot[:, :].unsqueeze(1).broadcast_to([ROWS, 2, U]), ALU.mult)\
                                .then_inc(start_chain, 1)
                        if sums:
                            message(dve, i, m2, 3, msg_set)
                        if maxima:
                            dve.wait_ge(start_chain, 3 * i - 2)
                            nc.vector.tensor_reduce(starts[:, :], picked[:, :, :], AX.X, ALU.add).then_inc(start_chain, 1)
                        if sums:
                            dve.wait_ge(corrected, 2 * (i - 1))
                            add(i, 0, where[0])
                        if maxima:
                            dve.wait_ge(start_chain, 3 * i - 1)
                            nc.vector.tensor_tensor_scan(MT[:, :], brk[:, (m - 1) % 2, 0:P], MT[:, :], starts[:, 0:1], ALU.add, ALU.max)\
                                .then_inc(start_chain, 1)
                        if sums:
                            add(i, 1, where[1])
                        if maxima:
                            dve.wait_ge(start_chain, 3 * i)
                            nc.vector.tensor_tensor_scan(MT[:, ::-1], brk[:, (m - 1) % 2, P:0:-1], MT[:, ::-1], starts[:, 1:2], ALU.add, ALU.max)\
                                .then_inc(mt_set, 1)
                        if sums:
                            add(i, 2, where[2])
                            add(i, 3, where[3])
                        more = not isinstance(i, int) or i + 1 < STEPS
                        if more:
                            first_multiply(i + 1, (m + 1) % RING)
                        if sums:
                            add(i, 4, where[4])
                            add(i, 5, where[5])
                        if maxima:
                            dve.wait_ge(factor_set, i)
                            wait_count(dve, factors, i - 1)
                            first = first8[:, bass.ds(i - 1, 1)]
                            nc.vector.tensor_scalar(elsewhere[:, :], lane[0:HEADS, :], first, None, ALU.not_equal)
                            nc.vector.tensor_scalar(at_first[:, :], lane[0:HEADS, :], first, factor[:, 0:1], ALU.is_equal,
                                                    ALU.mult).then_inc(at_first_set, 1)
                        if more:
                            multiply(i + 1, (m + 1) % RING, 1)
                            reduce(i + 1, (m + 1) % RING, 0)
                        if sums:
                            add(i, U - 2, where[U - 2])
                            add(i, U - 1, where[U - 1])
                    first_multiply(0, 0)
                    multiply(0, 0, 1)
                    reduce(0, 0, 0)
                    nc.vector.memset(share8[:, :], 1.0 / HEADS).then_inc(cleared, 1)
                    nc.vector.memset(cross[:, :], -BIG).then_inc(cleared, 1)
                    nc.vector.memset(of_head[:, HEADS:P], 0.0).then_inc(cleared, 1)
                    square = ident[0:ROWS, 0:ROWS].rearrange("r (k h) -> r k h", h=HEADS)
                    nc.vector.tensor_reduce(of_slot[:, :], square, AX.X, ALU.add).then_inc(cleared, 1)
                    nc.vector.tensor_reduce(of_head[:, 0:HEADS], square.rearrange("r k h -> r h k"), AX.X, ALU.add).then_inc(cleared, 1)
                    nc.vector.tensor_copy(by_head[:, :, :], ident[0:HEADS, 0:HEADS].unsqueeze(1).broadcast_to([HEADS, U, HEADS]))\
                        .then_inc(cleared, 1)
                    chunked = [v.rearrange("h (c k) -> h c k", k=U) for v in (pen_b[:, :], pen_f[:, :], link8[:, 1:SLOTS + 1])]
                    nc.vector.tensor_tensor(chunked[0], chunked[1][:, :, ::-1], chunked[2][:, :, ::-1], ALU.add)\
                        .then_inc(cleared, 1)
                    dve.wait_ge(cleared, 7)
                    nc.vector.tensor_tensor(pen_f[:, :], pen_f[:, :], link8[:, 0:SLOTS], ALU.add).then_inc(cleared, 1)
                    nc.vector.memset(total[:, :], 0.0).then_inc(cleared, 1)
                    dve.wait_ge(cleared, 9)
                    steps(dve, step)
                    dve.wait_ge(added, SLOTS)
            q_ph.close()
            recycle()
            carve_late = carver(late, LATE)
            skip = sum_ph.enter_context(nc.sbuf_tensor("a_skip", [P, BLOCKS, D], F32))
            wr = carve_late([P, KC, 1])
            br = carve_late([P, 1])
            r_w1 = carve_late([P, KC, FH])
            r_w2 = carve_late([P, FC, D])
            r_b1 = carve_late([P, FC])
            r_b2 = carve_late([P, D])
            gamma = carve_late([P, D])
            beta = carve_late([P, D])

            def route_loads(sp):
                sp.dma_start(wr[:, :, :], a["L1_ffn_wr"].rearrange("(c p) f -> p c f", p=P),
                             allow_slow_non_contiguous=True).then_inc(route_in, 16)
                load_broadcast(sp, br[:, :], a["L1_ffn_br"], route_in)
                sp.dma_start(r_w1[:, :, :], a["L1_ffn_w1"].rearrange("(c p) f -> p c f", p=P)).then_inc(route_in, 16)
                sp.dma_start(r_w2[:, :, :], a["L1_ffn_w2"].rearrange("(c p) f -> p c f", p=P)).then_inc(route_in, 16)
                sp.dma_start(r_b1[:, :], a["L1_ffn_b1"].rearrange("(c p) -> p c", p=P),
                             allow_slow_non_contiguous=True).then_inc(route_in, 16)
                load_broadcast(sp, r_b2[:, :], a["L1_ffn_b2"], route_in)
                load_broadcast(sp, gamma[:, :], a["L1_gnn_gamma"], route_in)
                load_broadcast(sp, beta[:, :], a["L1_gnn_beta"], route_in)
                sp.wait_ge(route_in, 16 * 8)

            project("skip", Z, KC, [(aw_skip, D)], lambda dve, b, po, chain, at: nc.vector.tensor_tensor(
                skip[:, bass.ds(b, 1), :], po[:, 0:D].unsqueeze(1), ab_skip[:, :].unsqueeze(1), ALU.add), 0,
                norm_of=X, meanwhile=route_loads)

            with ExitStack() as ph:
                den = ph.enter_context(nc.sbuf_tensor("f_den", [P, BLOCKS, HEADS], F32))
                (chain, divided, out_set, gelu_set, y_set, seen, applied, scaled, shifted, x_set, seen_x, var_set,
                 root_set, n_chain, var_x, root_x, n_chain_x, may_add) = (sem(f"f_{n}") for n in (
                     "chain", "divided", "out_set", "gelu_set", "y_set", "seen", "applied", "scaled", "shifted",
                     "x_set", "seen_x", "var_set", "root_set", "n_chain", "var_x", "root_x", "n_chain_x", "may_add"))
                block = ph.enter_context(nc.Block())
                by_block = total[:, :].rearrange("p (b f) -> p b f", f=AW)
                LAG = 3

                def one(b):
                    return bass.ds(b, 1)

                @block.vector
                def _(dve):
                    link = Chain(dve, chain)
                    link(nc.vector.tensor_scalar(den[:, :, :], by_block[:, :, D:AW], 1e-30, None, ALU.max))
                    link(nc.vector.reciprocal(den[:, :, :], den[:, :, :]))

                    def divide(b):
                        values = by_block[:, one(b), 0:D].rearrange("p o (n d) -> p (o n) d", d=HD)
                        nc.vector.tensor_tensor(values, values, den[:, one(b), :].rearrange("p o n -> p (o n)")
                                                .unsqueeze(2).broadcast_to([P, HEADS, HD]), ALU.mult).then_inc(divided, 1)

                    def add_skip(b):
                        dve.wait_ge(divided, b + 1)
                        nc.vector.tensor_tensor(skip[:, one(b), :], skip[:, one(b), :], by_block[:, one(b), 0:D], ALU.add)\
                            .then_inc(out_set, 1)

                    def look(b):
                        dve.wait_ge(y_set, b + 1)
                        stats_of(skip, b).then_inc(seen, 1)

                    def times_gamma(b):
                        dve.wait_ge(applied, b + 1)
                        nc.vector.tensor_tensor(skip[:, one(b), :], skip[:, one(b), :], gamma[:, :].unsqueeze(1), ALU.mult)\
                            .then_inc(scaled, 1)

                    def look_x(b):
                        dve.wait_ge(x_set, b + 1)
                        stats_of(X, b).then_inc(seen_x, 1)

                    def passes(first, second, third):
                        first(0)
                        for b in range(LAG):
                            first(b + 1)
                            second(b)
                        with dve.Fori(LAG, BLOCKS - 1) as b:
                            first(b + 1)
                            second(b)
                            third(b - LAG)
                        second(BLOCKS - 1)
                        for b in range(BLOCKS - 1 - LAG, BLOCKS):
                            third(b)
                    passes(divide, add_skip, look)
                    dve.wait_ge(seen, BLOCKS)
                    norm_ends(dve, Chain(dve, n_chain), var_set, root_set)
                    nc.vector.sem_inc(may_add, 1)
                    for b in range(2 * LAG):
                        times_gamma(b)
                    with dve.Fori(2 * LAG, BLOCKS) as b:
                        times_gamma(b)
                        look_x(b - 2 * LAG)
                    for b in range(BLOCKS - 2 * LAG, BLOCKS):
                        look_x(b)
                    dve.wait_ge(seen_x, BLOCKS)
                    norm_ends(dve, Chain(dve, n_chain_x), var_x, root_x)

                @block.scalar
                def _(act):
                    def gelu(b):
                        act.wait_ge(out_set, b + 1)
                        nc.scalar.activation(skip[:, one(b), :], skip[:, one(b), :], ACT.Gelu).then_inc(gelu_set, 1)
                    gelu(0)
                    with act.Fori(1, BLOCKS) as b:
                        gelu(b)
                    act.wait_ge(var_set, 1)
                    nc.scalar.activation(stat[:, :], stat[:, :], ACT.Sqrt).then_inc(root_set, 1)
                    act.wait_ge(may_add, 1)
                    with act.Fori(0, BLOCKS) as b:
                        nc.scalar.activation(skip[:, one(b), :], skip[:, one(b), :], ACT.Identity, scale=scale[:, one(b)],
                                             bias=shift[:, one(b)]).then_inc(applied, 1)
                    act.wait_ge(var_x, 1)
                    nc.scalar.activation(stat[:, :], stat[:, :], ACT.Sqrt).then_inc(root_x, 1)

                @block.gpsimd
                def _(pool):
                    with pool.Fori(0, BLOCKS) as b:
                        pool.wait_ge(gelu_set, b + 1)
                        nc.gpsimd.tensor_tensor(skip[:, one(b), :], skip[:, one(b), :], Z[:, one(b), :], ALU.add)\
                            .then_inc(y_set, 1)
                        nc.gpsimd.tensor_tensor(X[:, one(b), :], X[:, one(b), :], beta[:, :].unsqueeze(1), ALU.add)\
                            .then_inc(shifted, 1)
                    with pool.Fori(0, BLOCKS) as b:
                        pool.wait_ge(shifted, b + 1)
                        pool.wait_ge(scaled, b + 1)
                        nc.gpsimd.tensor_tensor(X[:, one(b), :], X[:, one(b), :], skip[:, one(b), :], ALU.add)\
                            .then_inc(x_set, 1)

        recycle()

        with ExitStack() as ph:
            def sb(name, shape, dt=F32):
                return ph.enter_context(nc.sbuf_tensor(name, shape, dt))

            zt_all = sb("r_zt_all", [P, KC, NODES])
            weight = sb("r_weight", [P, BLOCKS])
            every = sb("r_every", [P, NODES])
            project("route", Z, KC, [(wr, 1)], lambda dve, b, po, chain, at: nc.vector.tensor_tensor(
                weight[:, bass.ds(b, 1)], po[:, 0:1], br[:, :], ALU.add), 0, norm_of=X, save_t=zt_all)

            with ExitStack() as ph2:
                def sb2(name, shape, dt=F32):
                    return ph2.enter_context(nc.sbuf_tensor(name, shape, dt))

                ht = sb2("r_ht", [P, FC, 2 * P])
                y = sb2("r_y", [P, BLOCKS, D])
                wt = sb2("r_wt", [BLOCKS, P])
                larger = sb2("r_larger", [P, 2, NODES], mybir.dt.bfloat16)
                above = sb2("r_above", [P, BLOCKS])
                kept = sb2("r_kept", [P, BLOCKS])
                last_of = sb2("r_last_of", [P, BLOCKS])
                tie_count = sb2("r_tie_count", [P, BLOCKS])
                tie_until = sb2("r_tie_until", [P, BLOCKS])
                coef = sb2("r_coef", [P, BLOCKS])
                top_col = sb2("r_top_col", [P, 1])
                top_row = sb2("r_top_row", [1, P])
                top_one = sb2("r_top_one", [1, 1])
                top_all = sb2("r_top_all", [P, 1])
                ps_h = [ph2.enter_context(nc.psum_tensor(f"r_ps_h{c}", [P, 512], F32)) for c in range(4)]
                ps_y = [ph2.enter_context(nc.psum_tensor(f"r_ps_y{k}", [P, 512], F32)) for k in range(2)]
                pw = ph2.enter_context(nc.psum_tensor("r_pw", [P, 512], F32))
                (w_turned, wt_set, w_out, every_in, every_set, h_set, h_gelu, y_set, y_copied, chain, counted, base_set,
                 x_set, x_out, tie_step, tie_back, y_ready) = (sem(f"r_{n}") for n in (
                     "w_turned", "wt_set", "w_out", "every_in", "every_set", "h_set", "h_gelu", "y_set", "y_copied",
                     "chain", "counted", "base_set", "x_set", "x_out", "tie_step", "tie_back", "y_ready"))
                block = ph2.enter_context(nc.Block())
                LAST = FULL + 1 - 2 * (PAIRS - 1)
                TIE_AT = PAIRS - 5

                @block.tensor
                def _(pe):
                    nc.tensor.transpose(pw[0:BLOCKS, 0:P], weight[:, :], ident[:, :]).then_inc(w_turned, 1)

                    def step(n, blocks=2):
                        for h in range(FC):
                            wait_count(pe, h_gelu, FC * n + h - 3)
                            for c in range(KC):
                                last = nc.tensor.matmul(ps_h[h % 4][:, 0:blocks * P], r_w1[:, c, h * P:(h + 1) * P],
                                                        zt_all[:, c, bass.ds(n * 2 * P, blocks * P)],
                                                        start=(c == 0), stop=(c == KC - 1))
                            last.then_inc(h_set, 1)
                        for m in range(blocks):
                            wait_count(pe, y_copied, 2 * n + m - 1)
                            for h in range(FC):
                                pe.wait_ge(h_gelu, FC * n + h + 1)
                                last = nc.tensor.matmul(ps_y[m][:, 0:D], ht[:, h, m * P:(m + 1) * P], r_w2[:, h, :],
                                                        start=(h == 0), stop=(h == FC - 1))
                            last.then_inc(y_set, 1)
                    step(0)
                    with pe.Fori(1, TIE_AT) as n:
                        step(n)
                    pe.wait_ge(tie_step, 1)
                    nc.tensor.transpose(pw[0:1, 0:P], top_col[:, :], ident[:, :]).then_inc(tie_back, 1)
                    step(TIE_AT)
                    pe.wait_ge(tie_step, 2)
                    nc.tensor.matmul(pw[:, 128:129], ones[0:1, :], top_one[:, :], start=True, stop=True).then_inc(tie_back, 1)
                    step(TIE_AT + 1)
                    pe.wait_ge(tie_step, 3)
                    nc.tensor.matmul(pw[:, 256:256 + BLOCKS], before[:, :], last_of[:, :], start=True, stop=True)
                    nc.tensor.matmul(pw[:, 384:384 + BLOCKS], ones[:, :], last_of[:, :], start=True, stop=True).then_inc(tie_back, 1)
                    for n in range(TIE_AT + 2, PAIRS):
                        step(n, LAST if n == PAIRS - 1 else 2)

                @block.scalar
                def _(act):
                    act.wait_ge(w_turned, 1)
                    nc.scalar.activation(wt[:, :], pw[0:BLOCKS, 0:P], ACT.Copy).then_inc(wt_set, 1)

                    def copy_y(n, blocks):
                        for m in range(blocks):
                            act.wait_ge(y_set, 2 * n + m + 1)
                            nc.scalar.activation(y[:, bass.ds(2 * n + m, 1), :], ps_y[m][:, 0:D].unsqueeze(1), ACT.Copy)\
                                .then_inc(y_copied, 1)

                    def step(n, blocks=2):
                        for h in range(FC):
                            act.wait_ge(h_set, FC * n + h + 1)
                            nc.scalar.activation(ht[:, h, 0:blocks * P], ps_h[h % 4][:, 0:blocks * P], ACT.Gelu_apprx_tanh,
                                                 bias=r_b1[:, h:h + 1]).then_inc(h_gelu, 1)
                        copy_y(n, blocks)
                    step(0)
                    with act.Fori(1, PAIRS - 1) as n:
                        step(n)
                    step(PAIRS - 1, LAST)

                @block.sync
                def _(sp):
                    sp.wait_ge(wt_set, 1)
                    sp.dma_start(w_d[:, :], wt[:, :]).then_inc(w_out, 16)
                    sp.wait_ge(w_out, 16)
                    sp.dma_start(every[:, :], w_d.rearrange("(o b) p -> o (b p)", o=1).broadcast_to([P, NODES]))\
                        .then_inc(every_in, 16)
                    with sp.Fori(0, FULL) as b:
                        sp.wait_ge(x_set, b + 1)
                        sp.dma_start(out[bass.ds(b * P, P), :], X[:, bass.ds(b, 1), :].rearrange("p o f -> p (o f)"))\
                            .then_inc(x_out, 16)
                    sp.wait_ge(x_set, FULL + 1)
                    sp.dma_start(out[FULL * P:N, :], X[0:TAIL, FULL, :]).then_inc(x_out, 16)
                    sp.wait_ge(x_out, 16 * (FULL + 1))

                @block.gpsimd
                def _(pool):
                    with pool.Fori(0, BLOCKS) as b:
                        nc.gpsimd.tensor_tensor(X[:, bass.ds(b, 1), :], X[:, bass.ds(b, 1), :], Z[:, bass.ds(b, 1), :], ALU.add)\
                            .then_inc(base_set, 1)

                @block.vector
                def _(dve):
                    link = Chain(dve, chain)
                    dve.wait_ge(every_in, 16)
                    link(nc.vector.memset(every[:, N:NODES], -3.0e38))

                    def count(b, k):
                        wait_count(dve, counted, b - 1)
                        nc.vector.tensor_scalar(larger[:, k, :], every[:, :], weight[:, bass.ds(b, 1)], 0.0, ALU.is_gt,
                                                ALU.add, accum_out=above[:, bass.ds(b, 1)]).then_inc(counted, 1)
                    count(0, 0)
                    count(1, 1)
                    with dve.Fori(1, PAIRS) as i:
                        for k in range(2):
                            count(2 * i + k, k)
                    dve.wait_ge(counted, BLOCKS)
                    link(nc.vector.tensor_scalar(kept[:, :], above[:, :], float(KEEP), None, ALU.is_lt))
                    link(nc.vector.tensor_tensor(kept[:, :], kept[:, :], real[:, :], ALU.mult))
                    link(nc.vector.tensor_scalar(above[:, :], above[:, :], 1.0, None, ALU.add))
                    link(nc.vector.tensor_tensor(coef[:, :], above[:, :], kept[:, :], ALU.mult))
                    nc.vector.tensor_reduce(top_col[:, :], coef[:, :], AX.X, ALU.max).then_inc(tie_step, 1)
                    dve.wait_ge(tie_back, 1)
                    link(nc.vector.tensor_copy(top_row[:, :], pw[0:1, 0:P]))
                    nc.vector.tensor_reduce(top_one[:, :], top_row[:, :], AX.X, ALU.max).then_inc(tie_step, 1)
                    dve.wait_ge(tie_back, 2)
                    link(nc.vector.tensor_copy(top_all[:, :], pw[:, 128:129]))
                    nc.vector.scalar_tensor_tensor(out=last_of[:, :], in0=above[:, :], scalar=top_all[:, 0:1], in1=real[:, :],
                                                   op0=ALU.is_equal, op1=ALU.mult).then_inc(tie_step, 1)
                    dve.wait_ge(tie_back, 3)
                    link(nc.vector.tensor_copy(tie_count[:, :], pw[:, 384:384 + BLOCKS]))
                    link(nc.vector.tensor_tensor_scan(tie_until[:, :], ones[:, 0:BLOCKS], tie_count[:, :], 0.0, ALU.mult, ALU.add))
                    link(nc.vector.tensor_tensor(tie_until[:, :], tie_until[:, :], tie_count[:, :], ALU.subtract))
                    link(nc.vector.tensor_tensor(tie_until[:, :], tie_until[:, :], pw[:, 256:256 + BLOCKS], ALU.add))
                    link(nc.vector.tensor_tensor(tie_until[:, :], tie_until[:, :], last_of[:, :], ALU.mult))
                    link(nc.vector.tensor_tensor(above[:, :], above[:, :], tie_until[:, :], ALU.add))
                    link(nc.vector.scalar_tensor_tensor(out=coef[:, :], in0=above[:, :], scalar=float(KEEP) + 0.5,
                                                        in1=weight[:, :], op0=ALU.is_lt, op1=ALU.mult))

                    def bias_y(b):
                        dve.wait_ge(y_copied, b + 1)
                        one = bass.ds(b, 1)
                        nc.vector.tensor_tensor(y[:, one, :], y[:, one, :], r_b2[:, :].unsqueeze(1), ALU.add).then_inc(y_ready, 1)

                    def add_y(b):
                        one = bass.ds(b, 1)
                        dve.wait_ge(y_ready, b + 1)
                        dve.wait_ge(base_set, b + 1)
                        nc.vector.scalar_tensor_tensor(out=X[:, one, :], in0=y[:, one, :], scalar=coef[:, one],
                                                       in1=X[:, one, :], op0=ALU.mult, op1=ALU.add).then_inc(x_set, 1)
                    bias_y(0)
                    with dve.Fori(0, FULL) as b:
                        bias_y(b + 1)
                        add_y(b)
                    add_y(FULL)


_INS = ["x", "src", "dst", "L0_gnn_W1", "L0_gnn_b1", "L0_gnn_W2", "L0_gnn_b2", "L0_ffn_Wg", "L0_ffn_bg", "L0_ffn_bias",
        "L0_ffn_W1", "L0_ffn_b1", "L0_ffn_W2", "L0_ffn_b2", "L1_gnn_Wq", "L1_gnn_bq", "L1_gnn_Wk", "L1_gnn_bk",
        "L1_gnn_Wv", "L1_gnn_bv", "L1_gnn_Wskip", "L1_gnn_bskip", "L1_gnn_gamma", "L1_gnn_beta",
        "L1_ffn_wr", "L1_ffn_br", "L1_ffn_w1", "L1_ffn_b1", "L1_ffn_w2", "L1_ffn_b2"]


def kernel(**inputs):
    import numpy as _np
    import concourse.bacc as _bacc
    from concourse.bass_utils import run_bass_kernel_spmd as _run

    nc = _bacc.Bacc("TRN2", target_bir_lowering=False, num_devices=1)
    arrays, args = {}, {}
    for name in _INS:
        a = _np.ascontiguousarray(inputs[name])
        arrays[f"in_{name}"] = a
        args[name] = nc.dram_tensor(f"in_{name}", a.shape, mybir.dt.from_np(a.dtype), kind="ExternalInput").ap()
    out = nc.dram_tensor("out_x", inputs["x"].shape, F32, kind="ExternalOutput").ap()
    gnn_program(nc, args, out)
    r = _run(nc, [arrays], core_ids=[0])
    return r.results[0]["out_x"]
```
